# Optimizing a Trainium2 kernel written in Bass

```python
import numpy as np
import jax
import jax.numpy as jnp

def _softmax(x, axis=-1):
    return jax.nn.softmax(x, axis=axis)

def _gelu(x):
    return jax.nn.gelu(x, approximate=True)

def _silu(x):
    return jax.nn.silu(x)

def _sigmoid(x):
    return jax.nn.sigmoid(x)

def _layernorm(x, axis=-1, eps=1e-05):
    m = jnp.mean(x, axis=axis, keepdims=True)
    v = jnp.var(x, axis=axis, keepdims=True)
    return (x - m) / jnp.sqrt(v + eps)

def _scatter_add(tgt, idx, src, axis=0):
    return tgt.at[idx].add(src)

def _segment_sum(src, seg, n):
    return jax.ops.segment_sum(src, seg, n)
kernel_name = 'mk_cond_seq_d4_seqx_r4_92f1c6'

def setup_inputs(seed: int=0):
    np.random.seed(seed)
    _w = jnp.asarray

    def _rec_inputs():
        import jax
        import jax.numpy as jnp
        _rk = jax.random.key(seed)
        x = -7.109e-05 + 0.9999 * jax.random.normal(jax.random.fold_in(_rk, 1), (32, 256, 256), jnp.float32)
        _lenS = 256 - jax.random.randint(jax.random.fold_in(_rk, 7), (32,), 0, max(1, 256 // 4) + 1, jnp.int32)
        _lenS2 = 256 - jax.random.randint(jax.random.fold_in(_rk, 8), (32,), 0, max(1, 256 // 4) + 1, jnp.int32)
        condB_theta = jax.random.uniform(jax.random.fold_in(_rk, 11), (32,), jnp.float32, 0.0, 0.983423)
        condB_phi = jax.random.uniform(jax.random.fold_in(_rk, 12), (32,), jnp.float32, 0.0, 0.961312)
        itok_B_0_7 = jax.random.randint(jax.random.fold_in(_rk, 13), (32,), 0, 8, jnp.int32)
        itok_B_0_2 = jax.random.randint(jax.random.fold_in(_rk, 14), (32,), 0, 3, jnp.int32)
        itok_B_34_63 = jax.random.randint(jax.random.fold_in(_rk, 16), (32,), 34, 64, jnp.int32)
        fside_Bx16xSxS_0 = -1.47943e-05 + 1.00017 * jax.random.normal(jax.random.fold_in(_rk, 17), (32, 16, 256, 256), jnp.float32)
        _validS = jnp.arange(256)[None, :] < _lenS[:, None]
        _validS2 = jnp.arange(256)[None, :] < _lenS2[:, None]
        _causal = jnp.tril(jnp.ones((256, 256), dtype=bool))
        mask_Bx1xSxS_bk0 = jnp.logical_not(jnp.broadcast_to(_validS[:, None, None, :], (32, 1, 256, 256)))
        return (x, condB_theta, condB_phi, itok_B_0_7, itok_B_0_2, itok_B_34_63, fside_Bx16xSxS_0, mask_Bx1xSxS_bk0)
    x, condB_theta, condB_phi, itok_B_0_7, itok_B_0_2, itok_B_34_63, fside_Bx16xSxS_0, mask_Bx1xSxS_bk0 = _rec_inputs()

    def _L0_cond_setup():
        import jax, jax.numpy as jnp
        import numpy as np
        key = jax.random.key(seed)
        k1, k2, k3 = jax.random.split(key, 3)
        B, N, D = (16, 1024, 256)
        embeddings = jax.random.normal(k1, (B, N, D), dtype=jnp.float32)
        theta = jax.random.uniform(k2, (B,), dtype=jnp.float32)
        phi = jax.random.uniform(k3, (B,), dtype=jnp.float32)
        return {'embeddings': embeddings, 'theta': theta, 'phi': phi}
    _L0_cond_all = _L0_cond_setup()
    _L0_cond_in = {k: v for k, v in _L0_cond_all.items() if k in ()}
    del _L0_cond_all

    def _L1_cond_setup():
        import jax, jax.numpy as jnp
        import numpy as np
        E, H, I = (8, 256, 1024)
        B, S = (4, 256)
        LN_EPS = 1e-12
        key = jax.random.key(seed)
        ks = jax.random.split(key, 8)
        x = jax.random.normal(ks[0], (B, S, H), dtype=jnp.float32)
        expert_idx = jax.random.randint(ks[1], (B,), 0, E, dtype=jnp.int64)
        Wi = jax.random.normal(ks[2], (E, H, I), dtype=jnp.float32) * 0.02
        bi = jnp.zeros((E, I), dtype=jnp.float32)
        Wo = jax.random.normal(ks[3], (E, I, H), dtype=jnp.float32) * 0.02
        bo = jnp.zeros((E, H), dtype=jnp.float32)
        gamma = jnp.ones((E, H), dtype=jnp.float32)
        beta = jnp.zeros((E, H), dtype=jnp.float32)
        return {'input_tensor': x, 'expert_idx': expert_idx, 'Wi': Wi, 'bi': bi, 'Wo': Wo, 'bo': bo, 'gamma': gamma, 'beta': beta}
    _L1_cond_all = _L1_cond_setup()
    _L1_cond_in = {k: v for k, v in _L1_cond_all.items() if k in ('Wi', 'bi', 'Wo', 'bo', 'gamma', 'beta')}
    del _L1_cond_all

    def _L2_cond_setup():
        import jax, jax.numpy as jnp
        import numpy as np
        H = 256
        EPS = 1e-05

        def _gelu(x):
            return jax.nn.gelu(x, approximate=False)
        key = jax.random.key(seed)
        ks = jax.random.split(key, 16)
        s = 1.0 / np.sqrt(H)
        inp = {'x': jax.random.normal(ks[0], (64, 256, H), dtype=jnp.float32), 'condition': jax.random.randint(ks[1], (64,), 0, 3), 'w1_nr': jax.random.normal(ks[2], (H, H), dtype=jnp.float32) * s, 'b1_nr': jnp.zeros((H,), dtype=jnp.float32), 'w2_nr': jax.random.normal(ks[3], (H, H), dtype=jnp.float32) * s, 'b2_nr': jnp.zeros((H,), dtype=jnp.float32), 'w1_tsr': jax.random.normal(ks[4], (H, H), dtype=jnp.float32) * s, 'b1_tsr': jnp.zeros((H,), dtype=jnp.float32), 'w2_tsr': jax.random.normal(ks[5], (H, H), dtype=jnp.float32) * s, 'b2_tsr': jnp.zeros((H,), dtype=jnp.float32), 'w1_sr': jax.random.normal(ks[6], (H, 2 * H), dtype=jnp.float32) * s, 'b1_sr': jnp.zeros((2 * H,), dtype=jnp.float32), 'w2_sr': jax.random.normal(ks[7], (2 * H, H), dtype=jnp.float32) * (1.0 / np.sqrt(2 * H)), 'b2_sr': jnp.zeros((H,), dtype=jnp.float32), 'w3_sr': jax.random.normal(ks[8], (H, H), dtype=jnp.float32) * s, 'b3_sr': jnp.zeros((H,), dtype=jnp.float32), 'gamma': jnp.ones((H,), dtype=jnp.float32), 'beta': jnp.zeros((H,), dtype=jnp.float32)}
        return inp
    _L2_cond_all = _L2_cond_setup()
    _L2_cond_in = {k: v for k, v in _L2_cond_all.items() if k in ('w1_nr', 'b1_nr', 'w2_nr', 'b2_nr', 'w1_tsr', 'b1_tsr', 'w2_tsr', 'b2_tsr', 'w1_sr', 'b1_sr', 'w2_sr', 'b2_sr', 'w3_sr', 'b3_sr', 'gamma', 'beta')}
    del _L2_cond_all

    def _L3_cond_setup():
        import jax, jax.numpy as jnp
        import numpy as np
        import math
        D_MODEL = 256
        N_HEAD = 16
        HEAD_DIM = D_MODEL // N_HEAD
        D_FF = 1024
        NUM_STEPS = 100.0
        RESCALE = 4000.0
        EPS = 1e-05

        def _sin_emb(t):
            half = D_MODEL // 2
            x = t.astype(jnp.float32) / NUM_STEPS * RESCALE
            freqs = jnp.exp(jnp.arange(half, dtype=jnp.float32) * (-math.log(10000.0) / (half - 1)))
            e = x[:, None] * freqs[None, :]
            return jnp.concatenate([jnp.sin(e), jnp.cos(e)], axis=-1)

        def _ln(x):
            m = jnp.mean(x, axis=-1, keepdims=True)
            v = jnp.var(x, axis=-1, keepdims=True)
            return (x - m) / jnp.sqrt(v + EPS)

        def _gelu2(x):
            return x * jax.nn.sigmoid(1.702 * x)
        key = jax.random.key(seed)
        ks = jax.random.split(key, 24)
        B, S, D, F = (4, 128, D_MODEL, D_FF)
        std = 0.02
        inp = {'src': jax.random.normal(ks[0], (B, S, D), dtype=jnp.float32), 'src_mask': jax.random.randint(ks[1], (B, 1, S, S), 0, 2).astype(bool), 'timestep': jax.random.randint(ks[2], (B,), 0, 100, dtype=jnp.int32), 'attention_bias': jax.random.normal(ks[3], (B, N_HEAD, S, S), dtype=jnp.float32), 'W_ada': jax.random.normal(ks[4], (D, 2 * D), dtype=jnp.float32) * std, 'b_ada': jnp.zeros((2 * D,), dtype=jnp.float32), 'Wq': jax.random.normal(ks[5], (D, D), dtype=jnp.float32) * std, 'bq': jnp.zeros((D,), dtype=jnp.float32), 'Wk': jax.random.normal(ks[6], (D, D), dtype=jnp.float32) * std, 'bk': jnp.zeros((D,), dtype=jnp.float32), 'Wv': jax.random.normal(ks[7], (D, D), dtype=jnp.float32) * std, 'bv': jnp.zeros((D,), dtype=jnp.float32), 'Wo': jax.random.normal(ks[8], (D, D), dtype=jnp.float32) * std, 'bo': jnp.zeros((D,), dtype=jnp.float32), 'W1': jax.random.normal(ks[9], (D, F), dtype=jnp.float32) * std, 'b1': jnp.zeros((F,), dtype=jnp.float32), 'W2': jax.random.normal(ks[10], (F, D), dtype=jnp.float32) * std, 'b2': jnp.zeros((D,), dtype=jnp.float32), 'g2': jnp.ones((D,), dtype=jnp.float32), 'beta2': jnp.zeros((D,), dtype=jnp.float32)}
        return inp
    _L3_cond_all = _L3_cond_setup()
    _L3_cond_in = {k: v for k, v in _L3_cond_all.items() if k in ('W_ada', 'b_ada', 'Wq', 'bq', 'Wk', 'bk', 'Wv', 'bv', 'Wo', 'bo', 'W1', 'b1', 'W2', 'b2', 'g2', 'beta2')}
    del _L3_cond_all
    return {'x': x, 'condB_theta': condB_theta, 'condB_phi': condB_phi, 'itok_B_0_7': itok_B_0_7, 'itok_B_0_2': itok_B_0_2, 'itok_B_34_63': itok_B_34_63, 'fside_Bx16xSxS_0': fside_Bx16xSxS_0, 'mask_Bx1xSxS_bk0': mask_Bx1xSxS_bk0, 'L1_cond_Wi': _L1_cond_in['Wi'], 'L1_cond_bi': _L1_cond_in['bi'], 'L1_cond_Wo': _L1_cond_in['Wo'], 'L1_cond_bo': _L1_cond_in['bo'], 'L1_cond_gamma': _L1_cond_in['gamma'], 'L1_cond_beta': _L1_cond_in['beta'], 'L2_cond_w1_nr': _L2_cond_in['w1_nr'], 'L2_cond_b1_nr': _L2_cond_in['b1_nr'], 'L2_cond_w2_nr': _L2_cond_in['w2_nr'], 'L2_cond_b2_nr': _L2_cond_in['b2_nr'], 'L2_cond_w1_tsr': _L2_cond_in['w1_tsr'], 'L2_cond_b1_tsr': _L2_cond_in['b1_tsr'], 'L2_cond_w2_tsr': _L2_cond_in['w2_tsr'], 'L2_cond_b2_tsr': _L2_cond_in['b2_tsr'], 'L2_cond_w1_sr': _L2_cond_in['w1_sr'], 'L2_cond_b1_sr': _L2_cond_in['b1_sr'], 'L2_cond_w2_sr': _L2_cond_in['w2_sr'], 'L2_cond_b2_sr': _L2_cond_in['b2_sr'], 'L2_cond_w3_sr': _L2_cond_in['w3_sr'], 'L2_cond_b3_sr': _L2_cond_in['b3_sr'], 'L2_cond_gamma': _L2_cond_in['gamma'], 'L2_cond_beta': _L2_cond_in['beta'], 'L3_cond_W_ada': _L3_cond_in['W_ada'], 'L3_cond_b_ada': _L3_cond_in['b_ada'], 'L3_cond_Wq': _L3_cond_in['Wq'], 'L3_cond_bq': _L3_cond_in['bq'], 'L3_cond_Wk': _L3_cond_in['Wk'], 'L3_cond_bk': _L3_cond_in['bk'], 'L3_cond_Wv': _L3_cond_in['Wv'], 'L3_cond_bv': _L3_cond_in['bv'], 'L3_cond_Wo': _L3_cond_in['Wo'], 'L3_cond_bo': _L3_cond_in['bo'], 'L3_cond_W1': _L3_cond_in['W1'], 'L3_cond_b1': _L3_cond_in['b1'], 'L3_cond_W2': _L3_cond_in['W2'], 'L3_cond_b2': _L3_cond_in['b2'], 'L3_cond_g2': _L3_cond_in['g2'], 'L3_cond_beta2': _L3_cond_in['beta2']}

def reference(x, condB_theta, condB_phi, itok_B_0_7, itok_B_0_2, itok_B_34_63, fside_Bx16xSxS_0, mask_Bx1xSxS_bk0, L1_cond_Wi, L1_cond_bi, L1_cond_Wo, L1_cond_bo, L1_cond_gamma, L1_cond_beta, L2_cond_w1_nr, L2_cond_b1_nr, L2_cond_w2_nr, L2_cond_b2_nr, L2_cond_w1_tsr, L2_cond_b1_tsr, L2_cond_w2_tsr, L2_cond_b2_tsr, L2_cond_w1_sr, L2_cond_b1_sr, L2_cond_w2_sr, L2_cond_b2_sr, L2_cond_w3_sr, L2_cond_b3_sr, L2_cond_gamma, L2_cond_beta, L3_cond_W_ada, L3_cond_b_ada, L3_cond_Wq, L3_cond_bq, L3_cond_Wk, L3_cond_bk, L3_cond_Wv, L3_cond_bv, L3_cond_Wo, L3_cond_bo, L3_cond_W1, L3_cond_b1, L3_cond_W2, L3_cond_b2, L3_cond_g2, L3_cond_beta2):
    import jax
    import jax.numpy as jnp

    def _L0_cond_ref(embeddings, theta, phi):
        import jax, jax.numpy as jnp
        import numpy as np
        B, N, D = embeddings.shape
        e = embeddings.reshape(B, N, D // 4, 4)
        ct = jnp.cos(theta)[:, None, None]
        st = jnp.sin(theta)[:, None, None]
        cp = jnp.cos(phi)[:, None, None]
        sp = jnp.sin(phi)[:, None, None]
        x0, x1, x2, x3 = (e[..., 0], e[..., 1], e[..., 2], e[..., 3])
        out = jnp.stack([x0 * ct + x1 * st, -x0 * st + x1 * ct, x2 * cp + x3 * sp, -x2 * sp + x3 * cp], axis=-1)
        return out.reshape(B, N, D)

    def _L1_cond_ref(input_tensor, expert_idx, Wi, bi, Wo, bo, gamma, beta):
        import jax, jax.numpy as jnp
        import numpy as np
        E, H, I = (8, 256, 1024)
        B, S = (4, 256)
        LN_EPS = 1e-12
        Wi_b = Wi[expert_idx]
        bi_b = bi[expert_idx]
        Wo_b = Wo[expert_idx]
        bo_b = bo[expert_idx]
        g_b = gamma[expert_idx]
        be_b = beta[expert_idx]
        h = jax.nn.gelu(jnp.einsum('bsh,bhi->bsi', input_tensor, Wi_b) + bi_b[:, None, :], approximate=False)
        o = jnp.einsum('bsi,bih->bsh', h, Wo_b) + bo_b[:, None, :]
        r = o + input_tensor
        mu = jnp.mean(r, axis=-1, keepdims=True)
        var = jnp.mean(jnp.square(r - mu), axis=-1, keepdims=True)
        y = (r - mu) * jax.lax.rsqrt(var + LN_EPS)
        return y * g_b[:, None, :] + be_b[:, None, :]

    def _L2_cond_ref(x, condition, w1_nr, b1_nr, w2_nr, b2_nr, w1_tsr, b1_tsr, w2_tsr, b2_tsr, w1_sr, b1_sr, w2_sr, b2_sr, w3_sr, b3_sr, gamma, beta):
        import jax, jax.numpy as jnp
        import numpy as np
        H = 256
        EPS = 1e-05

        def _gelu(x):
            return jax.nn.gelu(x, approximate=False)
        out_nr = _gelu(jnp.einsum('bth,hk->btk', x, w1_nr) + b1_nr)
        out_nr = jnp.einsum('bth,hk->btk', out_nr, w2_nr) + b2_nr
        out_tsr = _gelu(jnp.einsum('bth,hk->btk', x, w1_tsr) + b1_tsr)
        out_tsr = jnp.einsum('bth,hk->btk', out_tsr, w2_tsr) + b2_tsr
        h = _gelu(jnp.einsum('bth,hk->btk', x, w1_sr) + b1_sr)
        h = _gelu(jnp.einsum('bth,hk->btk', h, w2_sr) + b2_sr)
        out_sr = jnp.einsum('bth,hk->btk', h, w3_sr) + b3_sr
        c = condition[:, None, None]
        out = jnp.where(c == 0, out_nr, jnp.where(c == 1, out_tsr, jnp.where(c == 2, out_sr, jnp.zeros_like(x))))
        y = x + out
        mu = jnp.mean(y, axis=-1, keepdims=True)
        var = jnp.mean((y - mu) ** 2, axis=-1, keepdims=True)
        return (y - mu) * jax.lax.rsqrt(var + EPS) * gamma + beta

    def _L3_cond_ref(src, src_mask, timestep, attention_bias, W_ada, b_ada, Wq, bq, Wk, bk, Wv, bv, Wo, bo, W1, b1, W2, b2, g2, beta2):
        import jax, jax.numpy as jnp
        import numpy as np
        import math
        D_MODEL = 256
        N_HEAD = 16
        HEAD_DIM = D_MODEL // N_HEAD
        D_FF = 1024
        NUM_STEPS = 100.0
        RESCALE = 4000.0
        EPS = 1e-05

        def _sin_emb(t):
            half = D_MODEL // 2
            x = t.astype(jnp.float32) / NUM_STEPS * RESCALE
            freqs = jnp.exp(jnp.arange(half, dtype=jnp.float32) * (-math.log(10000.0) / (half - 1)))
            e = x[:, None] * freqs[None, :]
            return jnp.concatenate([jnp.sin(e), jnp.cos(e)], axis=-1)

        def _ln(x):
            m = jnp.mean(x, axis=-1, keepdims=True)
            v = jnp.var(x, axis=-1, keepdims=True)
            return (x - m) / jnp.sqrt(v + EPS)

        def _gelu2(x):
            return x * jax.nn.sigmoid(1.702 * x)
        B, S, D = src.shape
        emb = jax.nn.silu(_sin_emb(timestep)) @ W_ada + b_ada
        scale, shift = jnp.split(emb[:, None, :], 2, axis=-1)
        x = _ln(src) * (1.0 + scale) + shift
        q = (x @ Wq + bq).reshape(B, S, N_HEAD, HEAD_DIM).transpose(0, 2, 1, 3)
        k = (x @ Wk + bk).reshape(B, S, N_HEAD, HEAD_DIM).transpose(0, 2, 1, 3)
        v = (x @ Wv + bv).reshape(B, S, N_HEAD, HEAD_DIM).transpose(0, 2, 1, 3)
        scores = jnp.einsum('bhqd,bhkd->bhqk', q / math.sqrt(HEAD_DIM), k)
        scores = scores + attention_bias
        scores = jnp.where(src_mask, -jnp.inf, scores.astype(jnp.float32))
        probs = jax.nn.softmax(scores, axis=-1).astype(v.dtype)
        ctx = jnp.einsum('bhqk,bhkd->bhqd', probs, v)
        ctx = ctx.transpose(0, 2, 1, 3).reshape(B, S, D)
        x = x + (ctx @ Wo + bo)
        h = _ln(x) * g2 + beta2
        ff = _gelu2(h @ W1 + b1) @ W2 + b2
        return x + ff
    x = _L0_cond_ref(x, condB_theta, condB_phi)
    x = _L1_cond_ref(x, itok_B_0_7, L1_cond_Wi, L1_cond_bi, L1_cond_Wo, L1_cond_bo, L1_cond_gamma, L1_cond_beta)
    x = _L2_cond_ref(x, itok_B_0_2, L2_cond_w1_nr, L2_cond_b1_nr, L2_cond_w2_nr, L2_cond_b2_nr, L2_cond_w1_tsr, L2_cond_b1_tsr, L2_cond_w2_tsr, L2_cond_b2_tsr, L2_cond_w1_sr, L2_cond_b1_sr, L2_cond_w2_sr, L2_cond_b2_sr, L2_cond_w3_sr, L2_cond_b3_sr, L2_cond_gamma, L2_cond_beta)
    x = _L3_cond_ref(x, mask_Bx1xSxS_bk0, itok_B_34_63, fside_Bx16xSxS_0, L3_cond_W_ada, L3_cond_b_ada, L3_cond_Wq, L3_cond_bq, L3_cond_Wk, L3_cond_bk, L3_cond_Wv, L3_cond_bv, L3_cond_Wo, L3_cond_bo, L3_cond_W1, L3_cond_b1, L3_cond_W2, L3_cond_b2, L3_cond_g2, L3_cond_beta2)
    return x

_drawn_inputs = setup_inputs


def setup_inputs(seed=0):
    import zlib

    import numpy as np

    out = dict(_drawn_inputs(seed))
    spreads = {'L1_cond_bi': (0.0, 0.1),
     'L1_cond_bo': (0.0, 0.1),
     'L1_cond_gamma': (1.0, 0.2),
     'L1_cond_beta': (0.0, 0.1),
     'L2_cond_b1_nr': (0.0, 0.1),
     'L2_cond_b2_nr': (0.0, 0.1),
     'L2_cond_b1_tsr': (0.0, 0.1),
     'L2_cond_b2_tsr': (0.0, 0.1),
     'L2_cond_b1_sr': (0.0, 0.381),
     'L2_cond_b2_sr': (0.0, 0.267),
     'L2_cond_b3_sr': (0.0, 0.1),
     'L2_cond_gamma': (1.0, 0.2),
     'L2_cond_beta': (0.0, 0.1),
     'L3_cond_b_ada': (0.0, 0.1),
     'L3_cond_bq': (0.0, 0.8),
     'L3_cond_bk': (0.0, 0.8),
     'L3_cond_bv': (0.0, 0.1),
     'L3_cond_bo': (0.0, 0.1),
     'L3_cond_b1': (0.0, 0.1),
     'L3_cond_b2': (0.0, 0.1),
     'L3_cond_g2': (1.0, 0.6),
     'L3_cond_beta2': (0.0, 0.77)}
    factors = {'fside_Bx16xSxS_0': 7.043, 'L3_cond_Wq': 8.0, 'L3_cond_Wk': 8.0}
    for name, (base, spread) in spreads.items():
        noise = np.random.default_rng([zlib.crc32(name.encode()), seed]).standard_normal(out[name].shape)
        drawn = base * np.exp(spread * noise) if base else spread * noise
        out[name] = jnp.asarray(drawn.astype(out[name].dtype))
    for name, factor in factors.items():
        out[name] = (out[name] * factor).astype(out[name].dtype)
    return out
```

```python
from contextlib import ExitStack

import numpy as np

import concourse.bass as bass
from concourse import mybir

P = 128
F32 = mybir.dt.float32
F32R = mybir.dt.float32r
I32 = mybir.dt.int32
U8 = mybir.dt.uint8
ALU = mybir.AluOpType
ACT = mybir.ActivationFunctionType

C_FREQ, C_ROW, C_KIND = 0, 1, 2
TWO_PI = 6.283185307179586
PI_A = 6.28125
PI_B = float(np.float32(TWO_PI - PI_A).view(np.uint32) & np.uint32(0xFFFFF000)) * 0 + float(
    (np.float32(TWO_PI - PI_A).view(np.uint32) & np.uint32(0xFFFFF000)).view(np.float32))
PI_C = TWO_PI - PI_A - PI_B
ROUND_MAGIC = 12582912.0
PI_BELOW = 3.1415925
MASKED = -1.0e30


class Signal:

    def __init__(self, sem):
        self.sem, self.count = sem, 0


class Lane:

    def __init__(self):
        self.steps, self.waited = [], {}

    def wait(self, *marks):
        for mark in marks:
            if mark is None:
                continue
            signal, value = mark
            if self.waited.get(signal, 0) < value:
                self.waited[signal] = value
                self.steps.append(lambda e, s=signal.sem, v=value: e.wait_ge(s, v))

    def run(self, make, signal=None, by=1):
        if signal is None:
            self.steps.append(make)
            return None
        self.steps.append(lambda e: make(e).then_inc(signal.sem, by))
        signal.count += by
        return (signal, signal.count)

    def play(self, engine):
        for step in self.steps:
            step(engine)


def conditioned_stack(nc, x_in, theta_in, phi_in, expert_in, branch_in, step_in, fside_in, mask_in, w, consts_in, out_d):
    NB, S, H = x_in.shape
    NH = fside_in.shape[1]
    HD = H // NH
    E, _, FF = w["L1_cond_Wi"].shape
    T = S // P
    K = H // P
    M = FF // P
    NPAIR = NH // 2
    SR = w["L2_cond_w1_sr"].shape[1]
    assert (T, K, HD) == (2, 2, 16) and SR == 4 * P and FF == 8 * P

    ctx = ExitStack()
    with ctx:
        def sb(name, shape, dt=F32):
            return ctx.enter_context(nc.sbuf_tensor(name, shape, dt))

        def signal(name):
            return Signal(ctx.enter_context(nc.semaphore(name)))

        ident = sb("ident", [P, P])
        eye = sb("eye", [P, K, H], F32R)
        consts = sb("consts", [P, 4])
        W = {}
        for name, cols in (("w1_nr", K * H), ("w2_nr", K * H), ("w1_tsr", K * H), ("w2_tsr", K * H),
                           ("w1_sr", K * SR), ("w2_sr", SR // P * H), ("w3_sr", K * H),
                           ("Wq", K * H), ("Wk", K * H), ("Wv", K * H), ("Wo", K * H),
                           ("W1", K * FF), ("W2", M * H)):
            W[name] = (sb(name + "_hi", [P, cols], F32R), sb(name + "_lo", [P, cols], F32R))
        NRAW, NEXP = 2, 2
        raw = sb("raw", [P, NRAW, 2 * K * H])
        exp_hi = sb("exp_hi", [P, NEXP, 2 * K * H], F32R)
        exp_lo = sb("exp_lo", [P, NEXP, 2 * K * H], F32R)
        q_stack = sb("q_stack", [P, NPAIR, S], F32R)
        k_stack = sb("k_stack", [P, NPAIR, S], F32R)
        NBIAS = 4
        bias_ring = sb("bias_ring", [P, NBIAS, 2, S])
        NX = 4
        x_scores = sb("x_scores", [P, NX, 2, S])
        NP_ = 2
        probs = sb("probs", [P, NP_, K, S])
        v_aug = sb("v_aug", [P, T, NH, 32])
        ctx_raw = sb("ctx_raw", [P, 2, S])
        ctx_nat = sb("ctx_nat", [P, T, H])
        mask_u8 = sb("mask_u8", [P, T, S], U8)
        mask_add = sb("mask_add", [P, T, S])
        NHID, NGELU = 3, 2
        gelu_out = sb("gelu_out", [P, NGELU, 2, S])
        hid_hi = sb("hid_hi", [P, NHID, 2, S], F32R)
        hid_lo = sb("hid_lo", [P, NHID, 2, S], F32R)
        xa_hi, xa_lo = sb("xa_hi", [P, K, S], F32R), sb("xa_lo", [P, K, S], F32R)
        xb_hi, xb_lo = sb("xb_hi", [P, K, S], F32R), sb("xb_lo", [P, K, S], F32R)
        xc_hi, xc_lo = sb("xc_hi", [P, K, S], F32R), sb("xc_lo", [P, K, S], F32R)
        x_nat = sb("x_nat", [P, T, H])
        rot_a = sb("rot_a", [P, T, H])
        y_nat = sb("y_nat", [P, T, H])
        xo_nat = sb("xo_nat", [P, T, H])
        gamma2 = sb("gamma2", [P, H])
        beta2 = sb("beta2", [P, H])
        rot_cos = sb("rot_cos", [P, NB, 4])
        rot_sin = sb("rot_sin", [P, NB, 4])
        N1 = M + 2 * K + K
        chosen = sb("chosen", [P, N1, NB])
        mod = sb("mod", [P, 2 * K, NB])
        NCOL = SR // P + K + 2 * K + K + K + M + 2 * K
        cols = sb("cols", [P, NCOL])
        NROWS = 32
        bias_raw = sb("bias_raw", [NROWS, H])
        bias_rows = sb("bias_rows", [2 * NROWS, H], F32R)
        select = sb("select", [2 * NROWS, 4, NB])
        stage_sel = sb("stage_sel", [2 * NROWS, 4, P], F32R)
        ones = sb("ones", [2 * NROWS, P])
        idx = sb("idx", [1, 2, NB], I32)
        stats = sb("stats", [P, T, 6])
        mean_var = sb("mean_var", [P, T, 2])
        rstd = sb("rstd", [P, T])
        half_neg = sb("half_neg", [P, T])
        row_max = sb("row_max", [P, NX, 2])
        rden = sb("rden", [P, T, 4])

        pS = ctx.enter_context(nc.psum_tensor("pS", [P, 2, T, S], F32))
        pX = ctx.enter_context(nc.psum_tensor("pX", [P, 2, K, S], F32))
        pC = ctx.enter_context(nc.psum_tensor("pC", [P, S], F32))
        ND, OUT = 2, 2
        pD = ctx.enter_context(nc.psum_tensor("pD", [P, ND + 1, 2, S], F32))

        dma = {n: signal("dma_" + n) for n in ("const", "cols", "rows", "x", "mask", "idx", "stack", "out", "bcast", "ada")}
        dma_raw = [signal(f"dma_raw{i}") for i in range(NRAW)]
        dma_bias = [signal(f"dma_bias{i}") for i in range(NBIAS)]
        pe_set, pe_dense, pe_tr, pe_s, pe_x, pe_c = (signal("pe_" + n) for n in ("set", "dense", "tr", "s", "x", "c"))
        act_set, act_dense, act_exp, act_w = (signal("act_" + n) for n in ("set", "dense", "exp", "w"))
        dve_set, dve_dense, dve_max, dve_sub, dve_small = (signal("dve_" + n) for n in ("set", "dense", "max", "sub", "small"))
        pool_set, pool_bias, pool_lo, pool_norm, pool_w = (signal("pool_" + n) for n in ("set", "bias", "lo", "norm", "w"))
        pe_n, act_n, dve_n = (signal(n) for n in ("pe_narrow", "act_narrow", "dve_narrow"))
        pe_r, act_r, dve_r = (signal(n) for n in ("pe_deep", "act_deep", "dve_deep"))

        PE, AC, VE, PO, SP = Lane(), Lane(), Lane(), Lane(), Lane()

        def flat(ap):
            return ap.rearrange("p a b -> p (a b)")

        def f32(ap):
            return ap.bitcast(F32)

        def mm(o, lhsT, rhs, start=False, stop=False, sig=None, **kw):
            return PE.run(lambda e: e.matmul(o, lhsT, rhs, start=start, stop=stop, skip_group_check=True, **kw), sig)

        def transpose(o, i, sig=None):
            return PE.run(lambda e: e.transpose(o, i, ident[:, :]), sig)

        def act(o, i, func, sig, bias=0.0, scale=1.0):
            return AC.run(lambda e: e.activation(o, i, func, bias=bias, scale=scale), sig)

        def tt(lane, o, a, b, op, sig):
            return lane.run(lambda e: e.tensor_tensor(o, a, b, op), sig)

        def ts(lane, o, a, s1, op0, sig, s2=None, op1=None):
            if op1 is None:
                return lane.run(lambda e: e.tensor_scalar(o, a, s1, None, op0), sig)
            return lane.run(lambda e: e.tensor_scalar(o, a, s1, s2, op0, op1), sig)

        def stt(o, a, s, b, op0, op1, sig):
            return VE.run(lambda e: e.scalar_tensor_tensor(o, a, s, b, op0, op1), sig)

        def split_terms(left, right):
            return [(left[0], right[0]), (left[0], right[1]), (left[1], right[0])]

        def products(o, terms, start, stop, sig=None):
            mark = None
            for n, (a, b) in enumerate(terms):
                last = n == len(terms) - 1
                mark = mm(o, a, b, start=start and n == 0, stop=stop and last, sig=sig if last else None)
            return mark

        dense_free = [[] for _ in range(ND + 1)]
        turn = {"dense": 0}

        def take_bank():
            n = turn["dense"] % ND
            turn["dense"] += 1
            PE.wait(*dense_free[n])
            dense_free[n] = []
            return n

        def load(dst, src, sig, **kw):
            return SP.run(lambda e: e.dma_start(dst, src, **kw), sig, by=16)

        load(consts[:, :], consts_in, dma["const"])
        load(idx[0:1, 0, :], expert_in.rearrange("(a b) -> a b", a=1), dma["idx"])
        got_idx = load(idx[0:1, 1, :], branch_in.rearrange("(a b) -> a b", a=1), dma["idx"])
        as_int = flat(rot_a[:, :, :]).bitcast(I32)
        scratch = flat(y_nat[:, :, :])
        for n, src in enumerate((expert_in, branch_in, step_in)):
            load(as_int[:, n * NB:(n + 1) * NB], src.partition_broadcast(P), dma["const"])
        ang = flat(x_nat[:, :, :])
        load(ang[:, 0:NB], theta_in.partition_broadcast(P), dma["const"])
        got_const = load(ang[:, NB:2 * NB], phi_in.partition_broadcast(P), dma["const"])

        col_at, at = {}, 0
        for name, n in (("L2_cond_b1_sr", SR // P), ("L2_cond_b2_sr", K), ("L3_cond_b_ada", 2 * K),
                        ("L3_cond_bq", K), ("L3_cond_bk", K), ("L3_cond_b1", M), ("L3_cond_g2", K),
                        ("L3_cond_beta2", K)):
            if name in ("L3_cond_bq", "L3_cond_bk"):
                for par in range(2):
                    src = w[name].rearrange("(g r d) -> g r d", r=2, d=HD)[:, par, :]
                    for g in range(NPAIR):
                        got_cols = load(cols[g * HD:(g + 1) * HD, at + par:at + par + 1],
                                        src[g, :].rearrange("(d a) -> d a", a=1), dma["cols"])
            else:
                got_cols = load(cols[:, at:at + n], w[name].rearrange("(n p) -> p n", p=P), dma["cols"],
                                allow_slow_non_contiguous=True)
            col_at[name] = at
            at += n

        def col(name, n=0):
            return cols[:, col_at[name] + n:col_at[name] + n + 1]

        rows_zero = VE.run(lambda e: e.memset(bias_raw[:, :], 0.0), dve_set)
        R_BRANCH, R_O, R_FF, R_V = E, E + 3, E + 4, E + 5
        SP.wait(rows_zero)
        load(bias_raw[0:E, :], w["L1_cond_bo"], dma["rows"])
        for r, name in ((R_BRANCH, "L2_cond_b2_nr"), (R_BRANCH + 1, "L2_cond_b2_tsr"), (R_BRANCH + 2, "L2_cond_b3_sr"),
                        (R_O, "L3_cond_bo"), (R_FF, "L3_cond_b2"), (R_V, "L3_cond_bv")):
            got_rows = load(bias_raw[r:r + 1, :], w[name].rearrange("(a n) -> a n", a=1), dma["rows"])
        scores_flat = x_scores[:, :, :, :].rearrange("p a b c -> p (a b c)")
        pick_bi, pick = scores_flat[:, 0:FF + H], scores_flat[:, FF + H:FF + 3 * H]
        load(pick_bi[0:E, 0:FF], w["L1_cond_bi"], dma["rows"])
        load(pick[0:E, 0:H], w["L1_cond_gamma"], dma["rows"])
        load(pick[0:E, H:2 * H], w["L1_cond_beta"], dma["rows"])
        load(pick_bi[0:1, FF:FF + H], w["L2_cond_b1_nr"].rearrange("(a n) -> a n", a=1), dma["rows"])
        got_rows = load(pick_bi[1:2, FF:FF + H], w["L2_cond_b1_tsr"].rearrange("(a n) -> a n", a=1), dma["rows"])
        load(gamma2[:, :], w["L2_cond_gamma"].partition_broadcast(P), dma["bcast"])
        got_bcast = load(beta2[:, :], w["L2_cond_beta"].partition_broadcast(P), dma["bcast"])

        PO.run(lambda e: e.memset(ident[:, :], 0.0), pool_set)
        PO.wait((pool_set, pool_set.count))
        got_ident = PO.run(lambda e: e.affine_select(out=ident[:, :], in_=ident[:, :], compare_op=ALU.not_equal,
                                                     fill=1.0, base=0, pattern=[[-1, P]], channel_multiplier=1),
                           pool_set)
        got_half = PO.run(lambda e: e.memset(half_neg[:, :], -0.5), pool_set)

        def vset(make):
            VE.wait((dve_set, dve_set.count))
            return VE.run(make, dve_set)

        VE.wait(got_ident)
        vset(lambda e: e.memset(f32(flat(eye[:, :, :])), 0.0))
        for k in range(K):
            vset(lambda e, k=k: e.tensor_copy(eye[:, k, k * P:(k + 1) * P], ident[:, :]))
        vset(lambda e: e.memset(ones[:, :], 1.0))
        vset(lambda e: e.memset(v_aug[:, :, :, :], 0.0))
        vset(lambda e: e.memset(v_aug[:, :, :, HD:HD + 1], 1.0))
        vset(lambda e: e.memset(select[:, :, :], 0.0))

        VE.wait(got_const)
        as_float = scratch[:, 0:3 * NB]
        vset(lambda e: e.tensor_copy(as_float, as_int[:, 0:3 * NB]))
        fx, fc, fs = (scratch[:, n * NB:(n + 1) * NB] for n in range(3))
        row_id = consts[:, C_ROW:C_ROW + 1]
        R2 = 2 * NROWS
        vset(lambda e: e.tensor_scalar(select[:, 0, :], fx[0:R2, :], row_id[0:R2, :], None, ALU.is_equal))
        vset(lambda e: e.tensor_scalar(select[:, 1, :], fc[0:R2, :], float(R_BRANCH), row_id[0:R2, :], ALU.add, ALU.is_equal))
        kind = consts[:, C_KIND:C_KIND + 1]
        vset(lambda e: e.tensor_scalar(select[:, 1, :], select[:, 1, :], kind[0:R2, :], None, ALU.mult))
        expert_row = consts[:, C_KIND + 1:C_KIND + 2]
        vset(lambda e: e.tensor_scalar(select[:, 0, :], select[:, 0, :], expert_row[0:R2, :], None, ALU.mult))
        branch_hot = scratch[:, 3 * NB:4 * NB]
        vset(lambda e: e.tensor_scalar(branch_hot, fc, row_id, None, ALU.is_equal))
        onev = scratch[:, 4 * NB:4 * NB + 4]
        for n, r in ((2, R_O), (3, R_FF), (1, R_V)):
            vset(lambda e, n=n, r=r: e.tensor_scalar(onev[:, n:n + 1], row_id, float(r), None, ALU.is_equal))
        for n in (1, 2, 3):
            pass
        v_sel = sb("v_sel", [R2, P], F32R)
        vset(lambda e: e.tensor_scalar(v_sel[:, :], ones[:, :], onev[0:R2, 1:2], None, ALU.mult))
        vset(lambda e: e.tensor_scalar(stage_sel[:, 2, :], ones[:, :], onev[0:R2, 2:3], None, ALU.mult))
        got_sel = vset(lambda e: e.tensor_scalar(stage_sel[:, 3, :], ones[:, :], onev[0:R2, 3:4], None, ALU.mult))
        VE.wait(got_rows)
        vset(lambda e: e.tensor_copy(bias_rows[0:NROWS, :], bias_raw[:, :]))
        vset(lambda e: e.tensor_tensor(bias_raw[:, :], bias_raw[:, :], f32(bias_rows[0:NROWS, :]), ALU.subtract))
        got_bias_rows = vset(lambda e: e.tensor_copy(bias_rows[NROWS:R2, :], bias_raw[:, :]))
        VE.wait(got_cols)
        QS_ = float(HD) ** -0.5
        got_bq = vset(lambda e: e.tensor_scalar(cols[:, col_at["L3_cond_bq"]:col_at["L3_cond_bq"] + K],
                                                cols[:, col_at["L3_cond_bq"]:col_at["L3_cond_bq"] + K],
                                                QS_, None, ALU.mult))

        n0 = take_bank()
        pick_ps = flat(pD[:, n0, :, :])
        PE.wait(got_bias_rows, got_rows)
        for n in range(M):
            mm(pick_ps[:, n * NB:(n + 1) * NB], pick_bi[0:E, n * P:(n + 1) * P], select[0:E, 0, :], True, True)
        for n in range(2 * K):
            mm(pick_ps[:, (M + n) * NB:(M + n + 1) * NB], pick[0:E, n * P:(n + 1) * P], select[0:E, 0, :], True, True)
        for n in range(K):
            a = M + 2 * K + n
            got_pick = mm(pick_ps[:, a * NB:(a + 1) * NB], pick_bi[0:2, FF + n * P:FF + (n + 1) * P],
                          branch_hot[0:2, :], True, True, sig=pe_set)
        VE.wait(got_pick)
        got_chosen = vset(lambda e: e.tensor_copy(chosen[:, :, :].rearrange("p a b -> p (a b)"), pick_ps[:, 0:N1 * NB]))
        dense_free[n0].append(got_chosen)

        def sine(dst, src, turn_by, tmp):
            vset(lambda e: e.tensor_scalar(tmp, src, 1.0 / TWO_PI, 0.25 * turn_by, ALU.mult, ALU.add))
            vset(lambda e: e.tensor_scalar(tmp, tmp, ROUND_MAGIC, None, ALU.add))
            vset(lambda e: e.tensor_scalar(tmp, tmp, ROUND_MAGIC, None, ALU.subtract))
            vset(lambda e: e.scalar_tensor_tensor(dst, tmp, -PI_A, src, ALU.mult, ALU.add))
            vset(lambda e: e.scalar_tensor_tensor(dst, tmp, -PI_B, dst, ALU.mult, ALU.add))
            vset(lambda e: e.scalar_tensor_tensor(dst, tmp, -PI_C, dst, ALU.mult, ALU.add))
            vset(lambda e: e.tensor_scalar(dst, dst, turn_by * TWO_PI / 4, PI_BELOW, ALU.add, ALU.min))
            ready = vset(lambda e: e.tensor_scalar(dst, dst, -PI_BELOW, None, ALU.max))
            AC.wait(ready)
            done = act(dst, dst, ACT.Sin, act_set)
            AC.wait(done)
            VE.wait(done)
            return done

        tmp = scratch[:, 5 * NB:7 * NB]
        cos2, sin2 = ang[:, 2 * NB:4 * NB], ang[:, 4 * NB:6 * NB]
        sine(cos2, ang[:, 0:2 * NB], 1, tmp)
        sine(sin2, ang[:, 0:2 * NB], 0, tmp)
        for j in range(4):
            a = (j // 2) * NB
            vset(lambda e, j=j, a=a: e.tensor_copy(rot_cos[:, :, j], cos2[:, a:a + NB]))
            got_rot = vset(lambda e, j=j, a=a: e.tensor_scalar(rot_sin[:, :, j], sin2[:, a:a + NB],
                                                     1.0 if j % 2 == 0 else -1.0, None, ALU.mult))
        vset(lambda e: e.tensor_scalar(fs, fs, 0.01, 4000.0, ALU.mult, ALU.mult))
        e_arg = scratch[:, 7 * NB:8 * NB]
        vset(lambda e: e.tensor_scalar(e_arg, fs, consts[:, C_FREQ:C_FREQ + 1], None, ALU.mult))
        emb = scratch[:, 8 * NB:10 * NB]
        sine(emb[:, 0:NB], e_arg, 0, tmp[:, 0:NB])
        sine(emb[:, NB:2 * NB], e_arg, 1, tmp[:, 0:NB])
        emb_act = scratch[:, 10 * NB:12 * NB]
        got_emb = act(emb_act, emb, ACT.Silu, act_set)
        ada = probs[:, :, :, :].rearrange("p a b c -> p (a b c)")
        ada_v = ada.rearrange("p (k n) -> p k n", k=K)
        got_ada = load(ada_v, w["L3_cond_W_ada"].rearrange("(k p) n -> p k n", p=P), dma["ada"])
        n0 = take_bank()
        ada_ps = flat(pD[:, n0, :, :])
        PE.wait(got_emb, got_ada)
        for n in range(2 * K):
            for k in range(K):
                got_mod = mm(ada_ps[:, n * NB:(n + 1) * NB], ada_v[:, k, n * P:(n + 1) * P],
                             emb_act[:, k * NB:(k + 1) * NB], k == 0, k == K - 1, sig=pe_set)
        VE.wait(got_mod)
        for n in range(2 * K):
            mod_ready = vset(lambda e, n=n: e.tensor_scalar(mod[:, n, :], ada_ps[:, n * NB:(n + 1) * NB],
                                                col("L3_cond_b_ada", n), 1.0 if n < K else 0.0, ALU.add, ALU.add))
        dense_free[n0].append(mod_ready)
        setup_done = mod_ready
        for lane in (PE, AC, PO, SP, VE):
            lane.wait(setup_done, got_ident, got_half, got_sel, got_bq, got_rot, got_bcast, got_emb)

        raw_free = [[] for _ in range(NRAW)]
        raw_n = [0]

        def take_raw():
            n = raw_n[0] % NRAW
            raw_n[0] += 1
            SP.wait(*raw_free[n])
            raw_free[n] = []
            return n

        def split_weight(name, src, permute=False, scale=1.0):
            hi, lo = W[name]
            k_n, n_n = src.shape[0] // P, src.shape[1]
            per = 1024 // n_n
            v = src.rearrange("(k p) n -> p k n", p=P)
            mark = None
            for k0 in range(0, k_n, per):
                kk = min(per, k_n - k0)
                n = take_raw()
                size = kk * n_n
                got = load(raw[:, n, 0:size].rearrange("p (k n) -> p k n", k=kk), v[:, k0:k0 + kk, :], dma_raw[n])
                o = slice(k0 * n_n, k0 * n_n + size)
                if not permute:
                    pieces = [(raw[:, n, 0:size], hi[:, o], lo[:, o])]
                else:
                    pieces = []
                    for k in range(kk):
                        r = raw[:, n, k * n_n:(k + 1) * n_n].rearrange("p (g r d) -> p r g d", r=2, d=HD)
                        h_, l_ = (t[:, (k0 + k) * n_n:(k0 + k + 1) * n_n].rearrange("p (r g d) -> p r g d", r=2, d=HD)
                                  for t in (hi, lo))
                        pieces += [(r[:, par], h_[:, par], l_[:, par]) for par in range(2)]
                AC.wait(got)
                VE.wait(got)
                for r, h_, l_ in pieces:
                    hi_done = act(h_, r, ACT.Copy, act_w, scale=scale)
                    VE.wait(hi_done)
                    mark = stt(l_, r, scale, f32(h_), ALU.mult, ALU.subtract, dve_set)
                raw_free[n] = [mark]
            return mark

        gelu_free = [[] for _ in range(NGELU)]
        hid_free = [[] for _ in range(NHID)]
        counts = {"gelu": 0, "hid": 0, "exp": 0, "bias": 0, "x": 0, "probs": 0, "s": 0, "pX": 0, "pC": 0}
        exp_free = [[] for _ in range(NEXP)]
        st = {}

        def split_T(bank, hi, lo, before, values=None):
            AC.wait(*before)
            src = flat(pD[:, bank, :, :]) if values is None else values
            h = act(flat(hi[:, :, :]), src, ACT.Copy, act_dense)
            VE.wait(h)
            return tt(VE, flat(lo[:, :, :]), src, f32(flat(hi[:, :, :])), ALU.subtract, dve_dense)

        def transposed(src_nat, before):
            n = take_bank()
            PE.wait(*before)
            for k in range(K):
                for t in range(T):
                    m = transpose(pD[:, n, k, t * P:(t + 1) * P], src_nat[:, t, k * P:(k + 1) * P],
                                  pe_tr if (k, t) == (K - 1, T - 1) else None)
            return n, m

        def layer_norm(srcs, eps, dst, before, dst_free=()):
            VE.wait(*before)
            VE.wait(st.get("norm_read"))
            for t in range(T):
                s = VE.run(lambda e, t=t: e.bn_stats(stats[:, t, :], srcs[t]), dve_small)
            VE.wait(s)
            for t in range(T):
                s = VE.run(lambda e, t=t: e.bn_aggr(mean_var[:, t, :], stats[:, t, :]), dve_small)
            PO.wait(s)
            p = PO.run(lambda e: e.tensor_scalar(rstd[:, :], mean_var[:, :, 1], eps, None, ALU.add), pool_norm)
            PO.wait(p)
            p = PO.run(lambda e: e.tensor_tensor(rstd[:, :], rstd[:, :], half_neg[:, :], ALU.pow), pool_norm)
            VE.wait(p, *dst_free)
            for t in range(T):
                s = VE.run(lambda e, t=t: e.tensor_scalar(dst[:, t, :], srcs[t], mean_var[:, t, 0:1],
                                                          rstd[:, t:t + 1], ALU.subtract, ALU.mult), dve_dense)
            st["norm_read"] = s
            return s

        def affine_T(bank, read, scales, shifts, hi, lo, free):
            n = counts["gelu"] % NGELU
            counts["gelu"] += 1
            AC.wait(read, *gelu_free[n], *free)
            buf = gelu_out[:, n, :, :]
            for k in range(K):
                m = act(buf[:, k, :], pD[:, bank, k, :], ACT.Identity, act_dense, bias=shifts[k], scale=scales[k])
            dense_free[bank].append(m)
            AC.wait(m)
            VE.wait(*free)
            lo_done = split_T(None, hi, lo, [], values=flat(buf))
            gelu_free[n] = [lo_done]
            return lo_done

        def hidden(bank, read, biases, func):
            g = counts["gelu"] % NGELU
            counts["gelu"] += 1
            s = counts["hid"] % NHID
            counts["hid"] += 1
            AC.wait(read, *gelu_free[g])
            for n in range(2):
                m = act(gelu_out[:, g, n, :], pD[:, bank, n, :], func, act_dense, bias=biases[n])
            dense_free[bank].append(m)
            AC.wait(m, *hid_free[s])
            src = flat(gelu_out[:, g, :, :])
            h = act(flat(hid_hi[:, s, :, :]), src, ACT.Copy, act_dense)
            PO.wait(h, *hid_free[s])
            low = tt(PO, flat(hid_lo[:, s, :, :]), src, f32(flat(hid_hi[:, s, :, :])), ALU.subtract, pool_lo)
            gelu_free[g] = [low]
            return s, low

        def open_out(sel, before):
            n = OUT
            PE.wait(*before, *dense_free[n])
            dense_free[n] = []
            rows = bias_rows[:, :].unsqueeze(1).to_broadcast([2 * NROWS, T, H])
            mm(pD[:, n, :, :], sel, rows, start=True)
            return n

        def add_residual(bank, hi, lo):
            for t in range(T):
                for k in range(K):
                    for part in (hi, lo):
                        mm(pD[:, bank, t, :], part[:, k, t * P:(t + 1) * P], eye[:, k, :])

        def load_x(b):
            SP.wait(st.get("x_nat_free"))
            st["x"] = load(x_nat[:, :, :], x_in[b].rearrange("(t p) h -> p t h", p=P), dma["x"])

        def load_expert(b, m2, reg):
            n = take_raw()
            wi = w["L1_cond_Wi"].rearrange("e (k p) n -> p e k n", p=P)
            wo = w["L1_cond_Wo"].rearrange("e (m p) n -> p e m n", p=P)
            half = K * H

            def start(e, src, dst, lo, hi, is_wi):
                r = reg["value"]
                s = wi[:, bass.ds(r, 1), :, lo:hi] if is_wi else wo[:, bass.ds(r, 1), lo:hi, :]
                return e.dma_start(dst, s.rearrange("p a k n -> p (a k) n"))
            SP.run(lambda e: start(e, None, raw[:, n, 0:half].rearrange("p (k n) -> p k n", k=K),
                                   m2 * 2 * P, (m2 + 1) * 2 * P, True), dma_raw[n], by=16)
            got = SP.run(lambda e: start(e, None, raw[:, n, half:2 * half].rearrange("p (m n) -> p m n", m=2),
                                         2 * m2, 2 * m2 + 2, False), dma_raw[n], by=16)
            s = counts["exp"] % NEXP
            counts["exp"] += 1
            AC.wait(got, *exp_free[s])
            h = act(exp_hi[:, s, :], raw[:, n, :], ACT.Copy, act_w)
            PO.wait(h, *exp_free[s])
            low = tt(PO, exp_lo[:, s, :], raw[:, n, :], f32(exp_hi[:, s, :]), ALU.subtract, pool_w)
            raw_free[n] = [low]
            return s, low

        def front(b):
            reg = {}

            def read_expert(e):
                reg["value"] = e.value_load(idx[0:1, 0, b:b + 1], min_val=0, max_val=E - 1)
            SP.wait(got_idx)
            SP.run(read_expert)
            pieces = [load_expert(b, 0, reg), load_expert(b, 1, reg)]
            VE.wait(st["x"], st.get("rot_free"))
            xg = x_nat[:, :, :].rearrange("p t (g j) -> p (t g) j", j=4)
            ag = rot_a[:, :, :].rearrange("p t (g j) -> p (t g) j", j=4)
            G = T * H // 4
            cos_b = rot_cos[:, b, :].unsqueeze(1).to_broadcast([P, G, 4])
            sin_b = rot_sin[:, b, :].unsqueeze(1).to_broadcast([P, G, 4])
            a = tt(VE, ag, xg, cos_b, ALU.mult, dve_dense)
            VE.wait(st.get("y_free"))
            yg = y_nat[:, :, :].rearrange("p t (g j) -> p (t g) j", j=4)
            for r in range(2):
                c = tt(VE, yg[:, :, r::2], xg[:, :, 1 - r::2], sin_b[:, :, r::2], ALU.mult, dve_dense)
            VE.wait(c)
            x0 = tt(VE, flat(x_nat[:, :, :]), flat(rot_a[:, :, :]), flat(y_nat[:, :, :]), ALU.add, dve_dense)
            bank, m = transposed(x_nat, [x0])
            st["x_nat_free"] = m
            if b + 1 < NB:
                load_x(b + 1)
            AC.wait(st.get("xa_free"))
            lo = split_T(bank, xa_hi, xa_lo, [m])
            dense_free[bank].append(lo)
            AC.wait(st.get("sel0_free"), st.get("sel1_free"))
            for n in range(2):
                sel = act(stage_sel[:, n, :], ones[:, :], ACT.Copy, act_dense, scale=select[:, n, b:b + 1])
            yield
            out = open_out(stage_sel[:, 0, :], [sel])
            PE.wait(lo)
            add_residual(out, xa_hi, xa_lo)
            xa = (xa_hi, xa_lo)

            def wide_in(m2, piece):
                s, low = piece
                PE.wait(low)
                bank = take_bank()
                for n in range(2):
                    terms = []
                    for k in range(K):
                        cs = slice(k * H + n * P, k * H + (n + 1) * P)
                        terms += split_terms((exp_hi[:, s, cs], exp_lo[:, s, cs]), (xa_hi[:, k, :], xa_lo[:, k, :]))
                    mark = products(pD[:, bank, n, :], terms, True, True, pe_dense)
                return hidden(bank, mark, [chosen[:, 2 * m2 + n, b:b + 1] for n in range(2)], ACT.Gelu)

            def wide_out(m2, piece, hid):
                s, _ = piece
                hs, low = hid
                PE.wait(low)
                for t in range(T):
                    terms = []
                    for n in range(2):
                        cs = slice(K * H + n * H, K * H + (n + 1) * H)
                        terms += split_terms(
                            (hid_hi[:, hs, n, t * P:(t + 1) * P], hid_lo[:, hs, n, t * P:(t + 1) * P]),
                            (exp_hi[:, s, cs], exp_lo[:, s, cs]))
                    mark = products(pD[:, out, t, :], terms, False, m2 == M // 2 - 1, pe_dense)
                hid_free[hs] = [mark]
                exp_free[s] = [mark]
                return mark

            hids = []
            for m2 in range(M // 2):
                hids.append(wide_in(m2, pieces[m2]))
                if m2:
                    wide_out(m2 - 1, pieces[m2 - 1], hids[m2 - 1])
                    if m2 + 1 < M // 2:
                        pieces.append(load_expert(b, m2 + 1, reg))
                yield
            mark = wide_out(M // 2 - 1, pieces[-1], hids[-1])
            st["sel0_free"] = mark
            y = layer_norm([pD[:, out, t, :] for t in range(T)], 1e-12, y_nat, [mark])
            dense_free[out].append(y)
            yield
            bank, m = transposed(y_nat, [y])
            lo = affine_T(bank, m, [chosen[:, M + k, b:b + 1] for k in range(K)],
                          [chosen[:, M + K + k, b:b + 1] for k in range(K)], xa_hi, xa_lo, [mark])
            yield
            out = open_out(stage_sel[:, 1, :], [sel])
            PE.wait(lo)
            add_residual(out, xa_hi, xa_lo)
            bank_a, bank_b = take_bank(), take_bank()
            h0 = counts["hid"] % NHID
            slots = [(h0 + i) % NHID for i in range(NHID)]
            for lane in (AC, VE):
                for s in slots:
                    lane.wait(*hid_free[s])
                for g in range(NGELU):
                    lane.wait(*gelu_free[g])
            PE.wait(*[m for s in slots for m in hid_free[s]])
            branch_of(b, out, bank_a, bank_b, slots)
            closed = mm(pD[:, out, :, :], zero_sel[:, :], bias_rows[:, :].unsqueeze(1).to_broadcast([R2, T, H]),
                        stop=True, sig=pe_dense)
            st["sel1_free"] = closed
            st["xa_free"] = closed
            dense_free[bank_a].append(closed)
            dense_free[bank_b].append(closed)
            for s in slots:
                hid_free[s] = [closed]
            for g in range(NGELU):
                gelu_free[g] = [closed]
            y = layer_norm([pD[:, out, t, :] for t in range(T)], 1e-5, y_nat, [closed], [m])
            dense_free[out].append(y)
            VE.wait(y)
            gb = [t_[:, :].unsqueeze(1).to_broadcast([P, T, H]) for t_ in (gamma2, beta2)]
            y = tt(VE, y_nat[:, :, :], y_nat[:, :, :], gb[0], ALU.mult, dve_dense)
            VE.wait(y)
            y = tt(VE, y_nat[:, :, :], y_nat[:, :, :], gb[1], ALU.add, dve_dense)
            y = layer_norm([y_nat[:, t, :] for t in range(T)], 1e-5, rot_a, [y])
            st["x2"] = y
            st["y_free"] = y
            yield

        zero_sel = sb("zero_sel", [R2, P], F32R)
        VE.run(lambda e: e.memset(f32(zero_sel[:, :]), 0.0), dve_set)

        def branch_of(b, out, bank_a, bank_b, slots):
            xa = [(xa_hi[:, k, :], xa_lo[:, k, :]) for k in range(K)]
            s0, s1, s2 = slots
            narrow0 = {s: s.count for s in (pe_n, act_n, dve_n)}
            deep0 = {s: s.count for s in (pe_r, act_r, dve_r)}
            pad = {pe_n: 1, act_n: 3, dve_n: 1, pe_r: 3, act_r: 9, dve_r: 3}

            def layer_T(e, bank, n, wt, width, ins, m):
                hi, lo = W[wt]
                count = 0
                for k, x_ in enumerate(ins):
                    cs = slice(k * width + m * P, k * width + (m + 1) * P)
                    for a_, b_ in split_terms((hi[:, cs], lo[:, cs]), x_):
                        last = e.matmul(pD[:, bank, n, :], a_, b_, start=count == 0,
                                        stop=count == 3 * len(ins) - 1, skip_group_check=True)
                        count += 1
                return last

            def layer_nat(e, wt, slot):
                hi, lo = W[wt]
                for t in range(T):
                    for n in range(2):
                        cs = slice(n * H, (n + 1) * H)
                        ts_ = slice(t * P, (t + 1) * P)
                        for a_, b_ in split_terms((hid_hi[:, slot, n, ts_], hid_lo[:, slot, n, ts_]),
                                                  (hi[:, cs], lo[:, cs])):
                            e.matmul(pD[:, out, t, :], a_, b_, start=False, stop=False, skip_group_check=True)

            def pe_narrow(e, name, with_out=True):
                for n in range(2):
                    last = layer_T(e, bank_a, n, "w1_" + name, H, xa, n)
                last.then_inc(pe_n.sem, 1)
                e.wait_ge(dve_n.sem, dve_n0 + 1)
                if with_out:
                    layer_nat(e, "w2_" + name, s0)
                e.sem_inc(pe_r.sem, pad[pe_r])

            def pe_deep(e):
                for m in range(4):
                    last = layer_T(e, (bank_a, bank_b)[m // 2], m % 2, "w1_sr", SR, xa, m)
                    if m % 2:
                        last.then_inc(pe_r.sem, 1)
                e.wait_ge(dve_r.sem, dve_r0 + 2)
                h1 = [(hid_hi[:, s, n, :], hid_lo[:, s, n, :]) for s in (s0, s1) for n in range(2)]
                for m in range(2):
                    last = layer_T(e, bank_a, m, "w2_sr", H, h1, m)
                last.then_inc(pe_r.sem, 1)
                e.wait_ge(dve_r.sem, dve_r0 + 3)
                layer_nat(e, "w3_sr", s2)
                e.sem_inc(pe_n.sem, pad[pe_n])

            def gelu_and_hi(e, bank, g, slot, biases, sem, base):
                for n in range(2):
                    e.activation(gelu_out[:, g, n, :], pD[:, bank, n, :], ACT.Gelu, bias=biases[n]).then_inc(sem, 1)
                e.wait_ge(sem, base + 2)
                e.activation(flat(hid_hi[:, slot, :, :]), flat(gelu_out[:, g, :, :]), ACT.Copy).then_inc(sem, 1)

            def act_narrow(e):
                e.wait_ge(pe_n.sem, pe_n0 + 1)
                gelu_and_hi(e, bank_a, 0, s0, [chosen[:, M + 2 * K + n, b:b + 1] for n in range(2)], act_n.sem, act_n0)
                e.sem_inc(act_r.sem, pad[act_r])

            def act_deep(e):
                for i, (bank, g, slot, name, first) in enumerate(
                        ((bank_a, 0, s0, "L2_cond_b1_sr", 0), (bank_b, 1, s1, "L2_cond_b1_sr", 2),
                         (bank_a, 0, s2, "L2_cond_b2_sr", 0))):
                    e.wait_ge(pe_r.sem, pe_r0 + i + 1)
                    gelu_and_hi(e, bank, g, slot, [col(name, first + n) for n in range(2)], act_r.sem, act_r0 + 3 * i)
                e.sem_inc(act_n.sem, pad[act_n])

            def lo_part(e, g, slot, sem):
                e.tensor_tensor(flat(hid_lo[:, slot, :, :]), flat(gelu_out[:, g, :, :]),
                                f32(flat(hid_hi[:, slot, :, :])), ALU.subtract).then_inc(sem, 1)

            def dve_narrow(e):
                e.wait_ge(act_n.sem, act_n0 + 3)
                lo_part(e, 0, s0, dve_n.sem)
                e.sem_inc(dve_r.sem, pad[dve_r])

            def dve_deep(e):
                for i, (g, slot) in enumerate(((0, s0), (1, s1), (0, s2))):
                    e.wait_ge(act_r.sem, act_r0 + 3 * i + 3)
                    lo_part(e, g, slot, dve_r.sem)
                e.sem_inc(dve_n.sem, pad[dve_n])

            pe_n0, act_n0, dve_n0 = (narrow0[s] for s in (pe_n, act_n, dve_n))
            pe_r0, act_r0, dve_r0 = (deep0[s] for s in (pe_r, act_r, dve_r))
            for s, n in pad.items():
                s.count += n

            def on_pe(e):
                c = e.value_load(idx[0:1, 1, b:b + 1])
                with e.If(c == 2):
                    pe_deep(e)
                with e.Else():
                    with e.If(c == 1):
                        pe_narrow(e, "tsr")
                    with e.Else():
                        with e.If(c == 0):
                            pe_narrow(e, "nr")
                        with e.Else():
                            pe_narrow(e, "nr", with_out=False)

            def two_way(deep, narrow):
                def make(e):
                    c = e.value_load(idx[0:1, 1, b:b + 1])
                    with e.If(c == 2):
                        deep(e)
                    with e.Else():
                        narrow(e)
                return make

            PE.run(on_pe)
            AC.run(two_way(act_deep, act_narrow))
            VE.run(two_way(dve_deep, dve_narrow))

        def load_mask(b):
            SP.wait(st.get("mask_u8_free"))
            got = load(mask_u8[:, :, :], mask_in[b, 0].rearrange("(t p) k -> p t k", p=P), dma["mask"])
            st["mask"] = got

        def make_mask(b):
            VE.wait(st["mask"], st.get("mask_add_free"))
            st["mask_u8_free"] = st["mask_ready"] = ts(
                VE, flat(mask_add[:, :, :]), flat(mask_u8[:, :, :]), MASKED, ALU.mult, dve_dense)

        def load_bias(b, h):
            n = counts["bias"] % NBIAS
            counts["bias"] += 1
            SP.wait(*bias_free[n])
            got = load(bias_ring[:, n, :, :],
                       fside_in[b, h].rearrange("(t p) k -> p t k", p=P), dma_bias[n])
            bias_at[(b, h)] = (n, got)

        bias_free = [[] for _ in range(NBIAS)]
        bias_at = {}
        bias_order = [(b, h) for b in range(NB) for h in range(NH)]
        bias_next = [0]

        def prefetch_bias(limit):
            while bias_next[0] < min(limit, len(bias_order)):
                load_bias(*bias_order[bias_next[0]])
                bias_next[0] += 1

        def qkv(b):
            bank, m = transposed(rot_a, [st["x2"]])
            st["rot_free"] = m
            lo = affine_T(bank, m, [mod[:, k, b:b + 1] for k in range(K)],
                          [mod[:, K + k, b:b + 1] for k in range(K)], xb_hi, xb_lo, [st.get("xb_free")])
            make_mask(b)
            if b + 1 < NB:
                load_mask(b + 1)
            PE.wait(lo)
            staged = []
            for name, bias_name in (("Wq", "L3_cond_bq"), ("Wk", "L3_cond_bk")):
                hi, lo_ = W[name]
                bank = take_bank()
                for par in range(2):
                    terms = []
                    for k in range(K):
                        cs = slice(k * H + par * P, k * H + (par + 1) * P)
                        terms += split_terms((hi[:, cs], lo_[:, cs]), (xb_hi[:, k, :], xb_lo[:, k, :]))
                    mark = products(pD[:, bank, par, :], terms, True, True, pe_dense)
                s = counts["hid"] % NHID
                counts["hid"] += 1
                AC.wait(mark, *hid_free[s])
                VE.wait(*hid_free[s])
                for par in range(2):
                    h = act(hid_hi[:, s, par, :], pD[:, bank, par, :], ACT.Identity, act_dense, bias=col(bias_name, par))
                VE.wait(h)
                for par in range(2):
                    l = stt(hid_lo[:, s, par, :], pD[:, bank, par, :], col(bias_name, par),
                            f32(hid_hi[:, s, par, :]), ALU.add, ALU.subtract, dve_dense)
                dense_free[bank].append(l)
                staged.append((s, l))
            SP.wait(st.get("stack_free"))
            for (s, l), stack, order in ((staged[0], q_stack, (0, 0, 1, 1)), (staged[1], k_stack, (0, 1, 0, 1))):
                SP.wait(l)
                for par in range(2):
                    for slot, part in enumerate(order):
                        src = (hid_hi, hid_lo)[part]
                        for g in range(NPAIR):
                            p0 = par * 4 * HD + slot * HD
                            done = load(f32(stack[p0:p0 + HD, g, :]), f32(src[g * HD:(g + 1) * HD, s, par, :]), dma["stack"])
            for s, _ in staged:
                hid_free[s] = [done]
            st["stack"] = done
            bank = open_out(v_sel[:, :], [])
            for t in range(T):
                terms = []
                for k in range(K):
                    cs = slice(k * H, (k + 1) * H)
                    terms += split_terms((xb_hi[:, k, t * P:(t + 1) * P], xb_lo[:, k, t * P:(t + 1) * P]),
                                         (W["Wv"][0][:, cs], W["Wv"][1][:, cs]))
                mark = products(pD[:, bank, t, :], terms, False, True, pe_dense)
            AC.wait(mark, st.get("v_free"))
            for t in range(T):
                v = act(v_aug[:, t, :, 0:HD], pD[:, bank, t, :].rearrange("p (h d) -> p h d", d=HD), ACT.Copy, act_dense)
            dense_free[bank].append(v)
            st["v"] = v
            yield

        s_free = [[], []]
        x_free = [[] for _ in range(NX)]
        pX_free = [[], []]
        probs_free = [[] for _ in range(NP_)]
        pC_free = []
        ctx_raw_free = [[], []]

        def attention(b):
            todo = {}

            def scores(h):
                g, par = h // 2, h % 2
                n, got = bias_at[(b, h)]
                PO.wait(got, st["mask_ready"])
                biased = tt(PO, bias_ring[:, n, :, :], bias_ring[:, n, :, :], mask_add[:, :, :], ALU.add, pool_bias)
                st["mask_add_free"] = biased
                PE.wait(st["stack"], *s_free[par])
                rows = slice(par * 4 * HD, (par + 1) * 4 * HD)
                for t in range(T):
                    m = mm(pS[:, par, t, :], q_stack[rows, g, t * P:(t + 1) * P], k_stack[rows, g, :],
                           True, True, sig=pe_s)
                st["stack_free"] = m
                xn = counts["x"] % NX
                counts["x"] += 1
                VE.wait(m, biased, *x_free[xn])
                for t in range(T):
                    mx = VE.run(lambda e, t=t: e.tensor_tensor_reduce(
                        x_scores[:, xn, t, :], pS[:, par, t, :], bias_ring[:, n, t, :], 1.0, -3.4e38,
                        ALU.add, ALU.max, row_max[:, xn, t:t + 1]), dve_max)
                s_free[par] = [mx]
                bias_free[n] = [mx]
                VE.wait(mx)
                for t in range(T):
                    sub = ts(VE, x_scores[:, xn, t, :], x_scores[:, xn, t, :], row_max[:, xn, t:t + 1],
                             ALU.subtract, dve_sub)
                prefetch_bias(bias_next[0] + 1)
                return (xn, sub)

            def exponentials(h, unit):
                xn, sub = unit
                xb = counts["pX"] % 2
                counts["pX"] += 1
                PE.wait(sub, *pX_free[xb])
                for t in range(T):
                    for k in range(K):
                        m = transpose(pX[:, xb, k, t * P:(t + 1) * P], x_scores[:, xn, t, k * P:(k + 1) * P],
                                      pe_x if (t, k) == (T - 1, K - 1) else None)
                x_free[xn] = [m]
                pb = counts["probs"] % NP_
                counts["probs"] += 1
                AC.wait(m, *probs_free[pb])
                e_ = act(flat(probs[:, pb, :, :]), flat(pX[:, xb, :, :]), ACT.Exp, act_exp)
                pX_free[xb] = [e_]
                return (h, pb, e_)

            def values(h, pb, e_):
                half = (h // 4) % 2
                q0 = 32 * (h % 4)
                if h % 4 == 0:
                    PE.wait(*pC_free)
                PE.wait(e_, st["v"])
                for k in range(K):
                    m = mm(pC[q0:q0 + 32, :], v_aug[:, k, h, :], probs[:, pb, k, :], k == 0, k == K - 1,
                           sig=pe_c if k == K - 1 else None, tile_position=(0, q0))
                probs_free[pb] = [m]
                if h % 4 == 3:
                    AC.wait(m, *ctx_raw_free[half])
                    c = act(ctx_raw[:, half, :], pC[:, :], ACT.Copy, act_dense)
                    pC_free[:] = [c]
                    todo["normalize"] = (h // 4, half, c)
                st["v_free"] = m

            def normalize(j, half, c):
                bank = take_bank()
                PE.wait(c)
                for t in range(T):
                    m = transpose(pD[:, bank, t, 0:P], ctx_raw[:, half, t * P:(t + 1) * P], pe_tr)
                ctx_raw_free[half] = [m]
                v = pD[:, bank, :, 0:P].rearrange("p t (h c) -> p t h c", c=32)
                VE.wait(m, st.get("rden_free"), st.get("ctx_nat_free"))
                r = VE.run(lambda e: e.reciprocal(rden[:, :, :], v[:, :, :, HD]), dve_small)
                VE.wait(r)
                for t in range(T):
                    o = ctx_nat[:, t, j * 4 * HD:(j + 1) * 4 * HD].rearrange("p (h d) -> p h d", d=HD)
                    done = tt(VE, o, v[:, t, :, 0:HD], rden[:, t, :].unsqueeze(2).to_broadcast([P, 4, HD]),
                              ALU.mult, dve_dense)
                st["rden_free"] = done
                st["ctx"] = done
                dense_free[bank].append(done)

            def maybe_normalize():
                if "normalize" in todo:
                    normalize(*todo.pop("normalize"))

            units = [scores(0), scores(1)]
            ready = None
            for h in range(NH):
                if h + 2 < NH:
                    units.append(scores(h + 2))
                if ready:
                    values(*ready)
                    maybe_normalize()
                ready = exponentials(h, units[h])
                if h % 2:
                    yield
            values(*ready)
            maybe_normalize()
            yield

        def tail(b):
            bank, m = transposed(ctx_nat, [st["ctx"]])
            st["ctx_nat_free"] = m
            AC.wait(st.get("xc_free"))
            lo = split_T(bank, xc_hi, xc_lo, [m])
            dense_free[bank].append(lo)
            out = open_out(stage_sel[:, 2, :], [])
            add_residual(out, xb_hi, xb_lo)
            PE.wait(lo)
            for t in range(T):
                terms = []
                for k in range(K):
                    cs = slice(k * H, (k + 1) * H)
                    terms += split_terms((xc_hi[:, k, t * P:(t + 1) * P], xc_lo[:, k, t * P:(t + 1) * P]),
                                         (W["Wo"][0][:, cs], W["Wo"][1][:, cs]))
                mark = products(pD[:, out, t, :], terms, False, True, pe_dense)
            st["xb_free"] = mark
            AC.wait(mark, st.get("xo_free"))
            xo = act(flat(xo_nat[:, :, :]), flat(pD[:, out, :, :]), ACT.Copy, act_dense)
            dense_free[out].append(xo)
            y = layer_norm([xo_nat[:, t, :] for t in range(T)], 1e-5, ffn_in, [xo], [st.get("ffn_in_free")])
            bank, m = transposed(ffn_in, [y])
            st["ffn_in_free"] = m
            lo = affine_T(bank, m, [col("L3_cond_g2", k) for k in range(K)],
                          [col("L3_cond_beta2", k) for k in range(K)], xc_hi, xc_lo, [mark])
            yield
            out = open_out(stage_sel[:, 3, :], [])
            PE.wait(lo)
            hids = []
            for m2 in range(M // 2 + 1):
                if m2 < M // 2:
                    bank = take_bank()
                    for n in range(2):
                        terms = []
                        for k in range(K):
                            c0 = k * FF + (2 * m2 + n) * P
                            cs = slice(c0, c0 + P)
                            terms += split_terms((W["W1"][0][:, cs], W["W1"][1][:, cs]), (xc_hi[:, k, :], xc_lo[:, k, :]))
                        mark = products(pD[:, bank, n, :], terms, True, True, pe_dense)
                    st["xc_free"] = mark
                    hids.append(hidden(bank, mark, [col("L3_cond_b1", 2 * m2 + n) for n in range(2)],
                                       ACT.Gelu_apprx_sigmoid))
                if m2:
                    hs, low = hids[m2 - 1]
                    PE.wait(low)
                    for t in range(T):
                        terms = []
                        for n in range(2):
                            c0 = (2 * (m2 - 1) + n) * H
                            cs = slice(c0, c0 + H)
                            terms += split_terms(
                                (hid_hi[:, hs, n, t * P:(t + 1) * P], hid_lo[:, hs, n, t * P:(t + 1) * P]),
                                (W["W2"][0][:, cs], W["W2"][1][:, cs]))
                        mark = products(pD[:, out, t, :], terms, False, m2 == M // 2, pe_dense)
                    hid_free[hs] = [mark]
                yield
            VE.wait(mark, xo)
            done = tt(VE, flat(xo_nat[:, :, :]), flat(pD[:, out, :, :]), flat(xo_nat[:, :, :]), ALU.add, dve_dense)
            dense_free[out].append(done)
            SP.wait(done)
            st["xo_free"] = load(out_d[b].rearrange("(t p) h -> p t h", p=P), xo_nat[:, :, :], dma["out"])
            yield

        ffn_in = sb("ffn_in", [P, T, H])

        load_x(0)
        load_mask(0)
        prefetch_bias(NBIAS)
        mark = None
        for name in ("w1_nr", "w2_nr", "w1_tsr", "w2_tsr", "w1_sr", "w2_sr", "w3_sr"):
            mark = split_weight(name, w["L2_cond_" + name])
        mark = split_weight("Wq", w["L3_cond_Wq"], permute=True, scale=QS_)
        mark = split_weight("Wk", w["L3_cond_Wk"], permute=True)
        for name in ("Wv", "Wo", "W1", "W2"):
            mark = split_weight(name, w["L3_cond_" + name])
        PE.wait(mark)

        def run(gen):
            for _ in gen:
                pass

        def weave(main, other):
            main, other = iter(main), iter(other)
            live = [main, other]
            while live:
                for g_ in list(live):
                    try:
                        next(g_)
                    except StopIteration:
                        live.remove(g_)

        run(front(0))
        run(qkv(0))
        for b in range(1, NB):
            weave(attention(b - 1), front(b))
            run(tail(b - 1))
            run(qkv(b))
        run(attention(NB - 1))
        run(tail(NB - 1))
        SP.wait((dma["out"], dma["out"].count))

        block = ctx.enter_context(nc.Block())
        block.tensor(PE.play)
        block.scalar(AC.play)
        block.vector(VE.play)
        block.gpsimd(PO.play)
        block.sync(SP.play)


_WEIGHTS = ["L1_cond_Wi", "L1_cond_bi", "L1_cond_Wo", "L1_cond_bo", "L1_cond_gamma", "L1_cond_beta",
            "L2_cond_w1_nr", "L2_cond_b1_nr", "L2_cond_w2_nr", "L2_cond_b2_nr", "L2_cond_w1_tsr", "L2_cond_b1_tsr",
            "L2_cond_w2_tsr", "L2_cond_b2_tsr", "L2_cond_w1_sr", "L2_cond_b1_sr", "L2_cond_w2_sr", "L2_cond_b2_sr",
            "L2_cond_w3_sr", "L2_cond_b3_sr", "L2_cond_gamma", "L2_cond_beta", "L3_cond_W_ada", "L3_cond_b_ada",
            "L3_cond_Wq", "L3_cond_bq", "L3_cond_Wk", "L3_cond_bk", "L3_cond_Wv", "L3_cond_bv", "L3_cond_Wo",
            "L3_cond_bo", "L3_cond_W1", "L3_cond_b1", "L3_cond_W2", "L3_cond_b2", "L3_cond_g2", "L3_cond_beta2"]
_DATA = ["x", "condB_theta", "condB_phi", "itok_B_0_7", "itok_B_0_2", "itok_B_34_63", "fside_Bx16xSxS_0",
         "mask_Bx1xSxS_bk0"]


def constant_table(experts, half):
    table = np.zeros((P, 4), np.float32)
    table[:half, C_FREQ] = np.exp(np.arange(half, dtype=np.float32) * np.float32(-np.log(10000.0) / (half - 1)))
    row = np.arange(P) % 32
    table[:, C_ROW] = row
    table[:, C_KIND] = (row >= experts) & (row < experts + 3)
    table[:, C_KIND + 1] = row < experts
    return table


def kernel(**inputs):
    import numpy as _np
    import concourse.bacc as _bacc
    from concourse import mybir as _mybir
    from concourse.bass_utils import run_bass_kernel_spmd as _run

    nc = _bacc.Bacc("TRN2", target_bir_lowering=False, num_devices=1)
    arrays, aps = {}, {}

    def declare(name, a):
        arrays[f"in_{name}"] = a
        aps[name] = nc.dram_tensor(f"in_{name}", a.shape, _mybir.dt.from_np(a.dtype), kind="ExternalInput").ap()

    for name in _DATA + _WEIGHTS:
        declare(name, _np.ascontiguousarray(inputs[name]))
    declare("consts", constant_table(inputs["L1_cond_Wi"].shape[0], inputs["x"].shape[2] // 2))
    out = nc.dram_tensor("out_0", inputs["x"].shape, _mybir.dt.float32, kind="ExternalOutput").ap()
    conditioned_stack(nc, *[aps[n] for n in _DATA], {n: aps[n] for n in _WEIGHTS}, aps["consts"], out)
    r = _run(nc, [arrays], core_ids=[0])
    return r.results[0]["out_0"]
```

```python
from contextlib import ExitStack

import numpy as np

import concourse.bass as bass
from concourse import mybir

P = 128
F32 = mybir.dt.float32
F32R = mybir.dt.float32r
I32 = mybir.dt.int32
U8 = mybir.dt.uint8
ALU = mybir.AluOpType
ACT = mybir.ActivationFunctionType

C_FREQ, C_ROW, C_KIND = 0, 1, 2
TWO_PI = 6.283185307179586
PI_A = 6.28125
PI_B = float(np.float32(TWO_PI - PI_A).view(np.uint32) & np.uint32(0xFFFFF000)) * 0 + float(
    (np.float32(TWO_PI - PI_A).view(np.uint32) & np.uint32(0xFFFFF000)).view(np.float32))
PI_C = TWO_PI - PI_A - PI_B
ROUND_MAGIC = 12582912.0
PI_BELOW = 3.1415925
MASKED = -1.0e30


ROOT_MAGIC = float(0x5F3759DF)


class Signal:

    def __init__(self, sem):
        self.sem, self.count = sem, 0


class Lane:

    def __init__(self):
        self.steps, self.waited = [], {}

    def wait(self, *marks):
        for mark in marks:
            if mark is None:
                continue
            signal, value = mark
            if self.waited.get(signal, 0) < value:
                self.waited[signal] = value
                self.steps.append(lambda e, s=signal.sem, v=value: e.wait_ge(s, v))

    def run(self, make, signal=None, by=1):
        if signal is None:
            self.steps.append(make)
            return None
        self.steps.append(lambda e: make(e).then_inc(signal.sem, by))
        signal.count += by
        return (signal, signal.count)

    def play(self, engine):
        for step in self.steps:
            step(engine)


def conditioned_stack(nc, x_in, theta_in, phi_in, expert_in, branch_in, step_in, fside_in, mask_in, w, consts_in, out_d):
    NB, S, H = x_in.shape
    NH = fside_in.shape[1]
    HD = H // NH
    E, _, FF = w["L1_cond_Wi"].shape
    T = S // P
    K = H // P
    M = FF // P
    NPAIR = NH // 2
    SR = w["L2_cond_w1_sr"].shape[1]
    assert (T, K, HD) == (2, 2, 16) and SR == 4 * P and FF == 8 * P

    ctx = ExitStack()
    with ctx:
        def sb(name, shape, dt=F32):
            return ctx.enter_context(nc.sbuf_tensor(name, shape, dt))

        def signal(name):
            return Signal(ctx.enter_context(nc.semaphore(name)))

        ident = sb("ident", [P, P])
        eye = sb("eye", [P, K, H], F32R)
        consts = sb("consts", [P, 4])
        W = {}
        for name, cols in (("w1_nr", K * H), ("w2_nr", K * H), ("w1_tsr", K * H), ("w2_tsr", K * H),
                           ("w1_sr", K * SR), ("w2_sr", SR // P * H), ("w3_sr", K * H),
                           ("Wq", K * H), ("Wk", K * H), ("Wv", K * H), ("Wo", K * H),
                           ("W1", K * FF), ("W2", M * H)):
            W[name] = (sb(name + "_hi", [P, cols], F32R), sb(name + "_lo", [P, cols], F32R))
        NRAW, NEXP = 2, 2
        raw = sb("raw", [P, NRAW, 2 * K * H])
        exp_hi = sb("exp_hi", [P, NEXP, 2 * K * H], F32R)
        exp_lo = sb("exp_lo", [P, NEXP, 2 * K * H], F32R)
        q_stack = sb("q_stack", [P, NPAIR, S], F32R)
        k_stack = sb("k_stack", [P, NPAIR, S], F32R)
        NBIAS = 4
        bias_ring = sb("bias_ring", [P, NBIAS, 2, S])
        NX = 3
        x_scores = sb("x_scores", [P, NX, 2, S])
        NP_ = 2
        probs = sb("probs", [P, NP_, K, S])
        v_aug = sb("v_aug", [P, T, NH, 32])
        ctx_raw = sb("ctx_raw", [P, S])
        ctx_nat = sb("ctx_nat", [P, T, H])
        mask_u8 = sb("mask_u8", [P, T, S], U8)
        mask_add = sb("mask_add", [P, T, S])
        NHID, NGELU = 3, 2
        gelu_out = sb("gelu_out", [P, NGELU, 2, S])
        hid_hi = sb("hid_hi", [P, NHID, 2, S], F32R)
        hid_lo = sb("hid_lo", [P, NHID, 2, S], F32R)
        xa_hi, xa_lo = sb("xa_hi", [P, K, S], F32R), sb("xa_lo", [P, K, S], F32R)
        xb = [(sb(f"xb_hi{i}", [P, K, S], F32R), sb(f"xb_lo{i}", [P, K, S], F32R)) for i in range(2)]
        xc_hi, xc_lo = sb("xc_hi", [P, K, S], F32R), sb("xc_lo", [P, K, S], F32R)
        x_nat = sb("x_nat", [P, T, H])
        rot_a = sb("rot_a", [P, T, H])
        y_nat = sb("y_nat", [P, T, H])
        xo_nat = sb("xo_nat", [P, T, H])
        gamma2 = sb("gamma2", [P, H])
        beta2 = sb("beta2", [P, H])
        rot_cos = sb("rot_cos", [P, NB, 4])
        rot_sin = sb("rot_sin", [P, NB, 4])
        N1 = M + 2 * K + K
        chosen = sb("chosen", [P, N1, NB])
        mod = sb("mod", [P, 2 * K, NB])
        NCOL = SR // P + K + 2 * K + K + K + M + 2 * K
        cols = sb("cols", [P, NCOL])
        NROWS = 32
        bias_raw = xo_nat[0:NROWS, 0, :]
        bias_rows = sb("bias_rows", [2 * NROWS, H], F32R)
        select = sb("select", [2 * NROWS, 4, NB])
        stage_sel = sb("stage_sel", [2 * NROWS, 4, P], F32R)
        ones = sb("ones", [2 * NROWS, P])
        idx = sb("idx", [1, 2, NB], I32)
        stats = sb("stats", [P, T, 6])
        mean_var = sb("mean_var", [P, T, 2])
        rstd = sb("rstd", [P, T])
        newton = sb("newton", [P, 3, T])
        row_max = sb("row_max", [P, NX, 2])
        rden = sb("rden", [P, T, 4])

        pS = ctx.enter_context(nc.psum_tensor("pS", [P, 2, T, S], F32))
        pX = ctx.enter_context(nc.psum_tensor("pX", [P, 2, K, S], F32))
        pC = ctx.enter_context(nc.psum_tensor("pC", [P, S], F32))
        ND, OUT = 2, 2
        pD = ctx.enter_context(nc.psum_tensor("pD", [P, ND + 1, 2, S], F32))

        dma = {n: signal("dma_" + n) for n in ("const", "cols", "rows", "x", "mask", "idx", "stack", "out", "bcast", "ada", "spill")}
        q_spill = nc.dram_tensor("q_spill", (2, 2, 2, HD * NPAIR * S), F32, kind="Internal").ap()
        k_spill = nc.dram_tensor("k_spill", (2, 2, 3, HD * NPAIR * S), F32, kind="Internal").ap()
        dma_raw = [signal(f"dma_raw{i}") for i in range(NRAW)]
        dma_bias = [signal(f"dma_bias{i}") for i in range(NBIAS)]
        pe_set, pe_dense, pe_tr, pe_s, pe_x, pe_c = (signal("pe_" + n) for n in ("set", "dense", "tr", "s", "x", "c"))
        act_set, act_dense, act_exp, act_w = (signal("act_" + n) for n in ("set", "dense", "exp", "w"))
        dve_set, dve_dense, dve_max, dve_sub, dve_small = (signal("dve_" + n) for n in ("set", "dense", "max", "sub", "small"))
        pool_set, pool_bias, pool_lo, pool_w = (signal("pool_" + n) for n in ("set", "bias", "lo", "w"))
        pe_n, act_n, dve_n = (signal(n) for n in ("pe_narrow", "act_narrow", "dve_narrow"))
        pe_r, act_r, dve_r = (signal(n) for n in ("pe_deep", "act_deep", "dve_deep"))

        PE, AC, VE, PO, SP = Lane(), Lane(), Lane(), Lane(), Lane()

        def flat(ap):
            return ap.rearrange("p a b -> p (a b)")

        def f32(ap):
            return ap.bitcast(F32)

        def mm(o, lhsT, rhs, start=False, stop=False, sig=None, **kw):
            return PE.run(lambda e: e.matmul(o, lhsT, rhs, start=start, stop=stop, skip_group_check=True, **kw), sig)

        def transpose(o, i, sig=None):
            return PE.run(lambda e: e.transpose(o, i, ident[:, :]), sig)

        def act(o, i, func, sig, bias=0.0, scale=1.0):
            return AC.run(lambda e: e.activation(o, i, func, bias=bias, scale=scale), sig)

        def tt(lane, o, a, b, op, sig):
            return lane.run(lambda e: e.tensor_tensor(o, a, b, op), sig)

        def ts(lane, o, a, s1, op0, sig, s2=None, op1=None):
            if op1 is None:
                return lane.run(lambda e: e.tensor_scalar(o, a, s1, None, op0), sig)
            return lane.run(lambda e: e.tensor_scalar(o, a, s1, s2, op0, op1), sig)

        def stt(o, a, s, b, op0, op1, sig):
            return VE.run(lambda e: e.scalar_tensor_tensor(o, a, s, b, op0, op1), sig)

        def split_terms(left, right):
            return [(left[0], right[0]), (left[0], right[1]), (left[1], right[0])]

        def products(o, terms, start, stop, sig=None):
            mark = None
            for n, (a, b) in enumerate(terms):
                last = n == len(terms) - 1
                mark = mm(o, a, b, start=start and n == 0, stop=stop and last, sig=sig if last else None)
            return mark

        dense_free = [[] for _ in range(ND + 1)]
        turn = {"dense": 0}

        def take_bank():
            n = turn["dense"] % ND
            turn["dense"] += 1
            PE.wait(*dense_free[n])
            dense_free[n] = []
            return n

        def load(dst, src, sig, **kw):
            return SP.run(lambda e: e.dma_start(dst, src, **kw), sig, by=16)

        load(consts[:, :], consts_in, dma["const"])
        load(idx[0:1, 0, :], expert_in.rearrange("(a b) -> a b", a=1), dma["idx"])
        got_idx = load(idx[0:1, 1, :], branch_in.rearrange("(a b) -> a b", a=1), dma["idx"])
        as_int = flat(rot_a[:, :, :]).bitcast(I32)
        scratch = flat(y_nat[:, :, :])
        for n, src in enumerate((expert_in, branch_in, step_in)):
            load(as_int[:, n * NB:(n + 1) * NB], src.partition_broadcast(P), dma["const"])
        ang = flat(x_nat[:, :, :])
        load(ang[:, 0:NB], theta_in.partition_broadcast(P), dma["const"])
        got_const = load(ang[:, NB:2 * NB], phi_in.partition_broadcast(P), dma["const"])

        col_at, at = {}, 0
        VECTORS = (("L2_cond_b1_sr", SR // P), ("L2_cond_b2_sr", K), ("L3_cond_b_ada", 2 * K), ("L3_cond_bq", K),
                   ("L3_cond_bk", K), ("L3_cond_b1", M), ("L3_cond_g2", K), ("L3_cond_beta2", K))
        vec_rows = [bias_ring[0:1, :, :, :].rearrange("p a b c -> p (a b c)"), flat(raw[0:1, :, :])]
        room = [NBIAS * 2 * S // P, NRAW * 2 * K * H // P]
        which, used = 0, 0
        vec_src = {}
        for name, n in VECTORS:
            if used + n > room[which]:
                which, used = which + 1, 0
            vec_src[name] = vec_rows[which][0:1, used * P:(used + n) * P]
            used += n
            got_cols = load(vec_src[name], w[name].rearrange("(a n) -> a n", a=1), dma["cols"])
            col_at[name] = at
            at += n

        def col(name, n=0):
            return cols[:, col_at[name] + n:col_at[name] + n + 1]

        rows_zero = VE.run(lambda e: e.memset(bias_raw, 0.0), dve_set)
        R_BRANCH, R_O, R_FF, R_V = E, E + 3, E + 4, E + 5
        SP.wait(rows_zero)
        load(bias_raw[0:E, :], w["L1_cond_bo"], dma["rows"])
        for r, name in ((R_BRANCH, "L2_cond_b2_nr"), (R_BRANCH + 1, "L2_cond_b2_tsr"), (R_BRANCH + 2, "L2_cond_b3_sr"),
                        (R_O, "L3_cond_bo"), (R_FF, "L3_cond_b2"), (R_V, "L3_cond_bv")):
            got_rows = load(bias_raw[r:r + 1, :], w[name].rearrange("(a n) -> a n", a=1), dma["rows"])
        scores_flat = x_scores[:, :, :, :].rearrange("p a b c -> p (a b c)")
        pick_bi = scores_flat[:, 0:FF + H]
        pick = flat(gelu_out[:, 0, :, :])
        load(pick_bi[0:E, 0:FF], w["L1_cond_bi"], dma["rows"])
        load(pick[0:E, 0:H], w["L1_cond_gamma"], dma["rows"])
        load(pick[0:E, H:2 * H], w["L1_cond_beta"], dma["rows"])
        load(pick_bi[0:1, FF:FF + H], w["L2_cond_b1_nr"].rearrange("(a n) -> a n", a=1), dma["rows"])
        got_rows = load(pick_bi[1:2, FF:FF + H], w["L2_cond_b1_tsr"].rearrange("(a n) -> a n", a=1), dma["rows"])
        load(gamma2[:, :], w["L2_cond_gamma"].partition_broadcast(P), dma["bcast"])
        got_bcast = load(beta2[:, :], w["L2_cond_beta"].partition_broadcast(P), dma["bcast"])

        PO.run(lambda e: e.memset(ident[:, :], 0.0), pool_set)
        PO.wait((pool_set, pool_set.count))
        got_ident = PO.run(lambda e: e.affine_select(out=ident[:, :], in_=ident[:, :], compare_op=ALU.not_equal,
                                                     fill=1.0, base=0, pattern=[[-1, P]], channel_multiplier=1),
                           pool_set)

        def vset(make):
            VE.wait((dve_set, dve_set.count))
            return VE.run(make, dve_set)

        VE.wait(got_ident)
        vset(lambda e: e.memset(f32(flat(eye[:, :, :])), 0.0))
        for k in range(K):
            vset(lambda e, k=k: e.tensor_copy(eye[:, k, k * P:(k + 1) * P], ident[:, :]))
        vset(lambda e: e.memset(ones[:, :], 1.0))
        vset(lambda e: e.memset(v_aug[:, :, :, :], 0.0))
        vset(lambda e: e.memset(v_aug[:, :, :, HD:HD + 1], 1.0))
        vset(lambda e: e.memset(select[:, :, :], 0.0))

        VE.wait(got_const)
        as_float = scratch[:, 0:3 * NB]
        vset(lambda e: e.tensor_copy(as_float, as_int[:, 0:3 * NB]))
        fx, fc, fs = (scratch[:, n * NB:(n + 1) * NB] for n in range(3))
        row_id = consts[:, C_ROW:C_ROW + 1]
        R2 = 2 * NROWS
        vset(lambda e: e.tensor_scalar(select[:, 0, :], fx[0:R2, :], row_id[0:R2, :], None, ALU.is_equal))
        vset(lambda e: e.tensor_scalar(select[:, 1, :], fc[0:R2, :], float(R_BRANCH), row_id[0:R2, :], ALU.add, ALU.is_equal))
        kind = consts[:, C_KIND:C_KIND + 1]
        vset(lambda e: e.tensor_scalar(select[:, 1, :], select[:, 1, :], kind[0:R2, :], None, ALU.mult))
        expert_row = consts[:, C_KIND + 1:C_KIND + 2]
        vset(lambda e: e.tensor_scalar(select[:, 0, :], select[:, 0, :], expert_row[0:R2, :], None, ALU.mult))
        branch_hot = scratch[:, 3 * NB:4 * NB]
        vset(lambda e: e.tensor_scalar(branch_hot, fc, row_id, None, ALU.is_equal))
        onev = scratch[:, 4 * NB:4 * NB + 4]
        for n, r in ((2, R_O), (3, R_FF), (1, R_V)):
            vset(lambda e, n=n, r=r: e.tensor_scalar(onev[:, n:n + 1], row_id, float(r), None, ALU.is_equal))
        v_sel = sb("v_sel", [R2, P], F32R)
        vset(lambda e: e.tensor_scalar(v_sel[:, :], ones[:, :], onev[0:R2, 1:2], None, ALU.mult))
        vset(lambda e: e.tensor_scalar(stage_sel[:, 2, :], ones[:, :], onev[0:R2, 2:3], None, ALU.mult))
        got_sel = vset(lambda e: e.tensor_scalar(stage_sel[:, 3, :], ones[:, :], onev[0:R2, 3:4], None, ALU.mult))
        VE.wait(got_rows)
        vset(lambda e: e.tensor_copy(bias_rows[0:NROWS, :], bias_raw))
        vset(lambda e: e.tensor_tensor(bias_raw, bias_raw, f32(bias_rows[0:NROWS, :]), ALU.subtract))
        got_bias_rows = vset(lambda e: e.tensor_copy(bias_rows[NROWS:R2, :], bias_raw))
        n0 = take_bank()
        turn_ps = flat(pD[:, n0, :, :])
        VE.wait(got_cols)
        for name, room_ in (("L3_cond_bq", xo_nat[0:1, 1, :]), ("L3_cond_bk", x_nat[0:1, 1, :])):
            for par in range(2):
                permuted = vset(lambda e, row=vec_src[name], room_=room_, par=par: e.tensor_copy(
                    room_[:, par * P:(par + 1) * P].rearrange("a (d g) -> a d g", g=NPAIR),
                    row.rearrange("a (g r d) -> a r d g", r=2, d=HD)[:, par, :, :]))
            vec_src[name] = room_
        PE.wait(got_cols, permuted)
        for name, n in VECTORS:
            for i in range(n):
                row = vec_src[name][:, i * P:(i + 1) * P]
                c = col_at[name] + i
                turned = mm(turn_ps[:, c:c + 1], row, ones[0:1, 0:1], True, True, sig=pe_set)
        VE.wait(turned)
        dense_free[n0].append(vset(lambda e: e.tensor_copy(cols[:, :], turn_ps[:, 0:NCOL])))
        QS_ = float(HD) ** -0.5
        got_bq = vset(lambda e: e.tensor_scalar(cols[:, col_at["L3_cond_bq"]:col_at["L3_cond_bq"] + K],
                                                cols[:, col_at["L3_cond_bq"]:col_at["L3_cond_bq"] + K],
                                                QS_, None, ALU.mult))

        n0 = take_bank()
        pick_ps = flat(pD[:, n0, :, :])
        PE.wait(got_bias_rows, got_rows)
        for n in range(M):
            mm(pick_ps[:, n * NB:(n + 1) * NB], pick_bi[0:E, n * P:(n + 1) * P], select[0:E, 0, :], True, True)
        for n in range(2 * K):
            mm(pick_ps[:, (M + n) * NB:(M + n + 1) * NB], pick[0:E, n * P:(n + 1) * P], select[0:E, 0, :], True, True)
        for n in range(K):
            a = M + 2 * K + n
            got_pick = mm(pick_ps[:, a * NB:(a + 1) * NB], pick_bi[0:2, FF + n * P:FF + (n + 1) * P],
                          branch_hot[0:2, :], True, True, sig=pe_set)
        VE.wait(got_pick)
        got_chosen = vset(lambda e: e.tensor_copy(chosen[:, :, :].rearrange("p a b -> p (a b)"), pick_ps[:, 0:N1 * NB]))
        dense_free[n0].append(got_chosen)

        def sine(dst, src, turn_by, tmp):
            vset(lambda e: e.tensor_scalar(tmp, src, 1.0 / TWO_PI, 0.25 * turn_by, ALU.mult, ALU.add))
            vset(lambda e: e.tensor_scalar(tmp, tmp, ROUND_MAGIC, None, ALU.add))
            vset(lambda e: e.tensor_scalar(tmp, tmp, ROUND_MAGIC, None, ALU.subtract))
            vset(lambda e: e.scalar_tensor_tensor(dst, tmp, -PI_A, src, ALU.mult, ALU.add))
            vset(lambda e: e.scalar_tensor_tensor(dst, tmp, -PI_B, dst, ALU.mult, ALU.add))
            vset(lambda e: e.scalar_tensor_tensor(dst, tmp, -PI_C, dst, ALU.mult, ALU.add))
            vset(lambda e: e.tensor_scalar(dst, dst, turn_by * TWO_PI / 4, PI_BELOW, ALU.add, ALU.min))
            ready = vset(lambda e: e.tensor_scalar(dst, dst, -PI_BELOW, None, ALU.max))
            AC.wait(ready)
            done = act(dst, dst, ACT.Sin, act_set)
            AC.wait(done)
            VE.wait(done)
            return done

        tmp = scratch[:, 5 * NB:7 * NB]
        cos2, sin2 = ang[:, 2 * NB:4 * NB], ang[:, 4 * NB:6 * NB]
        sine(cos2, ang[:, 0:2 * NB], 1, tmp)
        sine(sin2, ang[:, 0:2 * NB], 0, tmp)
        for j in range(4):
            a = (j // 2) * NB
            vset(lambda e, j=j, a=a: e.tensor_copy(rot_cos[:, :, j], cos2[:, a:a + NB]))
            got_rot = vset(lambda e, j=j, a=a: e.tensor_scalar(rot_sin[:, :, j], sin2[:, a:a + NB],
                                                     1.0 if j % 2 == 0 else -1.0, None, ALU.mult))
        vset(lambda e: e.tensor_scalar(fs, fs, 0.01, 4000.0, ALU.mult, ALU.mult))
        e_arg = scratch[:, 7 * NB:8 * NB]
        vset(lambda e: e.tensor_scalar(e_arg, fs, consts[:, C_FREQ:C_FREQ + 1], None, ALU.mult))
        emb = scratch[:, 8 * NB:10 * NB]
        sine(emb[:, 0:NB], e_arg, 0, tmp[:, 0:NB])
        sine(emb[:, NB:2 * NB], e_arg, 1, tmp[:, 0:NB])
        emb_act = scratch[:, 10 * NB:12 * NB]
        got_emb = act(emb_act, emb, ACT.Silu, act_set)
        ada = probs[:, :, :, :].rearrange("p a b c -> p (a b c)")
        ada_v = ada.rearrange("p (k n) -> p k n", k=K)
        got_ada = load(ada_v, w["L3_cond_W_ada"].rearrange("(k p) n -> p k n", p=P), dma["ada"])
        n0 = take_bank()
        ada_ps = flat(pD[:, n0, :, :])
        PE.wait(got_emb, got_ada)
        for n in range(2 * K):
            for k in range(K):
                got_mod = mm(ada_ps[:, n * NB:(n + 1) * NB], ada_v[:, k, n * P:(n + 1) * P],
                             emb_act[:, k * NB:(k + 1) * NB], k == 0, k == K - 1, sig=pe_set)
        VE.wait(got_mod)
        for n in range(2 * K):
            mod_ready = vset(lambda e, n=n: e.tensor_scalar(mod[:, n, :], ada_ps[:, n * NB:(n + 1) * NB],
                                                col("L3_cond_b_ada", n), 1.0 if n < K else 0.0, ALU.add, ALU.add))
        dense_free[n0].append(mod_ready)
        setup_done = mod_ready
        for lane in (PE, AC, PO, SP, VE):
            lane.wait(setup_done, got_ident, got_sel, got_bq, got_rot, got_bcast, got_emb, got_idx)

        raw_free = [[] for _ in range(NRAW)]
        raw_n = [0]

        def take_raw():
            n = raw_n[0] % NRAW
            raw_n[0] += 1
            SP.wait(*raw_free[n])
            raw_free[n] = []
            return n

        def split_weight(name, src, permute=False, scale=1.0):
            hi, lo = W[name]
            k_n, n_n = src.shape[0] // P, src.shape[1]
            per = 1024 // n_n
            v = src.rearrange("(k p) n -> p k n", p=P)
            mark = None
            for k0 in range(0, k_n, per):
                kk = min(per, k_n - k0)
                n = take_raw()
                size = kk * n_n
                got = load(raw[:, n, 0:size].rearrange("p (k n) -> p k n", k=kk), v[:, k0:k0 + kk, :], dma_raw[n])
                o = slice(k0 * n_n, k0 * n_n + size)
                if not permute:
                    pieces = [(raw[:, n, 0:size], hi[:, o], lo[:, o])]
                else:
                    pieces = []
                    for k in range(kk):
                        r = raw[:, n, k * n_n:(k + 1) * n_n].rearrange("p (g r d) -> p r d g", r=2, d=HD)
                        h_, l_ = (t[:, (k0 + k) * n_n:(k0 + k + 1) * n_n].rearrange("p (r d g) -> p r d g", r=2, d=HD)
                                  for t in (hi, lo))
                        pieces += [(r[:, par], h_[:, par], l_[:, par]) for par in range(2)]
                AC.wait(got)
                VE.wait(got)
                for r, h_, l_ in pieces:
                    hi_done = act(h_, r, ACT.Copy, act_w, scale=scale)
                    VE.wait(hi_done)
                    mark = stt(l_, r, scale, f32(h_), ALU.mult, ALU.subtract, dve_set)
                raw_free[n] = [mark]
            return mark

        gelu_free = [[] for _ in range(NGELU)]
        hid_free = [[] for _ in range(NHID)]
        counts = {"gelu": 0, "hid": 0, "exp": 0, "bias": 0, "x": 0, "probs": 0, "s": 0, "pX": 0, "pC": 0}
        exp_free = [[] for _ in range(NEXP)]
        st = {}

        def split_T(bank, hi, lo, before, values=None):
            AC.wait(*before)
            src = flat(pD[:, bank, :, :]) if values is None else values
            h = act(flat(hi[:, :, :]), src, ACT.Copy, act_dense)
            VE.wait(h)
            return tt(VE, flat(lo[:, :, :]), src, f32(flat(hi[:, :, :])), ALU.subtract, dve_dense)

        def transposed(src_nat, before):
            n = take_bank()
            PE.wait(*before)
            for k in range(K):
                for t in range(T):
                    m = transpose(pD[:, n, k, t * P:(t + 1) * P], src_nat[:, t, k * P:(k + 1) * P],
                                  pe_tr if (k, t) == (K - 1, T - 1) else None)
            return n, m

        def root_steps(eps):
            half, square = newton[:, 0, :], newton[:, 1, :]
            as_i, ve = rstd[:, :].bitcast(I32), newton[:, 2, :]

            def small(make):
                VE.wait((dve_small, dve_small.count))
                return VE.run(make, dve_small)
            small(lambda e: e.tensor_scalar(ve, mean_var[:, :, 1], eps, None, ALU.add))
            small(lambda e: e.tensor_scalar(half, mean_var[:, :, 1], eps, -0.5, ALU.add, ALU.mult))
            small(lambda e: e.tensor_scalar(as_i, ve.bitcast(I32), 1, None, ALU.logical_shift_right))
            small(lambda e: e.tensor_scalar(as_i, as_i, -1.0, ROOT_MAGIC, ALU.mult, ALU.add))
            for _ in range(3):
                small(lambda e: e.tensor_tensor(square, rstd[:, :], rstd[:, :], ALU.mult))
                small(lambda e: e.tensor_tensor(square, square, half, ALU.mult))
                s = small(lambda e: e.scalar_tensor_tensor(rstd[:, :], square, 1.5, rstd[:, :], ALU.add, ALU.mult))
            VE.wait(s)

        def layer_norm(srcs, eps, dst, before, dst_free=()):
            VE.wait(*before)
            VE.wait(st.get("norm_read"))
            for t in range(T):
                s = VE.run(lambda e, t=t: e.bn_stats(stats[:, t, :], srcs[t]), dve_small)
            VE.wait(s)
            for t in range(T):
                s = VE.run(lambda e, t=t: e.bn_aggr(mean_var[:, t, :], stats[:, t, :]), dve_small)
            root_steps(eps)
            VE.wait(*dst_free)
            for t in range(T):
                s = VE.run(lambda e, t=t: e.tensor_scalar(dst[:, t, :], srcs[t], mean_var[:, t, 0:1],
                                                          rstd[:, t:t + 1], ALU.subtract, ALU.mult), dve_dense)
            st["norm_read"] = s
            return s

        def affine_T(bank, read, scales, shifts, hi, lo, free):
            n = counts["gelu"] % NGELU
            counts["gelu"] += 1
            AC.wait(read, *gelu_free[n], *free)
            buf = gelu_out[:, n, :, :]
            for k in range(K):
                m = act(buf[:, k, :], pD[:, bank, k, :], ACT.Identity, act_dense, bias=shifts[k], scale=scales[k])
            dense_free[bank].append(m)
            AC.wait(m)
            VE.wait(*free)
            lo_done = split_T(None, hi, lo, [], values=flat(buf))
            gelu_free[n] = [lo_done]
            return lo_done

        def hidden(bank, read, biases, func, lane, sig):
            g = counts["gelu"] % NGELU
            counts["gelu"] += 1
            s = counts["hid"] % NHID
            counts["hid"] += 1
            src = flat(gelu_out[:, g, :, :])
            AC.wait(read)
            if func == ACT.Gelu:
                AC.wait(*gelu_free[g])
                for n in range(2):
                    m = act(gelu_out[:, g, n, :], pD[:, bank, n, :], func, act_dense, bias=biases[n])
                dense_free[bank].append(m)
            else:
                for n in range(2):
                    z = act(pD[:, bank, n, :], pD[:, bank, n, :], ACT.Identity, act_dense, bias=biases[n])
                AC.wait(z, *gelu_free[g])
                th = act(src, flat(pD[:, bank, :, :]), ACT.Tanh, act_dense, scale=1.702 / 2)
                VE.wait(th)
                m = stt(src, src, 1.0, flat(pD[:, bank, :, :]), ALU.add, ALU.mult, dve_dense)
                dense_free[bank].append(m)
            AC.wait(m, *hid_free[s])
            h = act(flat(hid_hi[:, s, :, :]), src, ACT.Copy, act_dense)
            lane.wait(h, *hid_free[s])
            low = tt(lane, flat(hid_lo[:, s, :, :]), src, f32(flat(hid_hi[:, s, :, :])), ALU.subtract, sig)
            gelu_free[g] = [low]
            return s, low

        def open_out(sel, before):
            n = OUT
            PE.wait(*before, *dense_free[n])
            dense_free[n] = []
            rows = bias_rows[:, :].unsqueeze(1).to_broadcast([2 * NROWS, T, H])
            mm(pD[:, n, :, :], sel, rows, start=True)
            return n

        def add_residual(bank, hi, lo):
            for t in range(T):
                for k in range(K):
                    for part in (hi, lo):
                        mm(pD[:, bank, t, :], part[:, k, t * P:(t + 1) * P], eye[:, k, :])

        def load_x(b):
            SP.wait(st.get("x_nat_free"))
            st["x"] = load(x_nat[:, :, :], x_in[b].rearrange("(t p) h -> p t h", p=P), dma["x"])

        expert_reg = {}

        def fetch_expert(b, m2):
            n = take_raw()
            wi = w["L1_cond_Wi"].rearrange("e (k p) n -> p e k n", p=P)
            wo = w["L1_cond_Wo"].rearrange("e (m p) n -> p e m n", p=P)
            half = K * H

            def read_expert(e):
                expert_reg[b] = e.value_load(idx[0:1, 0, b:b + 1], min_val=0, max_val=E - 1)

            def start(e, dst, first):
                r = bass.ds(expert_reg[b], 1)
                src = (wi[:, r, :, m2 * 2 * P:(m2 + 1) * 2 * P] if first else wo[:, r, 2 * m2:2 * m2 + 2, :])
                return e.dma_start(dst, src.rearrange("p a k n -> p (a k) n"))
            if m2 == 0:
                SP.run(read_expert)
            SP.run(lambda e: start(e, raw[:, n, 0:half].rearrange("p (k n) -> p k n", k=K), True), dma_raw[n], by=16)
            got = SP.run(lambda e: start(e, raw[:, n, half:2 * half].rearrange("p (m n) -> p m n", m=2), False),
                         dma_raw[n], by=16)
            fetched[(b, m2)] = (n, got)

        def split_expert(b, m2, lane, sig):
            n, got = fetched[(b, m2)]
            s = counts["exp"] % NEXP
            counts["exp"] += 1
            AC.wait(got, *exp_free[s])
            h = act(exp_hi[:, s, :], raw[:, n, :], ACT.Copy, act_w)
            lane.wait(h, *exp_free[s])
            low = tt(lane, exp_lo[:, s, :], raw[:, n, :], f32(exp_hi[:, s, :]), ALU.subtract, sig)
            raw_free[n] = [low]
            pieces[(b, m2)] = (s, low)

        fetched, pieces = {}, {}

        def rotate(b):
            VE.wait(st["x"], st.get("rot_free"))
            xg = x_nat[:, :, :].rearrange("p t (g j) -> p (t g) j", j=4)
            ag = rot_a[:, :, :].rearrange("p t (g j) -> p (t g) j", j=4)
            G = T * H // 4
            cos_b = rot_cos[:, b, :].unsqueeze(1).to_broadcast([P, G, 4])
            sin_b = rot_sin[:, b, :].unsqueeze(1).to_broadcast([P, G, 4])
            a = tt(VE, ag, xg, cos_b, ALU.mult, dve_dense)
            VE.wait(st.get("y_free"))
            yg = y_nat[:, :, :].rearrange("p t (g j) -> p (t g) j", j=4)
            for r in range(2):
                c = tt(VE, yg[:, :, r::2], xg[:, :, 1 - r::2], sin_b[:, :, r::2], ALU.mult, dve_dense)
            VE.wait(c)
            st["x0"] = tt(VE, flat(x_nat[:, :, :]), flat(rot_a[:, :, :]), flat(y_nat[:, :, :]), ALU.add, dve_dense)

        def turn_input(b):
            bank, m = transposed(x_nat, [st["x0"]])
            st["x_nat_free"] = m
            if b + 1 < NB:
                load_x(b + 1)
            AC.wait(st.get("xa_free"))
            lo = split_T(bank, xa_hi, xa_lo, [m])
            dense_free[bank].append(lo)
            AC.wait(st.get("sel0_free"), st.get("sel1_free"))
            for n in range(2):
                sel = act(stage_sel[:, n, :], ones[:, :], ACT.Copy, act_dense, scale=select[:, n, b:b + 1])
            st["x0T"], st["sel"] = lo, sel

        def wide(b):
            out = open_out(stage_sel[:, 0, :], [st["sel"]])
            PE.wait(st["x0T"])
            add_residual(out, xa_hi, xa_lo)

            def wide_in(m2, piece):
                s, low = piece
                PE.wait(low)
                bank = take_bank()
                for n in range(2):
                    terms = []
                    for k in range(K):
                        cs = slice(k * H + n * P, k * H + (n + 1) * P)
                        terms += split_terms((exp_hi[:, s, cs], exp_lo[:, s, cs]), (xa_hi[:, k, :], xa_lo[:, k, :]))
                    mark = products(pD[:, bank, n, :], terms, True, True, pe_dense)
                return hidden(bank, mark, [chosen[:, 2 * m2 + n, b:b + 1] for n in range(2)], ACT.Gelu, VE, dve_dense)

            def wide_out(m2, piece, hid):
                s, _ = piece
                hs, low = hid
                PE.wait(low)
                for t in range(T):
                    terms = []
                    for n in range(2):
                        cs = slice(K * H + n * H, K * H + (n + 1) * H)
                        terms += split_terms(
                            (hid_hi[:, hs, n, t * P:(t + 1) * P], hid_lo[:, hs, n, t * P:(t + 1) * P]),
                            (exp_hi[:, s, cs], exp_lo[:, s, cs]))
                    mark = products(pD[:, out, t, :], terms, False, m2 == M // 2 - 1, pe_dense)
                hid_free[hs] = [mark]
                exp_free[s] = [mark]
                return mark

            hids = []
            for m2 in range(M // 2):
                hids.append(wide_in(m2, pieces[(b, m2)]))
                yield
                if m2:
                    wide_out(m2 - 1, pieces[(b, m2 - 1)], hids[m2 - 1])
                    if m2 + 1 < M // 2:
                        split_expert(b, m2 + 1, VE, dve_dense)
                    if b + 1 < NB and m2 >= 2:
                        fetch_expert(b + 1, m2 - 2)
                    yield
            mark = wide_out(M // 2 - 1, pieces[(b, M // 2 - 1)], hids[-1])
            st["sel0_free"] = st["wide"] = mark
            yield

        def norm1(b):
            y = layer_norm([pD[:, OUT, t, :] for t in range(T)], 1e-12, y_nat, [st["wide"]])
            dense_free[OUT].append(y)
            yield
            bank, m = transposed(y_nat, [y])
            st["y_turned"] = m
            st["x1T"] = affine_T(bank, m, [chosen[:, M + k, b:b + 1] for k in range(K)],
                                 [chosen[:, M + K + k, b:b + 1] for k in range(K)], xa_hi, xa_lo, [st["wide"]])
            yield

        def branch(b):
            out = open_out(stage_sel[:, 1, :], [st["sel"]])
            PE.wait(st["x1T"])
            add_residual(out, xa_hi, xa_lo)
            bank_a, bank_b = take_bank(), take_bank()
            h0 = counts["hid"] % NHID
            slots = [(h0 + i) % NHID for i in range(NHID)]
            for lane in (AC, VE):
                for s in slots:
                    lane.wait(*hid_free[s])
                for g in range(NGELU):
                    lane.wait(*gelu_free[g])
            PE.wait(*[m for s in slots for m in hid_free[s]])
            branch_of(b, out, bank_a, bank_b, slots)
            closed = mm(pD[:, out, :, :], zero_sel[:, :], bias_rows[:, :].unsqueeze(1).to_broadcast([R2, T, H]),
                        stop=True, sig=pe_dense)
            st["sel1_free"] = closed
            st["xa_free"] = closed
            dense_free[bank_a].append(closed)
            dense_free[bank_b].append(closed)
            for s in slots:
                hid_free[s] = [closed]
            for g in range(NGELU):
                gelu_free[g] = [closed]
            st["branch"] = closed

        def norm23(b):
            y = layer_norm([pD[:, OUT, t, :] for t in range(T)], 1e-5, y_nat, [st["branch"]], [st["y_turned"]])
            dense_free[OUT].append(y)
            yield
            VE.wait(y)
            gb = [t_[:, :].unsqueeze(1).to_broadcast([P, T, H]) for t_ in (gamma2, beta2)]
            y = tt(VE, y_nat[:, :, :], y_nat[:, :, :], gb[0], ALU.mult, dve_dense)
            VE.wait(y)
            y = tt(VE, y_nat[:, :, :], y_nat[:, :, :], gb[1], ALU.add, dve_dense)
            yield
            y = layer_norm([y_nat[:, t, :] for t in range(T)], 1e-5, rot_a, [y])
            st["x2"] = y
            st["y_free"] = y
            yield

        zero_sel = sb("zero_sel", [R2, P], F32R)
        VE.run(lambda e: e.memset(f32(zero_sel[:, :]), 0.0), dve_set)

        def branch_of(b, out, bank_a, bank_b, slots):
            xa = [(xa_hi[:, k, :], xa_lo[:, k, :]) for k in range(K)]
            s0, s1, s2 = slots
            narrow0 = {s: s.count for s in (pe_n, act_n, dve_n)}
            deep0 = {s: s.count for s in (pe_r, act_r, dve_r)}
            pad = {pe_n: 1, act_n: 3, dve_n: 1, pe_r: 3, act_r: 9, dve_r: 3}

            def layer_T(e, bank, n, wt, width, ins, m):
                hi, lo = W[wt]
                count = 0
                for k, x_ in enumerate(ins):
                    cs = slice(k * width + m * P, k * width + (m + 1) * P)
                    for a_, b_ in split_terms((hi[:, cs], lo[:, cs]), x_):
                        last = e.matmul(pD[:, bank, n, :], a_, b_, start=count == 0,
                                        stop=count == 3 * len(ins) - 1, skip_group_check=True)
                        count += 1
                return last

            def layer_nat(e, wt, slot):
                hi, lo = W[wt]
                for t in range(T):
                    for n in range(2):
                        cs = slice(n * H, (n + 1) * H)
                        ts_ = slice(t * P, (t + 1) * P)
                        for a_, b_ in split_terms((hid_hi[:, slot, n, ts_], hid_lo[:, slot, n, ts_]),
                                                  (hi[:, cs], lo[:, cs])):
                            e.matmul(pD[:, out, t, :], a_, b_, start=False, stop=False, skip_group_check=True)

            def pe_narrow(e, name, with_out=True):
                for n in range(2):
                    last = layer_T(e, bank_a, n, "w1_" + name, H, xa, n)
                last.then_inc(pe_n.sem, 1)
                e.wait_ge(dve_n.sem, dve_n0 + 1)
                if with_out:
                    layer_nat(e, "w2_" + name, s0)
                e.sem_inc(pe_r.sem, pad[pe_r])

            def pe_deep(e):
                for m in range(4):
                    last = layer_T(e, (bank_a, bank_b)[m // 2], m % 2, "w1_sr", SR, xa, m)
                    if m % 2:
                        last.then_inc(pe_r.sem, 1)
                e.wait_ge(dve_r.sem, dve_r0 + 2)
                h1 = [(hid_hi[:, s, n, :], hid_lo[:, s, n, :]) for s in (s0, s1) for n in range(2)]
                for m in range(2):
                    last = layer_T(e, bank_a, m, "w2_sr", H, h1, m)
                last.then_inc(pe_r.sem, 1)
                e.wait_ge(dve_r.sem, dve_r0 + 3)
                layer_nat(e, "w3_sr", s2)
                e.sem_inc(pe_n.sem, pad[pe_n])

            def gelu_and_hi(e, bank, g, slot, biases, sem, base):
                for n in range(2):
                    e.activation(gelu_out[:, g, n, :], pD[:, bank, n, :], ACT.Gelu, bias=biases[n]).then_inc(sem, 1)
                e.wait_ge(sem, base + 2)
                e.activation(flat(hid_hi[:, slot, :, :]), flat(gelu_out[:, g, :, :]), ACT.Copy).then_inc(sem, 1)

            def act_narrow(e):
                e.wait_ge(pe_n.sem, pe_n0 + 1)
                gelu_and_hi(e, bank_a, 0, s0, [chosen[:, M + 2 * K + n, b:b + 1] for n in range(2)], act_n.sem, act_n0)
                e.sem_inc(act_r.sem, pad[act_r])

            def act_deep(e):
                for i, (bank, g, slot, name, first) in enumerate(
                        ((bank_a, 0, s0, "L2_cond_b1_sr", 0), (bank_b, 1, s1, "L2_cond_b1_sr", 2),
                         (bank_a, 0, s2, "L2_cond_b2_sr", 0))):
                    e.wait_ge(pe_r.sem, pe_r0 + i + 1)
                    gelu_and_hi(e, bank, g, slot, [col(name, first + n) for n in range(2)], act_r.sem, act_r0 + 3 * i)
                e.sem_inc(act_n.sem, pad[act_n])

            def lo_part(e, g, slot, sem):
                e.tensor_tensor(flat(hid_lo[:, slot, :, :]), flat(gelu_out[:, g, :, :]),
                                f32(flat(hid_hi[:, slot, :, :])), ALU.subtract).then_inc(sem, 1)

            def dve_narrow(e):
                e.wait_ge(act_n.sem, act_n0 + 3)
                lo_part(e, 0, s0, dve_n.sem)
                e.sem_inc(dve_r.sem, pad[dve_r])

            def dve_deep(e):
                for i, (g, slot) in enumerate(((0, s0), (1, s1), (0, s2))):
                    e.wait_ge(act_r.sem, act_r0 + 3 * i + 3)
                    lo_part(e, g, slot, dve_r.sem)
                e.sem_inc(dve_n.sem, pad[dve_n])

            pe_n0, act_n0, dve_n0 = (narrow0[s] for s in (pe_n, act_n, dve_n))
            pe_r0, act_r0, dve_r0 = (deep0[s] for s in (pe_r, act_r, dve_r))
            for s, n in pad.items():
                s.count += n

            def on_pe(e):
                c = e.value_load(idx[0:1, 1, b:b + 1])
                with e.If(c == 2):
                    pe_deep(e)
                with e.Else():
                    with e.If(c == 1):
                        pe_narrow(e, "tsr")
                    with e.Else():
                        with e.If(c == 0):
                            pe_narrow(e, "nr")
                        with e.Else():
                            pe_narrow(e, "nr", with_out=False)

            def two_way(deep, narrow):
                def make(e):
                    c = e.value_load(idx[0:1, 1, b:b + 1])
                    with e.If(c == 2):
                        deep(e)
                    with e.Else():
                        narrow(e)
                return make

            PE.run(on_pe)
            AC.run(two_way(act_deep, act_narrow))
            VE.run(two_way(dve_deep, dve_narrow))

        def load_mask(b):
            SP.wait(st.get("mask_u8_free"))
            got = load(mask_u8[:, :, :], mask_in[b, 0].rearrange("(t p) k -> p t k", p=P), dma["mask"])
            st["mask"] = got

        def make_mask(b):
            VE.wait(st["mask"], st.get("mask_add_free"))
            st["mask_u8_free"] = st["mask_ready"] = ts(
                VE, flat(mask_add[:, :, :]), flat(mask_u8[:, :, :]), MASKED, ALU.mult, dve_dense)

        def load_bias(b, h):
            n = counts["bias"] % NBIAS
            counts["bias"] += 1
            SP.wait(*bias_free[n])
            got = load(bias_ring[:, n, :, :],
                       fside_in[b, h].rearrange("(t p) k -> p t k", p=P), dma_bias[n])
            bias_at[(b, h)] = (n, got)

        bias_free = [[] for _ in range(NBIAS)]
        bias_at = {}
        bias_order = [(b, h) for b in range(NB) for h in range(NH)]
        bias_next = [0]

        def prefetch_bias(limit):
            while bias_next[0] < min(limit, len(bias_order)):
                load_bias(*bias_order[bias_next[0]])
                bias_next[0] += 1

        def qkv(b):
            xb_hi, xb_lo = xb[b % 2]
            bank, m = transposed(rot_a, [st["x2"]])
            st["rot_free"] = m
            lo = affine_T(bank, m, [mod[:, k, b:b + 1] for k in range(K)],
                          [mod[:, K + k, b:b + 1] for k in range(K)], xb_hi, xb_lo, [st.get(("xb_free", b % 2))])
            yield
            PE.wait(lo)
            staged = []
            for name, bias_name in (("Wq", "L3_cond_bq"), ("Wk", "L3_cond_bk")):
                hi, lo_ = W[name]
                bank = take_bank()
                for par in range(2):
                    terms = []
                    for k in range(K):
                        cs = slice(k * H + par * P, k * H + (par + 1) * P)
                        terms += split_terms((hi[:, cs], lo_[:, cs]), (xb_hi[:, k, :], xb_lo[:, k, :]))
                    mark = products(pD[:, bank, par, :], terms, True, True, pe_dense)
                s = counts["hid"] % NHID
                counts["hid"] += 1
                AC.wait(mark, *hid_free[s])
                VE.wait(*hid_free[s])
                for par in range(2):
                    h = act(hid_hi[:, s, par, :], pD[:, bank, par, :], ACT.Identity, act_dense, bias=col(bias_name, par))
                VE.wait(h)
                for par in range(2):
                    l = stt(hid_lo[:, s, par, :], pD[:, bank, par, :], col(bias_name, par),
                            f32(hid_hi[:, s, par, :]), ALU.add, ALU.subtract, dve_dense)
                dense_free[bank].append(l)
                staged.append((s, l))
            turn_ = b % 2
            for (s, l), spill, parts in ((staged[0], q_spill, (0, 1)), (staged[1], k_spill, (0, 1, 0))):
                SP.wait(l)
                for i, part in enumerate(parts):
                    out_ = spill[turn_, :, i].rearrange("r (p c) -> p r c", c=S)
                    spilled = load(out_, f32((hid_hi, hid_lo)[part][:, s, :, :]), dma["spill"])
            for s, _ in staged:
                hid_free[s] = [spilled]
            yield
            make_mask(b)
            if b + 1 < NB:
                load_mask(b + 1)
            SP.wait(spilled, st.get("stack_free"))
            for par in range(2):
                for half in range(2):
                    p0 = (2 * par + half) * 2 * HD
                    for spill, first, stack in ((q_spill, 0, q_stack), (k_spill, half, k_stack)):
                        src = spill[turn_, par, first:first + 2].rearrange("a (d gc) -> (a d) gc", d=HD)
                        done = load(f32(flat(stack[p0:p0 + 2 * HD, :, :])), src, dma["stack"])
            st["stack"] = done
            bank = open_out(v_sel[:, :], [])
            for t in range(T):
                terms = []
                for k in range(K):
                    cs = slice(k * H, (k + 1) * H)
                    terms += split_terms((xb_hi[:, k, t * P:(t + 1) * P], xb_lo[:, k, t * P:(t + 1) * P]),
                                         (W["Wv"][0][:, cs], W["Wv"][1][:, cs]))
                mark = products(pD[:, bank, t, :], terms, False, True, pe_dense)
            AC.wait(mark, st.get("v_free"))
            for t in range(T):
                v = act(v_aug[:, t, :, 0:HD], pD[:, bank, t, :].rearrange("p (h d) -> p h d", d=HD), ACT.Copy, act_dense)
            dense_free[bank].append(v)
            st["v"] = v
            yield

        s_free = [[], []]
        x_free = [[] for _ in range(NX)]
        pX_free = [[], []]
        probs_free = [[] for _ in range(NP_)]
        pC_free = []
        ctx_raw_free = []

        def attention(b):
            todo = {}

            def scores(h):
                g, par = h // 2, h % 2
                n, got = bias_at[(b, h)]
                PO.wait(got, st["mask_ready"])
                biased = tt(PO, bias_ring[:, n, :, :], bias_ring[:, n, :, :], mask_add[:, :, :], ALU.add, pool_bias)
                st["mask_add_free"] = biased
                PE.wait(st["stack"], *s_free[par])
                rows = slice(par * 4 * HD, (par + 1) * 4 * HD)
                for t in range(T):
                    m = mm(pS[:, par, t, :], q_stack[rows, g, t * P:(t + 1) * P], k_stack[rows, g, :],
                           True, True, sig=pe_s)
                st["stack_free"] = m
                xn = counts["x"] % NX
                counts["x"] += 1
                VE.wait(m, biased, *x_free[xn])
                for t in range(T):
                    mx = VE.run(lambda e, t=t: e.tensor_tensor_reduce(
                        x_scores[:, xn, t, :], pS[:, par, t, :], bias_ring[:, n, t, :], 1.0, -3.4e38,
                        ALU.add, ALU.max, row_max[:, xn, t:t + 1]), dve_max)
                s_free[par] = [mx]
                bias_free[n] = [mx]
                VE.wait(mx)
                for t in range(T):
                    sub = ts(VE, x_scores[:, xn, t, :], x_scores[:, xn, t, :], row_max[:, xn, t:t + 1],
                             ALU.subtract, dve_sub)
                prefetch_bias(bias_next[0] + 1)
                return (xn, sub)

            def exponentials(h, unit):
                xn, sub = unit
                xb = counts["pX"] % 2
                counts["pX"] += 1
                PE.wait(sub, *pX_free[xb])
                for t in range(T):
                    for k in range(K):
                        m = transpose(pX[:, xb, k, t * P:(t + 1) * P], x_scores[:, xn, t, k * P:(k + 1) * P],
                                      pe_x if (t, k) == (T - 1, K - 1) else None)
                x_free[xn] = [m]
                pb = counts["probs"] % NP_
                counts["probs"] += 1
                AC.wait(m, *probs_free[pb])
                e_ = act(flat(probs[:, pb, :, :]), flat(pX[:, xb, :, :]), ACT.Exp, act_exp)
                pX_free[xb] = [e_]
                return (h, pb, e_)

            def values(h, pb, e_):
                half = (h // 4) % 2
                q0 = 32 * (h % 4)
                if h % 4 == 0:
                    PE.wait(*pC_free)
                PE.wait(e_, st["v"])
                for k in range(K):
                    m = mm(pC[q0:q0 + 32, :], v_aug[:, k, h, :], probs[:, pb, k, :], k == 0, k == K - 1,
                           sig=pe_c if k == K - 1 else None, tile_position=(0, q0))
                probs_free[pb] = [m]
                if h % 4 == 3:
                    AC.wait(m, *ctx_raw_free)
                    c = act(ctx_raw[:, :], pC[:, :], ACT.Copy, act_dense)
                    pC_free[:] = [c]
                    todo["normalize"] = (h // 4, half, c)
                st["v_free"] = m

            def normalize(j, half, c):
                bank = take_bank()
                PE.wait(c)
                for t in range(T):
                    m = transpose(pD[:, bank, t, 0:P], ctx_raw[:, t * P:(t + 1) * P], pe_tr)
                ctx_raw_free[:] = [m]
                v = pD[:, bank, :, 0:P].rearrange("p t (h c) -> p t h c", c=32)
                VE.wait(m, st.get("rden_free"), st.get("ctx_nat_free"))
                r = VE.run(lambda e: e.reciprocal(rden[:, :, :], v[:, :, :, HD]), dve_small)
                VE.wait(r)
                for t in range(T):
                    o = ctx_nat[:, t, j * 4 * HD:(j + 1) * 4 * HD].rearrange("p (h d) -> p h d", d=HD)
                    done = tt(VE, o, v[:, t, :, 0:HD], rden[:, t, :].unsqueeze(2).to_broadcast([P, 4, HD]),
                              ALU.mult, dve_dense)
                st["rden_free"] = done
                st["ctx"] = done
                dense_free[bank].append(done)

            def maybe_normalize():
                if "normalize" in todo:
                    normalize(*todo.pop("normalize"))

            units = [scores(0), scores(1)]
            yield
            ready = None
            for h in range(NH):
                if h + 2 < NH:
                    units.append(scores(h + 2))
                yield
                if ready:
                    values(*ready)
                    maybe_normalize()
                ready = exponentials(h, units[h])
                yield
            values(*ready)
            maybe_normalize()
            yield

        def tail(b):
            xb_hi, xb_lo = xb[b % 2]
            bank, m = transposed(ctx_nat, [st["ctx"]])
            st["ctx_nat_free"] = m
            AC.wait(st.get("xc_free"))
            lo = split_T(bank, xc_hi, xc_lo, [m])
            dense_free[bank].append(lo)
            yield
            out = open_out(stage_sel[:, 2, :], [])
            add_residual(out, xb_hi, xb_lo)
            PE.wait(lo)
            for t in range(T):
                terms = []
                for k in range(K):
                    cs = slice(k * H, (k + 1) * H)
                    terms += split_terms((xc_hi[:, k, t * P:(t + 1) * P], xc_lo[:, k, t * P:(t + 1) * P]),
                                         (W["Wo"][0][:, cs], W["Wo"][1][:, cs]))
                mark = products(pD[:, out, t, :], terms, False, True, pe_dense)
            st["xb_free", b % 2] = mark
            AC.wait(mark, st.get("xo_free"))
            xo = act(flat(xo_nat[:, :, :]), flat(pD[:, out, :, :]), ACT.Copy, act_dense)
            dense_free[out].append(xo)
            y = layer_norm([xo_nat[:, t, :] for t in range(T)], 1e-5, ffn_in, [xo], [st.get("ffn_in_free")])
            yield
            bank, m = transposed(ffn_in, [y])
            st["ffn_in_free"] = m
            lo = affine_T(bank, m, [col("L3_cond_g2", k) for k in range(K)],
                          [col("L3_cond_beta2", k) for k in range(K)], xc_hi, xc_lo, [mark])
            yield
            out = open_out(stage_sel[:, 3, :], [])
            PE.wait(lo)
            hids = []
            for m2 in range(M // 2 + 1):
                if m2 < M // 2:
                    bank = take_bank()
                    for n in range(2):
                        terms = []
                        for k in range(K):
                            c0 = k * FF + (2 * m2 + n) * P
                            cs = slice(c0, c0 + P)
                            terms += split_terms((W["W1"][0][:, cs], W["W1"][1][:, cs]), (xc_hi[:, k, :], xc_lo[:, k, :]))
                        mark = products(pD[:, bank, n, :], terms, True, True, pe_dense)
                    st["xc_free"] = mark
                    hids.append(hidden(bank, mark, [col("L3_cond_b1", 2 * m2 + n) for n in range(2)],
                                       ACT.Tanh, PO, pool_lo))
                    yield
                if m2:
                    hs, low = hids[m2 - 1]
                    PE.wait(low)
                    for t in range(T):
                        terms = []
                        for n in range(2):
                            c0 = (2 * (m2 - 1) + n) * H
                            cs = slice(c0, c0 + H)
                            terms += split_terms(
                                (hid_hi[:, hs, n, t * P:(t + 1) * P], hid_lo[:, hs, n, t * P:(t + 1) * P]),
                                (W["W2"][0][:, cs], W["W2"][1][:, cs]))
                        mark = products(pD[:, out, t, :], terms, False, m2 == M // 2, pe_dense)
                    hid_free[hs] = [mark]
                yield
            VE.wait(mark, xo)
            done = tt(VE, flat(xo_nat[:, :, :]), flat(pD[:, out, :, :]), flat(xo_nat[:, :, :]), ALU.add, dve_dense)
            dense_free[out].append(done)
            SP.wait(done)
            st["xo_free"] = load(out_d[b].rearrange("(t p) h -> p t h", p=P), xo_nat[:, :, :], dma["out"])
            yield

        ffn_in = sb("ffn_in", [P, T, H])

        load_x(0)
        load_mask(0)
        prefetch_bias(NBIAS)
        mark = None
        for name in ("w1_nr", "w2_nr", "w1_tsr", "w2_tsr", "w1_sr", "w2_sr", "w3_sr"):
            mark = split_weight(name, w["L2_cond_" + name])
        mark = split_weight("Wq", w["L3_cond_Wq"], permute=True, scale=QS_)
        mark = split_weight("Wk", w["L3_cond_Wk"], permute=True)
        for name in ("Wv", "Wo", "W1", "W2"):
            mark = split_weight(name, w["L3_cond_" + name], scale=0.5 if name == "W2" else 1.0)
        PE.wait(mark)

        def step(gen, n=1):
            for _ in range(n):
                if gen is not None and next(gen, "end") == "end":
                    return False
            return gen is not None

        def finish(gen):
            while step(gen):
                pass

        for m2 in range(2):
            fetch_expert(0, m2)
        for m2 in range(2):
            split_expert(0, m2, PO, pool_w)
        for m2 in range(2, 4):
            fetch_expert(0, m2)
        rotate(0)
        turn_input(0)
        for b in range(NB + 2):
            now = b < NB
            heads = attention(b - 1) if 0 <= b - 1 < NB else None
            rest = tail(b - 2) if 0 <= b - 2 < NB else None
            if now:
                l1 = wide(b)
                step(l1, 3)
                step(heads)
                finish(l1)
                n1 = norm1(b)
                step(n1)
            step(rest)
            step(heads, 4)
            if now:
                step(n1)
            step(rest)
            step(heads, 4)
            if now:
                branch(b)
                n23 = norm23(b)
                step(n23)
            step(heads, 2)
            if now:
                step(n23)
            step(heads, 2)
            if now:
                step(n23)
                n3 = qkv(b)
                if b + 1 < NB:
                    split_expert(b + 1, 0, PO, pool_w)
                    split_expert(b + 1, 1, PO, pool_w)
                    fetch_expert(b + 1, 2)
                    fetch_expert(b + 1, 3)
            step(rest)
            for i in range(5):
                step(heads, 2)
                step(rest)
            if now:
                step(n3)
            for i in range(3):
                step(heads, 2)
                step(rest)
            if now:
                step(n3)
                if b + 1 < NB:
                    rotate(b + 1)
            finish(heads)
            finish(rest)
            if now:
                finish(n3)
                if b + 1 < NB:
                    turn_input(b + 1)
        SP.wait((dma["out"], dma["out"].count))

        block = ctx.enter_context(nc.Block())
        block.tensor(PE.play)
        block.scalar(AC.play)
        block.vector(VE.play)
        block.gpsimd(PO.play)
        block.sync(SP.play)


_WEIGHTS = ["L1_cond_Wi", "L1_cond_bi", "L1_cond_Wo", "L1_cond_bo", "L1_cond_gamma", "L1_cond_beta",
            "L2_cond_w1_nr", "L2_cond_b1_nr", "L2_cond_w2_nr", "L2_cond_b2_nr", "L2_cond_w1_tsr", "L2_cond_b1_tsr",
            "L2_cond_w2_tsr", "L2_cond_b2_tsr", "L2_cond_w1_sr", "L2_cond_b1_sr", "L2_cond_w2_sr", "L2_cond_b2_sr",
            "L2_cond_w3_sr", "L2_cond_b3_sr", "L2_cond_gamma", "L2_cond_beta", "L3_cond_W_ada", "L3_cond_b_ada",
            "L3_cond_Wq", "L3_cond_bq", "L3_cond_Wk", "L3_cond_bk", "L3_cond_Wv", "L3_cond_bv", "L3_cond_Wo",
            "L3_cond_bo", "L3_cond_W1", "L3_cond_b1", "L3_cond_W2", "L3_cond_b2", "L3_cond_g2", "L3_cond_beta2"]
_DATA = ["x", "condB_theta", "condB_phi", "itok_B_0_7", "itok_B_0_2", "itok_B_34_63", "fside_Bx16xSxS_0",
         "mask_Bx1xSxS_bk0"]


def constant_table(experts, half):
    table = np.zeros((P, 4), np.float32)
    table[:half, C_FREQ] = np.exp(np.arange(half, dtype=np.float32) * np.float32(-np.log(10000.0) / (half - 1)))
    row = np.arange(P) % 32
    table[:, C_ROW] = row
    table[:, C_KIND] = (row >= experts) & (row < experts + 3)
    table[:, C_KIND + 1] = row < experts
    return table


def kernel(**inputs):
    import numpy as _np
    import concourse.bacc as _bacc
    from concourse import mybir as _mybir
    from concourse.bass_utils import run_bass_kernel_spmd as _run

    nc = _bacc.Bacc("TRN2", target_bir_lowering=False, num_devices=1)
    arrays, aps = {}, {}

    def declare(name, a):
        arrays[f"in_{name}"] = a
        aps[name] = nc.dram_tensor(f"in_{name}", a.shape, _mybir.dt.from_np(a.dtype), kind="ExternalInput").ap()

    for name in _DATA + _WEIGHTS:
        declare(name, _np.ascontiguousarray(inputs[name]))
    declare("consts", constant_table(inputs["L1_cond_Wi"].shape[0], inputs["x"].shape[2] // 2))
    out = nc.dram_tensor("out_0", inputs["x"].shape, _mybir.dt.float32, kind="ExternalOutput").ap()
    conditioned_stack(nc, *[aps[n] for n in _DATA], {n: aps[n] for n in _WEIGHTS}, aps["consts"], out)
    r = _run(nc, [arrays], core_ids=[0])
    return r.results[0]["out_0"]
```

```python
from contextlib import ExitStack

import numpy as np

import concourse.bass as bass
from concourse import mybir

P = 128
F32 = mybir.dt.float32
F32R = mybir.dt.float32r
I32 = mybir.dt.int32
U8 = mybir.dt.uint8
ALU = mybir.AluOpType
ACT = mybir.ActivationFunctionType

C_FREQ, C_ROW, C_KIND = 0, 1, 2
TWO_PI = 6.283185307179586
PI_A = 6.28125
PI_B = float((np.float32(TWO_PI - PI_A).view(np.uint32) & np.uint32(0xFFFFF000)).view(np.float32))
PI_C = TWO_PI - PI_A - PI_B
ROUND_MAGIC = 12582912.0
PI_BELOW = 3.1415925
MASKED = -1.0e30
ROOT_MAGIC = float(0x5F3759DF)


ORDER = ("ffffffhffffffrfrhhhhffrhhrfhhhfhhhffhhrhrffh"
         "hhrhfrhhrrrhhrhrrhhrrhhrhfrrrhhfhhfhfhfffh")


class Signal:

    def __init__(self, sem):
        self.sem, self.count = sem, 0


class Lane:

    def __init__(self):
        self.steps, self.waited = [], {}

    def wait(self, *marks):
        for mark in marks:
            if mark is None:
                continue
            signal, value = mark
            if self.waited.get(signal, 0) < value:
                self.waited[signal] = value
                self.steps.append(lambda e, s=signal.sem, v=value: e.wait_ge(s, v))

    def run(self, make, signal=None, by=1):
        if signal is None:
            self.steps.append(make)
            return None
        self.steps.append(lambda e: make(e).then_inc(signal.sem, by))
        signal.count += by
        return (signal, signal.count)

    def play(self, engine):
        for step in self.steps:
            step(engine)


def conditioned_stack(nc, x_in, theta_in, phi_in, expert_in, branch_in, step_in, fside_in, mask_in, w, consts_in, out_d):
    NB, S, H = x_in.shape
    NH = fside_in.shape[1]
    HD = H // NH
    E, _, FF = w["L1_cond_Wi"].shape
    T = S // P
    K = H // P
    M = FF // P
    NPAIR = NH // 2
    SR = w["L2_cond_w1_sr"].shape[1]
    assert (T, K, HD) == (2, 2, 16) and SR == 4 * P and FF == 8 * P

    ctx = ExitStack()
    with ctx:
        def sb(name, shape, dt=F32):
            return ctx.enter_context(nc.sbuf_tensor(name, shape, dt))

        def signal(name):
            return Signal(ctx.enter_context(nc.semaphore(name)))

        ident = sb("ident", [P, P])
        eye = sb("eye", [P, K, H], F32R)
        consts = sb("consts", [P, 4])
        W = {}
        for name, cols in (("w1_nr", K * H), ("w2_nr", K * H), ("w1_tsr", K * H), ("w2_tsr", K * H),
                           ("w1_sr", K * SR), ("w2_sr", SR // P * H), ("w3_sr", K * H),
                           ("Wq", K * H), ("Wk", K * H), ("Wv", K * H), ("Wo", K * H),
                           ("W1", K * FF), ("W2", M * H)):
            W[name] = (sb(name + "_hi", [P, cols], F32R), sb(name + "_lo", [P, cols], F32R))
        NRAW, NEXP = 2, 2
        raw = sb("raw", [P, NRAW, 2 * K * H])
        exp_hi = sb("exp_hi", [P, NEXP, 2 * K * H], F32R)
        exp_lo = sb("exp_lo", [P, NEXP, 2 * K * H], F32R)
        q_stack = sb("q_stack", [P, NPAIR, S], F32R)
        k_stack = sb("k_stack", [P, NPAIR, S], F32R)
        NBIAS = 4
        bias_ring = sb("bias_ring", [P, NBIAS, 2, S])
        NX = 3
        x_scores = sb("x_scores", [P, NX, 2, S])
        NPROBS = 2
        probs = sb("probs", [P, NPROBS, K, S])
        v_aug = sb("v_aug", [P, T, NH, 32])
        ctx_raw = sb("ctx_raw", [P, S])
        ctx_nat = sb("ctx_nat", [P, T, H])
        mask_u8 = sb("mask_u8", [P, T, S], U8)
        mask_add = sb("mask_add", [P, T, S])
        NHID, NGELU = 3, 2
        gelu_out = sb("gelu_out", [P, NGELU, 2, S])
        hid_hi = sb("hid_hi", [P, NHID, 2, S], F32R)
        hid_lo = sb("hid_lo", [P, NHID, 2, S], F32R)
        xa_hi, xa_lo = sb("xa_hi", [P, K, S], F32R), sb("xa_lo", [P, K, S], F32R)
        xb = [(sb(f"xb_hi{i}", [P, K, S], F32R), sb(f"xb_lo{i}", [P, K, S], F32R)) for i in range(2)]
        xc_hi, xc_lo = sb("xc_hi", [P, K, S], F32R), sb("xc_lo", [P, K, S], F32R)
        x_nat = sb("x_nat", [P, T, H])
        rot_a = sb("rot_a", [P, T, H])
        y_nat = sb("y_nat", [P, T, H])
        xo_nat = sb("xo_nat", [P, T, H])
        ffn_in = sb("ffn_in", [P, T, H])
        gamma2 = sb("gamma2", [P, H])
        beta2 = sb("beta2", [P, H])
        rot_cos = sb("rot_cos", [P, NB, 4])
        rot_sin = sb("rot_sin", [P, NB, 4])
        N1 = M + 2 * K + K
        chosen = sb("chosen", [P, N1, NB])
        mod = sb("mod", [P, 2 * K, NB])
        NCOL = SR // P + K + 2 * K + K + K + 2 * K
        cols = sb("cols", [P, NCOL])
        NROWS = 32
        bias_raw = xo_nat[0:NROWS, 0, :]
        bias_rows = sb("bias_rows", [2 * NROWS, H], F32R)
        select = sb("select", [2 * NROWS, 4, NB])
        stage_sel = sb("stage_sel", [2 * NROWS, 4, P], F32R)
        ones = sb("ones", [2 * NROWS, P])
        idx = sb("idx", [1, 2, NB], I32)
        stats = sb("stats", [P, T, 6])
        mean_var = sb("mean_var", [P, T, 2])
        rstd = sb("rstd", [P, T])
        newton = sb("newton", [P, 3, T])
        row_max = sb("row_max", [P, NX, 2])
        rden = sb("rden", [P, T, 4])

        pS = ctx.enter_context(nc.psum_tensor("pS", [P, 2, T, S], F32))
        pX = ctx.enter_context(nc.psum_tensor("pX", [P, 2, K, S], F32))
        pC = ctx.enter_context(nc.psum_tensor("pC", [P, S], F32))
        ND, OUT = 2, 2
        pD = ctx.enter_context(nc.psum_tensor("pD", [P, ND + 1, 2, S], F32))

        dma = {n: signal("dma_" + n) for n in ("const", "cols", "rows", "x", "mask", "idx", "out", "bcast", "ada", "spill")}
        q_spill = nc.dram_tensor("q_spill", (2, 2, 2, HD * NPAIR * S), F32, kind="Internal").ap()
        k_spill = nc.dram_tensor("k_spill", (2, 2, 3, HD * NPAIR * S), F32, kind="Internal").ap()
        dma_raw = [signal(f"dma_raw{i}") for i in range(NRAW)]
        dma_stack = [signal(f"dma_stack{i}") for i in range(2)]
        dma_weights = [signal(f"dma_weights{i}") for i in range(2)]
        dma_bias = [signal(f"dma_bias{i}") for i in range(NBIAS)]
        pe_set, pe_dense, pe_tr, pe_s, pe_x, pe_c = (signal("pe_" + n) for n in ("set", "dense", "tr", "s", "x", "c"))
        act_set, act_dense, act_exp, act_w = (signal("act_" + n) for n in ("set", "dense", "exp", "w"))
        dve_set, dve_dense, dve_max, dve_sub, dve_small = (signal("dve_" + n) for n in ("set", "dense", "max", "sub", "small"))
        pool_set, pool_bias, pool_w = (signal("pool_" + n) for n in ("set", "bias", "w"))
        pe_n, act_n, dve_n = (signal(n) for n in ("pe_narrow", "act_narrow", "dve_narrow"))
        pe_r, act_r, dve_r = (signal(n) for n in ("pe_deep", "act_deep", "dve_deep"))

        PE, AC, VE, PO, SP = Lane(), Lane(), Lane(), Lane(), Lane()

        def flat(ap):
            return ap.rearrange("p a b -> p (a b)")

        def f32(ap):
            return ap.bitcast(F32)

        def mm(o, lhsT, rhs, start=False, stop=False, sig=None, **kw):
            return PE.run(lambda e: e.matmul(o, lhsT, rhs, start=start, stop=stop, skip_group_check=True, **kw), sig)

        def transpose(o, i, sig=None):
            return PE.run(lambda e: e.transpose(o, i, ident[:, :]), sig)

        def act(o, i, func, sig, bias=0.0, scale=1.0):
            return AC.run(lambda e: e.activation(o, i, func, bias=bias, scale=scale), sig)

        def tt(lane, o, a, b, op, sig):
            return lane.run(lambda e: e.tensor_tensor(o, a, b, op), sig)

        def ts(lane, o, a, s1, op0, sig, s2=None, op1=None):
            if op1 is None:
                return lane.run(lambda e: e.tensor_scalar(o, a, s1, None, op0), sig)
            return lane.run(lambda e: e.tensor_scalar(o, a, s1, s2, op0, op1), sig)

        def stt(o, a, s, b, op0, op1, sig):
            return VE.run(lambda e: e.scalar_tensor_tensor(o, a, s, b, op0, op1), sig)

        def split_terms(left, right):
            return [(left[0], right[0]), (left[0], right[1]), (left[1], right[0])]

        def products(o, terms, start, stop, sig=None):
            mark = None
            for n, (a, b) in enumerate(terms):
                last = n == len(terms) - 1
                mark = mm(o, a, b, start=start and n == 0, stop=stop and last, sig=sig if last else None)
            return mark

        dense_free = [[] for _ in range(ND + 1)]
        dense_banks = list(range(ND))

        def take_bank():
            n = dense_banks.pop(0)
            PE.wait(*dense_free[n])
            return n

        def give_bank(n, mark):
            dense_free[n] = [mark]
            if n != OUT:
                dense_banks.append(n)

        def load(dst, src, sig, **kw):
            return SP.run(lambda e: e.dma_start(dst, src, **kw), sig, by=16)

        load(consts[:, :], consts_in, dma["const"])
        load(idx[0:1, 0, :], expert_in.rearrange("(a b) -> a b", a=1), dma["idx"])
        got_idx = load(idx[0:1, 1, :], branch_in.rearrange("(a b) -> a b", a=1), dma["idx"])
        as_int = flat(rot_a[:, :, :]).bitcast(I32)
        scratch = flat(ffn_in[:, :, :])
        for n, src in enumerate((expert_in, branch_in, step_in)):
            load(as_int[:, n * NB:(n + 1) * NB], src.partition_broadcast(P), dma["const"])
        ang = flat(x_nat[:, :, :])
        load(ang[:, 0:NB], theta_in.partition_broadcast(P), dma["const"])
        got_const = load(ang[:, NB:2 * NB], phi_in.partition_broadcast(P), dma["const"])

        col_at, at = {}, 0
        VECTORS = (("L2_cond_b1_sr", SR // P), ("L2_cond_b2_sr", K), ("L3_cond_b_ada", 2 * K), ("L3_cond_bq", K),
                   ("L3_cond_bk", K), ("L3_cond_g2", K), ("L3_cond_beta2", K))
        vec_rows = [bias_ring[0:1, :, :, :].rearrange("p a b c -> p (a b c)"), flat(raw[0:1, :, :])]
        room = [NBIAS * 2 * S // P, NRAW * 2 * K * H // P]
        which, used = 0, 0
        vec_src = {}
        for name, n in VECTORS:
            if used + n > room[which]:
                which, used = which + 1, 0
            vec_src[name] = vec_rows[which][0:1, used * P:(used + n) * P]
            used += n
            got_cols = load(vec_src[name], w[name].rearrange("(a n) -> a n", a=1), dma["cols"])
            col_at[name] = at
            at += n

        def col(name, n=0):
            return cols[:, col_at[name] + n:col_at[name] + n + 1]

        rows_zero = VE.run(lambda e: e.memset(bias_raw, 0.0), dve_set)
        R_BRANCH, R_O, R_FF, R_V, R_HID = E, E + 3, E + 4, E + 5, E + 6
        SP.wait(rows_zero)
        load(bias_raw[0:E, :], w["L1_cond_bo"], dma["rows"])
        for r, name in ((R_BRANCH, "L2_cond_b2_nr"), (R_BRANCH + 1, "L2_cond_b2_tsr"), (R_BRANCH + 2, "L2_cond_b3_sr"),
                        (R_O, "L3_cond_bo"), (R_FF, "L3_cond_b2"), (R_V, "L3_cond_bv")):
            got_rows = load(bias_raw[r:r + 1, :], w[name].rearrange("(a n) -> a n", a=1), dma["rows"])
        load(bias_raw[R_HID:R_HID + M // 2, :], w["L3_cond_b1"].rearrange("(a n) -> a n", n=H), dma["rows"])
        scores_flat = x_scores[:, :, :, :].rearrange("p a b c -> p (a b c)")
        pick_bi = scores_flat[:, 0:FF + H]
        pick = flat(gelu_out[:, 0, :, :])
        load(pick_bi[0:E, 0:FF], w["L1_cond_bi"], dma["rows"])
        load(pick[0:E, 0:H], w["L1_cond_gamma"], dma["rows"])
        load(pick[0:E, H:2 * H], w["L1_cond_beta"], dma["rows"])
        load(pick_bi[0:1, FF:FF + H], w["L2_cond_b1_nr"].rearrange("(a n) -> a n", a=1), dma["rows"])
        got_rows = load(pick_bi[1:2, FF:FF + H], w["L2_cond_b1_tsr"].rearrange("(a n) -> a n", a=1), dma["rows"])
        load(gamma2[:, :], w["L2_cond_gamma"].partition_broadcast(P), dma["bcast"])
        got_bcast = load(beta2[:, :], w["L2_cond_beta"].partition_broadcast(P), dma["bcast"])

        PO.run(lambda e: e.memset(ident[:, :], 0.0), pool_set)
        PO.wait((pool_set, pool_set.count))
        got_ident = PO.run(lambda e: e.affine_select(out=ident[:, :], in_=ident[:, :], compare_op=ALU.not_equal,
                                                     fill=1.0, base=0, pattern=[[-1, P]], channel_multiplier=1),
                           pool_set)

        def vset(make):
            VE.wait((dve_set, dve_set.count))
            return VE.run(make, dve_set)

        VE.wait(got_ident)
        vset(lambda e: e.memset(f32(flat(eye[:, :, :])), 0.0))
        for k in range(K):
            vset(lambda e, k=k: e.tensor_copy(eye[:, k, k * P:(k + 1) * P], ident[:, :]))
        vset(lambda e: e.memset(ones[:, :], 1.0))
        vset(lambda e: e.memset(v_aug[:, :, :, :], 0.0))
        vset(lambda e: e.memset(v_aug[:, :, :, HD:HD + 1], 1.0))
        vset(lambda e: e.memset(select[:, :, :], 0.0))

        VE.wait(got_const)
        as_float = scratch[:, 0:3 * NB]
        vset(lambda e: e.tensor_copy(as_float, as_int[:, 0:3 * NB]))
        fx, fc, fs = (scratch[:, n * NB:(n + 1) * NB] for n in range(3))
        row_id = consts[:, C_ROW:C_ROW + 1]
        R2 = 2 * NROWS
        vset(lambda e: e.tensor_scalar(select[:, 0, :], fx[0:R2, :], row_id[0:R2, :], None, ALU.is_equal))
        vset(lambda e: e.tensor_scalar(select[:, 1, :], fc[0:R2, :], float(R_BRANCH), row_id[0:R2, :], ALU.add, ALU.is_equal))
        kind = consts[:, C_KIND:C_KIND + 1]
        vset(lambda e: e.tensor_scalar(select[:, 1, :], select[:, 1, :], kind[0:R2, :], None, ALU.mult))
        expert_row = consts[:, C_KIND + 1:C_KIND + 2]
        vset(lambda e: e.tensor_scalar(select[:, 0, :], select[:, 0, :], expert_row[0:R2, :], None, ALU.mult))
        branch_hot = scratch[:, 3 * NB:4 * NB]
        vset(lambda e: e.tensor_scalar(branch_hot, fc, row_id, None, ALU.is_equal))
        onev = scratch[:, 4 * NB:4 * NB + 4]
        for n, r in ((2, R_O), (3, R_FF), (1, R_V)):
            vset(lambda e, n=n, r=r: e.tensor_scalar(onev[:, n:n + 1], row_id, float(r), None, ALU.is_equal))
        v_sel = sb("v_sel", [R2, P], F32R)
        hid_sel = sb("hid_sel", [R2, M // 2], F32R)
        for m2 in range(M // 2):
            vset(lambda e, m2=m2: e.tensor_scalar(hid_sel[:, m2:m2 + 1], row_id[0:R2, :], float(R_HID + m2), None,
                                                  ALU.is_equal))
        vset(lambda e: e.tensor_scalar(v_sel[:, :], ones[:, :], onev[0:R2, 1:2], None, ALU.mult))
        vset(lambda e: e.tensor_scalar(stage_sel[:, 2, :], ones[:, :], onev[0:R2, 2:3], None, ALU.mult))
        got_sel = vset(lambda e: e.tensor_scalar(stage_sel[:, 3, :], ones[:, :], onev[0:R2, 3:4], None, ALU.mult))
        VE.wait(got_rows)
        vset(lambda e: e.tensor_copy(bias_rows[0:NROWS, :], bias_raw))
        vset(lambda e: e.tensor_tensor(bias_raw, bias_raw, f32(bias_rows[0:NROWS, :]), ALU.subtract))
        got_bias_rows = vset(lambda e: e.tensor_copy(bias_rows[NROWS:R2, :], bias_raw))
        n0 = take_bank()
        turn_ps = flat(pD[:, n0, :, :])
        VE.wait(got_cols)
        for name, room_ in (("L3_cond_bq", xo_nat[0:1, 1, :]), ("L3_cond_bk", x_nat[0:1, 1, :])):
            for par in range(2):
                permuted = vset(lambda e, row=vec_src[name], room_=room_, par=par: e.tensor_copy(
                    room_[:, par * P:(par + 1) * P].rearrange("a (d g) -> a d g", g=NPAIR),
                    row.rearrange("a (g r d) -> a r d g", r=2, d=HD)[:, par, :, :]))
            vec_src[name] = room_
        PE.wait(got_cols, permuted)
        for name, n in VECTORS:
            for i in range(n):
                row = vec_src[name][:, i * P:(i + 1) * P]
                c = col_at[name] + i
                turned = mm(turn_ps[:, c:c + 1], row, ones[0:1, 0:1], True, True, sig=pe_set)
        VE.wait(turned)
        give_bank(n0, vset(lambda e: e.tensor_copy(cols[:, :], turn_ps[:, 0:NCOL])))
        SCORE_SCALE = float(HD) ** -0.5
        got_bq = vset(lambda e: e.tensor_scalar(cols[:, col_at["L3_cond_bq"]:col_at["L3_cond_bq"] + K],
                                                cols[:, col_at["L3_cond_bq"]:col_at["L3_cond_bq"] + K],
                                                SCORE_SCALE, None, ALU.mult))

        n0 = take_bank()
        pick_ps = flat(pD[:, n0, :, :])
        PE.wait(got_bias_rows, got_rows)
        for n in range(M):
            mm(pick_ps[:, n * NB:(n + 1) * NB], pick_bi[0:E, n * P:(n + 1) * P], select[0:E, 0, :], True, True)
        for n in range(2 * K):
            mm(pick_ps[:, (M + n) * NB:(M + n + 1) * NB], pick[0:E, n * P:(n + 1) * P], select[0:E, 0, :], True, True)
        for n in range(K):
            a = M + 2 * K + n
            got_pick = mm(pick_ps[:, a * NB:(a + 1) * NB], pick_bi[0:2, FF + n * P:FF + (n + 1) * P],
                          branch_hot[0:2, :], True, True, sig=pe_set)
        VE.wait(got_pick)
        got_chosen = vset(lambda e: e.tensor_copy(chosen[:, :, :].rearrange("p a b -> p (a b)"), pick_ps[:, 0:N1 * NB]))
        give_bank(n0, got_chosen)

        def sine(dst, src, turn_by, tmp):
            vset(lambda e: e.tensor_scalar(tmp, src, 1.0 / TWO_PI, 0.25 * turn_by, ALU.mult, ALU.add))
            vset(lambda e: e.tensor_scalar(tmp, tmp, ROUND_MAGIC, None, ALU.add))
            vset(lambda e: e.tensor_scalar(tmp, tmp, ROUND_MAGIC, None, ALU.subtract))
            vset(lambda e: e.scalar_tensor_tensor(dst, tmp, -PI_A, src, ALU.mult, ALU.add))
            vset(lambda e: e.scalar_tensor_tensor(dst, tmp, -PI_B, dst, ALU.mult, ALU.add))
            vset(lambda e: e.scalar_tensor_tensor(dst, tmp, -PI_C, dst, ALU.mult, ALU.add))
            vset(lambda e: e.tensor_scalar(dst, dst, turn_by * TWO_PI / 4, PI_BELOW, ALU.add, ALU.min))
            ready = vset(lambda e: e.tensor_scalar(dst, dst, -PI_BELOW, None, ALU.max))
            AC.wait(ready)
            done = act(dst, dst, ACT.Sin, act_set)
            AC.wait(done)
            VE.wait(done)
            return done

        tmp = scratch[:, 5 * NB:7 * NB]
        cos2, sin2 = ang[:, 2 * NB:4 * NB], ang[:, 4 * NB:6 * NB]
        sine(cos2, ang[:, 0:2 * NB], 1, tmp)
        sine(sin2, ang[:, 0:2 * NB], 0, tmp)
        for j in range(4):
            a = (j // 2) * NB
            vset(lambda e, j=j, a=a: e.tensor_copy(rot_cos[:, :, j], cos2[:, a:a + NB]))
            got_rot = vset(lambda e, j=j, a=a: e.tensor_scalar(rot_sin[:, :, j], sin2[:, a:a + NB],
                                                     1.0 if j % 2 == 0 else -1.0, None, ALU.mult))
        ada = probs[:, :, :, :].rearrange("p a b c -> p (a b c)").rearrange("p (k n) -> p k n", k=K)
        got_ada = load(ada, w["L3_cond_W_ada"].rearrange("(k p) n -> p k n", p=P), dma["ada"])

        def embed():
            vset(lambda e: e.tensor_scalar(fs, fs, 0.01, 4000.0, ALU.mult, ALU.mult))
            e_arg = scratch[:, 7 * NB:8 * NB]
            vset(lambda e: e.tensor_scalar(e_arg, fs, consts[:, C_FREQ:C_FREQ + 1], None, ALU.mult))
            emb = scratch[:, 8 * NB:10 * NB]
            sine(emb[:, 0:NB], e_arg, 0, tmp[:, 0:NB])
            sine(emb[:, NB:2 * NB], e_arg, 1, tmp[:, 0:NB])
            emb_act = scratch[:, 10 * NB:12 * NB]
            got_emb = act(emb_act, emb, ACT.Silu, act_set)
            n0 = take_bank()
            ada_ps = flat(pD[:, n0, :, :])
            PE.wait(got_emb, got_ada)
            for n in range(2 * K):
                for k in range(K):
                    got_mod = mm(ada_ps[:, n * NB:(n + 1) * NB], ada[:, k, n * P:(n + 1) * P],
                                 emb_act[:, k * NB:(k + 1) * NB], k == 0, k == K - 1, sig=pe_set)
            VE.wait(got_mod)
            for n in range(2 * K):
                mod_ready = vset(lambda e, n=n: e.tensor_scalar(mod[:, n, :], ada_ps[:, n * NB:(n + 1) * NB],
                                                                col("L3_cond_b_ada", n), 1.0 if n < K else 0.0,
                                                                ALU.add, ALU.add))
            give_bank(n0, mod_ready)
            st["mod"] = mod_ready
            staging_free[0] = [got_mod]

        for lane in (PE, AC, PO, VE):
            lane.wait(got_chosen, got_ident, got_sel, got_bq, got_rot, got_bcast, got_idx)

        raw_free = [[] for _ in range(NRAW)]
        raw_n = [0]

        def take_raw():
            n = raw_n[0] % NRAW
            raw_n[0] += 1
            SP.wait(*raw_free[n])
            raw_free[n] = []
            return n

        st = {}

        staging = [probs[:, :, :, :].rearrange("p a b c -> p (a b c)"),
                   x_scores[:, 0:2, :, :].rearrange("p a b c -> p (a b c)")]
        staging_free = [[], []]
        staged = [0]

        def split_weight(name, src, permute=False, scale=1.0):
            hi, lo = W[name]
            k_n, n_n = src.shape[0] // P, src.shape[1]
            per = 1024 // n_n
            v = src.rearrange("(k p) n -> p k n", p=P)
            for k0 in range(0, k_n, per):
                kk = min(per, k_n - k0)
                n = staged[0] % 2
                staged[0] += 1
                SP.wait(*staging_free[n])
                size = kk * n_n
                piece = staging[n][:, 0:size]
                got = load(piece.rearrange("p (k n) -> p k n", k=kk), v[:, k0:k0 + kk, :], dma_weights[n])
                o = slice(k0 * n_n, k0 * n_n + size)
                if not permute:
                    pieces = [(piece, hi[:, o], lo[:, o])]
                else:
                    pieces = []
                    for k in range(kk):
                        r = piece[:, k * n_n:(k + 1) * n_n].rearrange("p (g r d) -> p r d g", r=2, d=HD)
                        h_, l_ = (t[:, (k0 + k) * n_n:(k0 + k + 1) * n_n].rearrange("p (r d g) -> p r d g", r=2, d=HD)
                                  for t in (hi, lo))
                        pieces += [(r[:, par], h_[:, par], l_[:, par]) for par in range(2)]
                AC.wait(got)
                VE.wait(got)
                for r, h_, l_ in pieces:
                    hi_done = act(h_, r, ACT.Copy, act_w, scale=scale)
                    VE.wait(hi_done)
                    mark = stt(l_, r, scale, f32(h_), ALU.mult, ALU.subtract, dve_set)
                staging_free[n] = [mark]
                st["weights"] = mark
                yield

        gelu_free = [[] for _ in range(NGELU)]
        hid_free = [[] for _ in range(NHID)]
        hid_slots = list(range(NHID))
        counts = {"gelu": 0, "bias": 0, "x": 0, "probs": 0, "pX": 0}
        exp_free = [[[], []] for _ in range(NEXP)]

        def split_T(bank, hi, lo, before, values=None):
            AC.wait(*before)
            src = flat(pD[:, bank, :, :]) if values is None else values
            h = act(flat(hi[:, :, :]), src, ACT.Copy, act_dense)
            VE.wait(h)
            return tt(VE, flat(lo[:, :, :]), src, f32(flat(hi[:, :, :])), ALU.subtract, dve_dense)

        def transposed(src_nat, before):
            n = take_bank()
            PE.wait(*before)
            for k in range(K):
                for t in range(T):
                    m = transpose(pD[:, n, k, t * P:(t + 1) * P], src_nat[:, t, k * P:(k + 1) * P],
                                  pe_tr if (k, t) == (K - 1, T - 1) else None)
            return n, m

        def root_steps(eps):
            half, square = newton[:, 0, :], newton[:, 1, :]
            as_i, ve = rstd[:, :].bitcast(I32), newton[:, 2, :]

            def small(make):
                VE.wait((dve_small, dve_small.count))
                return VE.run(make, dve_small)
            small(lambda e: e.tensor_scalar(ve, mean_var[:, :, 1], eps, None, ALU.add))
            small(lambda e: e.tensor_scalar(half, mean_var[:, :, 1], eps, -0.5, ALU.add, ALU.mult))
            small(lambda e: e.tensor_scalar(as_i, ve.bitcast(I32), 1, None, ALU.logical_shift_right))
            small(lambda e: e.tensor_scalar(as_i, as_i, -1.0, ROOT_MAGIC, ALU.mult, ALU.add))
            for _ in range(3):
                small(lambda e: e.tensor_tensor(square, rstd[:, :], rstd[:, :], ALU.mult))
                small(lambda e: e.tensor_tensor(square, square, half, ALU.mult))
                s = small(lambda e: e.scalar_tensor_tensor(rstd[:, :], square, 1.5, rstd[:, :], ALU.add, ALU.mult))
            VE.wait(s)

        def layer_norm(srcs, eps, dst, before, dst_free=()):
            VE.wait(*before)
            VE.wait(st.get("norm_read"))
            for t in range(T):
                s = VE.run(lambda e, t=t: e.bn_stats(stats[:, t, :], srcs[t]), dve_small)
            VE.wait(s)
            for t in range(T):
                s = VE.run(lambda e, t=t: e.bn_aggr(mean_var[:, t, :], stats[:, t, :]), dve_small)
            root_steps(eps)
            VE.wait(*dst_free)
            for t in range(T):
                s = VE.run(lambda e, t=t: e.tensor_scalar(dst[:, t, :], srcs[t], mean_var[:, t, 0:1],
                                                          rstd[:, t:t + 1], ALU.subtract, ALU.mult), dve_dense)
            st["norm_read"] = s
            return s

        def affine_T(bank, read, scales, shifts, hi, lo, free):
            yield
            n = counts["gelu"] % NGELU
            counts["gelu"] += 1
            AC.wait(read, *gelu_free[n], *free)
            buf = gelu_out[:, n, :, :]
            for k in range(K):
                m = act(buf[:, k, :], pD[:, bank, k, :], ACT.Identity, act_dense, bias=shifts[k], scale=scales[k])
            give_bank(bank, m)
            AC.wait(m)
            VE.wait(*free)
            lo_done = split_T(None, hi, lo, [], values=flat(buf))
            gelu_free[n] = [lo_done]
            return lo_done

        def take_hidden():
            return hid_slots.pop(0)

        def give_hidden(s, mark):
            hid_slots.append(s)
            hid_free[s] = [mark]

        def hidden(bank, read, func, biases=None):
            yield
            g = counts["gelu"] % NGELU
            counts["gelu"] += 1
            s = take_hidden()
            src = flat(gelu_out[:, g, :, :])
            AC.wait(read)
            if func == ACT.Gelu:
                AC.wait(*gelu_free[g])
                for n in range(2):
                    m = act(gelu_out[:, g, n, :], pD[:, bank, n, :], func, act_dense, bias=biases[n])
                give_bank(bank, m)
            else:
                AC.wait(*gelu_free[g])
                th = act(src, flat(pD[:, bank, :, :]), ACT.Tanh, act_dense, scale=1.702 / 2)
                VE.wait(th)
                m = stt(src, src, 1.0, flat(pD[:, bank, :, :]), ALU.add, ALU.mult, dve_dense)
                give_bank(bank, m)
            AC.wait(m, *hid_free[s])
            h = act(flat(hid_hi[:, s, :, :]), src, ACT.Copy, act_dense)
            VE.wait(h, *hid_free[s])
            low = tt(VE, flat(hid_lo[:, s, :, :]), src, f32(flat(hid_hi[:, s, :, :])), ALU.subtract, dve_dense)
            gelu_free[g] = [low]
            return s, low

        def open_out(sel, before, n=OUT):
            PE.wait(*before)
            if n == OUT:
                assert dense_free[n] is not None
                PE.wait(*dense_free[n])
                dense_free[n] = None
            rows = bias_rows[:, :].unsqueeze(1).to_broadcast([2 * NROWS, T, H])
            mm(pD[:, n, :, :], sel, rows, start=True)
            return n

        def add_residual(bank, hi, lo):
            for t in range(T):
                for k in range(K):
                    for part in (hi, lo):
                        mm(pD[:, bank, t, :], part[:, k, t * P:(t + 1) * P], eye[:, k, :])

        def load_x(b):
            SP.wait(st.get("x_nat_free"))
            st["x"] = load(x_nat[:, :, :], x_in[b].rearrange("(t p) h -> p t h", p=P), dma["x"])

        expert_reg = {}

        def fetch_expert(b, m2):
            n = take_raw()
            wi = w["L1_cond_Wi"].rearrange("e (k p) n -> p e k n", p=P)
            wo = w["L1_cond_Wo"].rearrange("e (m p) n -> p e m n", p=P)
            half = K * H

            def read_expert(e):
                expert_reg[b] = e.value_load(idx[0:1, 0, b:b + 1], min_val=0, max_val=E - 1)

            def start(e, dst, first):
                r = bass.ds(expert_reg[b], 1)
                src = (wi[:, r, :, m2 * 2 * P:(m2 + 1) * 2 * P] if first else wo[:, r, 2 * m2:2 * m2 + 2, :])
                return e.dma_start(dst, src.rearrange("p a k n -> p (a k) n"))
            if m2 == 0:
                SP.run(read_expert)
            SP.run(lambda e: start(e, raw[:, n, 0:half].rearrange("p (k n) -> p k n", k=K), True), dma_raw[n], by=16)
            got = SP.run(lambda e: start(e, raw[:, n, half:2 * half].rearrange("p (m n) -> p m n", m=2), False),
                         dma_raw[n], by=16)
            fetched[(b, m2)] = (n, got)

        def split_expert(b, m2, part, lane, sig):
            n, got = fetched[(b, m2)]
            s = m2 % NEXP
            size = K * H
            o = slice(part * size, (part + 1) * size)
            AC.wait(got, *exp_free[s][part])
            h = act(exp_hi[:, s, o], raw[:, n, o], ACT.Copy, act_w)
            lane.wait(h, *exp_free[s][part])
            low = tt(lane, exp_lo[:, s, o], raw[:, n, o], f32(exp_hi[:, s, o]), ALU.subtract, sig)
            raw_free[n].append(low)
            pieces[(b, m2, part)] = (s, low)

        fetched, pieces = {}, {}

        def rotate(b):
            VE.wait(st["x"], st.get("rot_free"))
            xg = x_nat[:, :, :].rearrange("p t (g j) -> p (t g) j", j=4)
            ag = rot_a[:, :, :].rearrange("p t (g j) -> p (t g) j", j=4)
            G = T * H // 4
            cos_b = rot_cos[:, b, :].unsqueeze(1).to_broadcast([P, G, 4])
            sin_b = rot_sin[:, b, :].unsqueeze(1).to_broadcast([P, G, 4])
            a = tt(VE, ag, xg, cos_b, ALU.mult, dve_dense)
            VE.wait(st.get("y_free"))
            yg = y_nat[:, :, :].rearrange("p t (g j) -> p (t g) j", j=4)
            for r in range(2):
                c = tt(VE, yg[:, :, r::2], xg[:, :, 1 - r::2], sin_b[:, :, r::2], ALU.mult, dve_dense)
            VE.wait(c)
            st["x0"] = tt(VE, flat(x_nat[:, :, :]), flat(rot_a[:, :, :]), flat(y_nat[:, :, :]), ALU.add, dve_dense)

        def turn_input(b):
            bank, m = transposed(x_nat, [st["x0"]])
            st["x_nat_free"] = m
            if b + 1 < NB:
                load_x(b + 1)
            AC.wait(st.get("xa_free"))
            lo = split_T(bank, xa_hi, xa_lo, [m])
            give_bank(bank, lo)
            AC.wait(st.get("sel0_free"), st.get("sel1_free"))
            for n in range(2):
                sel = act(stage_sel[:, n, :], ones[:, :], ACT.Copy, act_dense, scale=select[:, n, b:b + 1])
            st["x0T"], st["sel"] = lo, sel

        def wide(b):
            out = open_out(stage_sel[:, 0, :], [st["sel"]])
            PE.wait(st["x0T"])
            add_residual(out, xa_hi, xa_lo)

            def wide_in(m2):
                s, low = pieces[(b, m2, 0)]
                PE.wait(low)
                bank = take_bank()
                for n in range(2):
                    terms = []
                    for k in range(K):
                        cs = slice(k * H + n * P, k * H + (n + 1) * P)
                        terms += split_terms((exp_hi[:, s, cs], exp_lo[:, s, cs]), (xa_hi[:, k, :], xa_lo[:, k, :]))
                    mark = products(pD[:, bank, n, :], terms, True, True, pe_dense)
                exp_free[s][0] = [mark]
                if m2 + NEXP < M // 2:
                    split_expert(b, m2 + NEXP, 0, PO, pool_w)
                return (yield from hidden(bank, mark, ACT.Gelu, [chosen[:, 2 * m2 + n, b:b + 1] for n in range(2)]))

            def wide_out(m2, hid):
                s, wo_low = pieces[(b, m2, 1)]
                hs, low = hid
                PE.wait(low, wo_low)
                for t in range(T):
                    terms = []
                    for n in range(2):
                        cs = slice(K * H + n * H, K * H + (n + 1) * H)
                        terms += split_terms(
                            (hid_hi[:, hs, n, t * P:(t + 1) * P], hid_lo[:, hs, n, t * P:(t + 1) * P]),
                            (exp_hi[:, s, cs], exp_lo[:, s, cs]))
                    mark = products(pD[:, out, t, :], terms, False, m2 == M // 2 - 1, pe_dense)
                give_hidden(hs, mark)
                exp_free[s][1] = [mark]
                if m2 + NEXP < M // 2:
                    split_expert(b, m2 + NEXP, 1, VE, dve_dense)
                return mark

            hids = []
            for m2 in range(M // 2):
                hids.append((yield from wide_in(m2)))
                yield
                if m2:
                    wide_out(m2 - 1, hids[m2 - 1])
                    if b + 1 < NB and m2 >= 2:
                        fetch_expert(b + 1, m2 - 2)
                    yield
            mark = wide_out(M // 2 - 1, hids[-1])
            st["sel0_free"] = st["wide"] = mark
            yield

        def norm1(b):
            y = layer_norm([pD[:, OUT, t, :] for t in range(T)], 1e-12, y_nat, [st["wide"]])
            give_bank(OUT, y)
            yield
            bank, m = transposed(y_nat, [y])
            st["y_turned"] = m
            st["x1T"] = yield from affine_T(bank, m, [chosen[:, M + k, b:b + 1] for k in range(K)],
                                 [chosen[:, M + K + k, b:b + 1] for k in range(K)], xa_hi, xa_lo, [st["wide"]])
            yield

        def branch(b):
            out = open_out(stage_sel[:, 1, :], [st["sel"], st["weights"]])
            PE.wait(st["x1T"])
            add_residual(out, xa_hi, xa_lo)
            bank_a, bank_b = take_bank(), take_bank()
            slots = [take_hidden() for _ in range(NHID)]
            for lane in (AC, VE):
                for s in slots:
                    lane.wait(*hid_free[s])
                for g in range(NGELU):
                    lane.wait(*gelu_free[g])
            PE.wait(*[m for s in slots for m in hid_free[s]])
            first, second = branch_of(b, out, bank_a, bank_b, slots)
            first()
            yield
            second()
            closed = mm(pD[:, out, :, :], zero_sel[:, :], bias_rows[:, :].unsqueeze(1).to_broadcast([R2, T, H]),
                        stop=True, sig=pe_dense)
            st["sel1_free"] = closed
            st["xa_free"] = closed
            give_bank(bank_a, closed)
            give_bank(bank_b, closed)
            for s in slots:
                give_hidden(s, closed)
            for g in range(NGELU):
                gelu_free[g] = [closed]
            st["branch"] = closed

        def norm23(b):
            y = layer_norm([pD[:, OUT, t, :] for t in range(T)], 1e-5, y_nat, [st["branch"]], [st["y_turned"]])
            give_bank(OUT, y)
            yield
            VE.wait(y)
            gb = [t_[:, :].unsqueeze(1).to_broadcast([P, T, H]) for t_ in (gamma2, beta2)]
            y = tt(VE, y_nat[:, :, :], y_nat[:, :, :], gb[0], ALU.mult, dve_dense)
            VE.wait(y)
            y = tt(VE, y_nat[:, :, :], y_nat[:, :, :], gb[1], ALU.add, dve_dense)
            yield
            y = layer_norm([y_nat[:, t, :] for t in range(T)], 1e-5, rot_a, [y])
            st["x2"] = y
            st["y_free"] = y
            yield

        zero_sel = sb("zero_sel", [R2, P], F32R)
        VE.run(lambda e: e.memset(f32(zero_sel[:, :]), 0.0), dve_set)

        def branch_of(b, out, bank_a, bank_b, slots):
            xa = [(xa_hi[:, k, :], xa_lo[:, k, :]) for k in range(K)]
            s0, s1, s2 = slots
            narrow0 = {s: s.count for s in (pe_n, act_n, dve_n)}
            deep0 = {s: s.count for s in (pe_r, act_r, dve_r)}
            pad = {pe_n: 1, act_n: 3, dve_n: 1, pe_r: 3, act_r: 9, dve_r: 3}

            def layer_T(e, bank, n, wt, width, ins, m):
                hi, lo = W[wt]
                count = 0
                for k, x_ in enumerate(ins):
                    cs = slice(k * width + m * P, k * width + (m + 1) * P)
                    for a_, b_ in split_terms((hi[:, cs], lo[:, cs]), x_):
                        last = e.matmul(pD[:, bank, n, :], a_, b_, start=count == 0,
                                        stop=count == 3 * len(ins) - 1, skip_group_check=True)
                        count += 1
                return last

            def layer_nat(e, wt, slot):
                hi, lo = W[wt]
                for t in range(T):
                    for n in range(2):
                        cs = slice(n * H, (n + 1) * H)
                        ts_ = slice(t * P, (t + 1) * P)
                        for a_, b_ in split_terms((hid_hi[:, slot, n, ts_], hid_lo[:, slot, n, ts_]),
                                                  (hi[:, cs], lo[:, cs])):
                            e.matmul(pD[:, out, t, :], a_, b_, start=False, stop=False, skip_group_check=True)

            def pe_narrow_in(e, name):
                for n in range(2):
                    last = layer_T(e, bank_a, n, "w1_" + name, H, xa, n)
                last.then_inc(pe_n.sem, 1)

            def pe_narrow_out(e, name):
                e.wait_ge(dve_n.sem, dve_n0 + 1)
                if name:
                    layer_nat(e, "w2_" + name, s0)
                e.sem_inc(pe_r.sem, pad[pe_r])

            def pe_deep_in(e):
                for m in range(4):
                    last = layer_T(e, (bank_a, bank_b)[m // 2], m % 2, "w1_sr", SR, xa, m)
                    if m % 2:
                        last.then_inc(pe_r.sem, 1)

            def pe_deep_out(e):
                e.wait_ge(dve_r.sem, dve_r0 + 2)
                h1 = [(hid_hi[:, s, n, :], hid_lo[:, s, n, :]) for s in (s0, s1) for n in range(2)]
                for m in range(2):
                    last = layer_T(e, bank_a, m, "w2_sr", H, h1, m)
                last.then_inc(pe_r.sem, 1)
                e.wait_ge(dve_r.sem, dve_r0 + 3)
                layer_nat(e, "w3_sr", s2)
                e.sem_inc(pe_n.sem, pad[pe_n])

            def gelu_and_hi(e, bank, g, slot, biases, sem, base):
                for n in range(2):
                    e.activation(gelu_out[:, g, n, :], pD[:, bank, n, :], ACT.Gelu, bias=biases[n]).then_inc(sem, 1)
                e.wait_ge(sem, base + 2)
                e.activation(flat(hid_hi[:, slot, :, :]), flat(gelu_out[:, g, :, :]), ACT.Copy).then_inc(sem, 1)

            def act_narrow(e):
                e.wait_ge(pe_n.sem, pe_n0 + 1)
                gelu_and_hi(e, bank_a, 0, s0, [chosen[:, M + 2 * K + n, b:b + 1] for n in range(2)], act_n.sem, act_n0)

            def act_deep(e, i):
                bank, g, slot, name, first = ((bank_a, 0, s0, "L2_cond_b1_sr", 0), (bank_b, 1, s1, "L2_cond_b1_sr", 2),
                                              (bank_a, 0, s2, "L2_cond_b2_sr", 0))[i]
                e.wait_ge(pe_r.sem, pe_r0 + i + 1)
                gelu_and_hi(e, bank, g, slot, [col(name, first + n) for n in range(2)], act_r.sem, act_r0 + 3 * i)

            def lo_part(e, g, slot, sem):
                e.tensor_tensor(flat(hid_lo[:, slot, :, :]), flat(gelu_out[:, g, :, :]),
                                f32(flat(hid_hi[:, slot, :, :])), ALU.subtract).then_inc(sem, 1)

            def dve_narrow(e):
                e.wait_ge(act_n.sem, act_n0 + 3)
                lo_part(e, 0, s0, dve_n.sem)

            def dve_deep(e, i):
                e.wait_ge(act_r.sem, act_r0 + 3 * i + 3)
                lo_part(e, *((0, s0), (1, s1), (0, s2))[i], dve_r.sem)

            pe_n0, act_n0, dve_n0 = (narrow0[s] for s in (pe_n, act_n, dve_n))
            pe_r0, act_r0, dve_r0 = (deep0[s] for s in (pe_r, act_r, dve_r))
            for s, n in pad.items():
                s.count += n

            def on_pe(deep, narrow):
                def make(e):
                    c = e.value_load(idx[0:1, 1, b:b + 1])
                    with e.If(c == 2):
                        deep(e)
                    with e.Else():
                        with e.If(c == 1):
                            narrow(e, "tsr")
                        with e.Else():
                            with e.If(c == 0):
                                narrow(e, "nr")
                            with e.Else():
                                narrow(e, None)
                return make

            def two_way(deep, narrow):
                def make(e):
                    c = e.value_load(idx[0:1, 1, b:b + 1])
                    with e.If(c == 2):
                        for step_ in deep:
                            step_(e)
                    with e.Else():
                        for step_ in narrow:
                            step_(e)
                return make

            def first():
                PE.run(on_pe(pe_deep_in, lambda e, name: pe_narrow_in(e, name or "nr")))
                AC.run(two_way([lambda e: act_deep(e, 0), lambda e: act_deep(e, 1)], [act_narrow]))
                VE.run(two_way([lambda e: dve_deep(e, 0), lambda e: dve_deep(e, 1)], [dve_narrow]))

            def second():
                PE.run(on_pe(pe_deep_out, pe_narrow_out))
                AC.run(two_way([lambda e: act_deep(e, 2), lambda e: e.sem_inc(act_n.sem, pad[act_n])],
                               [lambda e: e.sem_inc(act_r.sem, pad[act_r])]))
                VE.run(two_way([lambda e: dve_deep(e, 2), lambda e: e.sem_inc(dve_n.sem, pad[dve_n])],
                               [lambda e: e.sem_inc(dve_r.sem, pad[dve_r])]))

            return first, second

        def load_mask(b):
            SP.wait(st.get("mask_u8_free"))
            got = load(mask_u8[:, :, :], mask_in[b, 0].rearrange("(t p) k -> p t k", p=P), dma["mask"])
            st["mask"] = got

        def make_mask(b):
            VE.wait(st["mask"], st.get("mask_add_free"))
            st["mask_u8_free"] = st["mask_ready"] = ts(
                VE, flat(mask_add[:, :, :]), flat(mask_u8[:, :, :]), MASKED, ALU.mult, dve_dense)

        def load_bias(b, h):
            n = counts["bias"] % NBIAS
            counts["bias"] += 1
            SP.wait(*bias_free[n])
            got = load(bias_ring[:, n, :, :],
                       fside_in[b, h].rearrange("(t p) k -> p t k", p=P), dma_bias[n])
            bias_at[(b, h)] = (n, got)

        bias_free = [[] for _ in range(NBIAS)]
        bias_at = {}
        bias_order = [(b, h) for b in range(NB) for h in range(NH)]
        bias_next = [0]

        def prefetch_bias(limit):
            while bias_next[0] < min(limit, len(bias_order)):
                load_bias(*bias_order[bias_next[0]])
                bias_next[0] += 1

        def qkv(b):
            xb_hi, xb_lo = xb[b % 2]
            assert b < 2 or st["xb_taken"] == b - 2
            bank, m = transposed(rot_a, [st["x2"]])
            st["rot_free"] = m
            lo = yield from affine_T(bank, m, [mod[:, k, b:b + 1] for k in range(K)],
                          [mod[:, K + k, b:b + 1] for k in range(K)], xb_hi, xb_lo, [st.get(("xb_free", b % 2)), st["mod"]])
            yield
            PE.wait(lo, st["weights"])
            staged = []
            for name, bias_name in (("Wq", "L3_cond_bq"), ("Wk", "L3_cond_bk")):
                hi, lo_ = W[name]
                bank = take_bank()
                for par in range(2):
                    terms = []
                    for k in range(K):
                        cs = slice(k * H + par * P, k * H + (par + 1) * P)
                        terms += split_terms((hi[:, cs], lo_[:, cs]), (xb_hi[:, k, :], xb_lo[:, k, :]))
                    mark = products(pD[:, bank, par, :], terms, True, True, pe_dense)
                yield
                s = take_hidden()
                AC.wait(mark, *hid_free[s])
                VE.wait(*hid_free[s])
                for par in range(2):
                    h = act(hid_hi[:, s, par, :], pD[:, bank, par, :], ACT.Identity, act_dense, bias=col(bias_name, par))
                VE.wait(h)
                for par in range(2):
                    l = stt(hid_lo[:, s, par, :], pD[:, bank, par, :], col(bias_name, par),
                            f32(hid_hi[:, s, par, :]), ALU.add, ALU.subtract, dve_dense)
                give_bank(bank, l)
                staged.append((s, l))
            turn_ = b % 2
            for (s, l), spill, parts in ((staged[0], q_spill, (0, 1)), (staged[1], k_spill, (0, 1, 0))):
                SP.wait(l)
                for i, part in enumerate(parts):
                    out_ = spill[turn_, :, i].rearrange("r (p c) -> p r c", c=S)
                    spilled = load(out_, f32((hid_hi, hid_lo)[part][:, s, :, :]), dma["spill"])
            for s, _ in staged:
                give_hidden(s, spilled)
            yield
            for part in range(2):
                g0, g1 = part * NPAIR // 2, (part + 1) * NPAIR // 2
                assert b == 0 or st["scored"] >= (b - 1, 2 * g1 - 1)
                SP.wait(spilled, st.get("stack_free"))
                for par in range(2):
                    for half in range(2):
                        p0 = (2 * par + half) * 2 * HD
                        for spill, first, stack in ((q_spill, 0, q_stack), (k_spill, half, k_stack)):
                            src = spill[turn_, par, first:first + 2].rearrange("a (d gc) -> (a d) gc", d=HD)
                            done = load(f32(flat(stack[p0:p0 + 2 * HD, g0:g1, :])), src[:, g0 * S:g1 * S], dma_stack[part])
                st["stack", b, part] = done
                if part == 0:
                    yield
            assert b == 0 or st["heads_done"] == b - 1
            make_mask(b)
            if b + 1 < NB:
                load_mask(b + 1)
            bank = open_out(v_sel[:, :], [st["weights"]], take_bank())
            for t in range(T):
                terms = []
                for k in range(K):
                    cs = slice(k * H, (k + 1) * H)
                    terms += split_terms((xb_hi[:, k, t * P:(t + 1) * P], xb_lo[:, k, t * P:(t + 1) * P]),
                                         (W["Wv"][0][:, cs], W["Wv"][1][:, cs]))
                mark = products(pD[:, bank, t, :], terms, False, True, pe_dense)
            yield
            AC.wait(mark, st.get("v_free"))
            for t in range(T):
                v = act(v_aug[:, t, :, 0:HD], pD[:, bank, t, :].rearrange("p (h d) -> p h d", d=HD), ACT.Copy, act_dense)
            give_bank(bank, v)
            st["v"] = v
            yield

        s_free = [[], []]
        x_free = [[] for _ in range(NX)]
        pX_free = [[], []]
        probs_free = [[] for _ in range(NPROBS)]
        pC_free = []
        ctx_raw_free = []

        def attention(b):
            todo = {}

            def scores(h):
                g, par = h // 2, h % 2
                n, got = bias_at[(b, h)]
                PO.wait(got, st["mask_ready"])
                biased = tt(PO, bias_ring[:, n, :, :], bias_ring[:, n, :, :], mask_add[:, :, :], ALU.add, pool_bias)
                st["mask_add_free"] = biased
                PE.wait(st["stack", b, 2 * g // NPAIR], *s_free[par])
                rows = slice(par * 4 * HD, (par + 1) * 4 * HD)
                for t in range(T):
                    m = mm(pS[:, par, t, :], q_stack[rows, g, t * P:(t + 1) * P], k_stack[rows, g, :],
                           True, True, sig=pe_s)
                st["stack_free"], st["scored"] = m, (b, h)
                xn = counts["x"] % NX
                counts["x"] += 1
                VE.wait(m, biased, *x_free[xn])
                for t in range(T):
                    mx = VE.run(lambda e, t=t: e.tensor_tensor_reduce(
                        x_scores[:, xn, t, :], pS[:, par, t, :], bias_ring[:, n, t, :], 1.0, -3.4e38,
                        ALU.add, ALU.max, row_max[:, xn, t:t + 1]), dve_max)
                s_free[par] = [mx]
                bias_free[n] = [mx]
                VE.wait(mx)
                for t in range(T):
                    sub = ts(VE, x_scores[:, xn, t, :], x_scores[:, xn, t, :], row_max[:, xn, t:t + 1],
                             ALU.subtract, dve_sub)
                prefetch_bias(bias_next[0] + 1)
                return (xn, sub)

            def exponentials(h, unit):
                xn, sub = unit
                xb = counts["pX"] % 2
                counts["pX"] += 1
                PE.wait(sub, *pX_free[xb])
                for t in range(T):
                    for k in range(K):
                        m = transpose(pX[:, xb, k, t * P:(t + 1) * P], x_scores[:, xn, t, k * P:(k + 1) * P],
                                      pe_x if (t, k) == (T - 1, K - 1) else None)
                x_free[xn] = [m]
                pb = counts["probs"] % NPROBS
                counts["probs"] += 1
                AC.wait(m, *probs_free[pb])
                e_ = act(flat(probs[:, pb, :, :]), flat(pX[:, xb, :, :]), ACT.Exp, act_exp)
                pX_free[xb] = [e_]
                return (h, pb, e_)

            def values(h, pb, e_):
                half = (h // 4) % 2
                q0 = 32 * (h % 4)
                if h % 4 == 0:
                    PE.wait(*pC_free)
                PE.wait(e_, st["v"])
                for k in range(K):
                    m = mm(pC[q0:q0 + 32, :], v_aug[:, k, h, :], probs[:, pb, k, :], k == 0, k == K - 1,
                           sig=pe_c if k == K - 1 else None, tile_position=(0, q0))
                probs_free[pb] = [m]
                if h % 4 == 3:
                    AC.wait(m, *ctx_raw_free)
                    c = act(ctx_raw[:, :], pC[:, :], ACT.Copy, act_dense)
                    pC_free[:] = [c]
                    todo["normalize"] = (h // 4, half, c)
                st["v_free"] = m

            def normalize(j, half, c):
                assert b == 0 or st["ctx_taken"] == b - 1
                xb = counts["pX"] % 2
                counts["pX"] += 1
                PE.wait(c, *pX_free[xb])
                for t in range(T):
                    m = transpose(pX[:, xb, t, 0:P], ctx_raw[:, t * P:(t + 1) * P], pe_tr)
                ctx_raw_free[:] = [m]
                v = pX[:, xb, :, 0:P].rearrange("p t (h c) -> p t h c", c=32)
                VE.wait(m, st.get("rden_free"), st.get("ctx_nat_free"))
                r = VE.run(lambda e: e.reciprocal(rden[:, :, :], v[:, :, :, HD]), dve_small)
                VE.wait(r)
                for t in range(T):
                    o = ctx_nat[:, t, j * 4 * HD:(j + 1) * 4 * HD].rearrange("p (h d) -> p h d", d=HD)
                    done = tt(VE, o, v[:, t, :, 0:HD], rden[:, t, :].unsqueeze(2).to_broadcast([P, 4, HD]),
                              ALU.mult, dve_dense)
                st["rden_free"] = done
                st["ctx"] = done
                pX_free[xb] = [done]

            def maybe_normalize():
                if "normalize" in todo:
                    normalize(*todo.pop("normalize"))

            units = [scores(0), scores(1)]
            yield
            ready = None
            for h in range(NH):
                if h + 2 < NH:
                    units.append(scores(h + 2))
                yield
                maybe_normalize()
                before = ready
                ready = exponentials(h, units[h])
                if before:
                    values(*before)
                yield
            values(*ready)
            yield
            maybe_normalize()
            st["heads_done"] = b
            yield

        def tail(b):
            xb_hi, xb_lo = xb[b % 2]
            bank, m = transposed(ctx_nat, [st["ctx"]])
            st["ctx_nat_free"], st["ctx_taken"] = m, b
            yield
            AC.wait(st.get("xc_free"))
            lo = split_T(bank, xc_hi, xc_lo, [m])
            give_bank(bank, lo)
            yield
            out = open_out(stage_sel[:, 2, :], [st["weights"]])
            add_residual(out, xb_hi, xb_lo)
            PE.wait(lo)
            for t in range(T):
                terms = []
                for k in range(K):
                    cs = slice(k * H, (k + 1) * H)
                    terms += split_terms((xc_hi[:, k, t * P:(t + 1) * P], xc_lo[:, k, t * P:(t + 1) * P]),
                                         (W["Wo"][0][:, cs], W["Wo"][1][:, cs]))
                mark = products(pD[:, out, t, :], terms, False, True, pe_dense)
            st["xb_free", b % 2], st["xb_taken"] = mark, b
            yield
            AC.wait(mark, st.get("xo_free"))
            xo = act(flat(xo_nat[:, :, :]), flat(pD[:, out, :, :]), ACT.Copy, act_dense)
            give_bank(out, xo)
            y = layer_norm([xo_nat[:, t, :] for t in range(T)], 1e-5, ffn_in, [xo], [st.get("ffn_in_free")])
            yield
            bank, m = transposed(ffn_in, [y])
            st["ffn_in_free"] = m
            lo = yield from affine_T(bank, m, [col("L3_cond_g2", k) for k in range(K)],
                          [col("L3_cond_beta2", k) for k in range(K)], xc_hi, xc_lo, [mark])
            yield
            out = open_out(stage_sel[:, 3, :], [])
            PE.wait(lo)
            hids = []
            for m2 in range(M // 2 + 1):
                if m2 < M // 2:
                    bank = take_bank()
                    for n in range(2):
                        terms = []
                        for k in range(K):
                            c0 = k * FF + (2 * m2 + n) * P
                            cs = slice(c0, c0 + P)
                            terms += split_terms((W["W1"][0][:, cs], W["W1"][1][:, cs]), (xc_hi[:, k, :], xc_lo[:, k, :]))
                        mm(pD[:, bank, n, :], bias_rows[:, n * P:(n + 1) * P],
                           hid_sel[:, m2:m2 + 1].to_broadcast([R2, S]), start=True)
                        mark = products(pD[:, bank, n, :], terms, False, True, pe_dense)
                    st["xc_free"] = mark
                    hids.append((yield from hidden(bank, mark, ACT.Tanh)))
                    yield
                if m2:
                    hs, low = hids[m2 - 1]
                    PE.wait(low)
                    for t in range(T):
                        terms = []
                        for n in range(2):
                            c0 = (2 * (m2 - 1) + n) * H
                            cs = slice(c0, c0 + H)
                            terms += split_terms(
                                (hid_hi[:, hs, n, t * P:(t + 1) * P], hid_lo[:, hs, n, t * P:(t + 1) * P]),
                                (W["W2"][0][:, cs], W["W2"][1][:, cs]))
                        mark = products(pD[:, out, t, :], terms, False, m2 == M // 2, pe_dense)
                    give_hidden(hs, mark)
                    if m2 < M // 2:
                        yield
            VE.wait(mark, xo)
            done = tt(VE, flat(xo_nat[:, :, :]), flat(pD[:, out, :, :]), flat(xo_nat[:, :, :]), ALU.add, dve_dense)
            give_bank(out, done)
            SP.wait(done)
            st["xo_free"] = load(out_d[b].rearrange("(t p) h -> p t h", p=P), xo_nat[:, :, :], dma["out"])
            yield

        SP.wait(turned, got_idx)
        for m2 in range(2):
            fetch_expert(0, m2)
        SP.wait(got_rot)
        load_x(0)
        SP.wait(got_chosen, got_sel)
        load_mask(0)
        prefetch_bias(NBIAS)

        def weights():
            embed()
            yield
            for name in ("w1_nr", "w2_nr", "w1_tsr", "w2_tsr", "w1_sr", "w2_sr", "w3_sr"):
                yield from split_weight(name, w["L2_cond_" + name])
            yield from split_weight("Wq", w["L3_cond_Wq"], permute=True, scale=SCORE_SCALE)
            yield from split_weight("Wk", w["L3_cond_Wk"], permute=True)
            for name in ("Wv", "Wo", "W1", "W2"):
                yield from split_weight(name, w["L3_cond_" + name], scale=0.5 if name == "W2" else 1.0)

        def front(b):
            yield from wide(b)
            yield from norm1(b)
            yield from branch(b)
            yield from norm23(b)
            if b + 1 < NB:
                for m2 in range(2):
                    for part in range(2):
                        split_expert(b + 1, m2, part, PO, pool_w)
                for m2 in range(2, 4):
                    fetch_expert(b + 1, m2)
            parts = qkv(b)
            next(parts)
            yield
            if b + 1 < NB:
                rotate(b + 1)
                yield
            next(parts)
            yield
            if b + 1 < NB:
                turn_input(b + 1)
                yield
            yield from parts

        for m2 in range(2):
            for part in range(2):
                split_expert(0, m2, part, PO, pool_w)
        for m2 in range(2, 4):
            fetch_expert(0, m2)
        rotate(0)
        turn_input(0)
        to_split = weights()
        for b in range(NB + 2):
            parts = {"f": front(b) if b < NB else None,
                     "h": attention(b - 1) if 0 <= b - 1 < NB else None,
                     "r": tail(b - 2) if 0 <= b - 2 < NB else None}
            for letter in ORDER:
                if parts[letter] is not None:
                    next(parts[letter], None)
                    next(to_split, None)
            for part in parts.values():
                assert part is None or next(part, "end") == "end"
        SP.wait((dma["out"], dma["out"].count))

        block = ctx.enter_context(nc.Block())
        block.tensor(PE.play)
        block.scalar(AC.play)
        block.vector(VE.play)
        block.gpsimd(PO.play)
        block.sync(SP.play)


_WEIGHTS = ["L1_cond_Wi", "L1_cond_bi", "L1_cond_Wo", "L1_cond_bo", "L1_cond_gamma", "L1_cond_beta",
            "L2_cond_w1_nr", "L2_cond_b1_nr", "L2_cond_w2_nr", "L2_cond_b2_nr", "L2_cond_w1_tsr", "L2_cond_b1_tsr",
            "L2_cond_w2_tsr", "L2_cond_b2_tsr", "L2_cond_w1_sr", "L2_cond_b1_sr", "L2_cond_w2_sr", "L2_cond_b2_sr",
            "L2_cond_w3_sr", "L2_cond_b3_sr", "L2_cond_gamma", "L2_cond_beta", "L3_cond_W_ada", "L3_cond_b_ada",
            "L3_cond_Wq", "L3_cond_bq", "L3_cond_Wk", "L3_cond_bk", "L3_cond_Wv", "L3_cond_bv", "L3_cond_Wo",
            "L3_cond_bo", "L3_cond_W1", "L3_cond_b1", "L3_cond_W2", "L3_cond_b2", "L3_cond_g2", "L3_cond_beta2"]
_DATA = ["x", "condB_theta", "condB_phi", "itok_B_0_7", "itok_B_0_2", "itok_B_34_63", "fside_Bx16xSxS_0",
         "mask_Bx1xSxS_bk0"]


def constant_table(experts, half):
    table = np.zeros((P, 4), np.float32)
    table[:half, C_FREQ] = np.exp(np.arange(half, dtype=np.float32) * np.float32(-np.log(10000.0) / (half - 1)))
    row = np.arange(P) % 32
    table[:, C_ROW] = row
    table[:, C_KIND] = (row >= experts) & (row < experts + 3)
    table[:, C_KIND + 1] = row < experts
    return table


def kernel(**inputs):
    import numpy as _np
    import concourse.bacc as _bacc
    from concourse import mybir as _mybir
    from concourse.bass_utils import run_bass_kernel_spmd as _run

    nc = _bacc.Bacc("TRN2", target_bir_lowering=False, num_devices=1)
    arrays, aps = {}, {}

    def declare(name, a):
        arrays[f"in_{name}"] = a
        aps[name] = nc.dram_tensor(f"in_{name}", a.shape, _mybir.dt.from_np(a.dtype), kind="ExternalInput").ap()

    for name in _DATA + _WEIGHTS:
        declare(name, _np.ascontiguousarray(inputs[name]))
    declare("consts", constant_table(inputs["L1_cond_Wi"].shape[0], inputs["x"].shape[2] // 2))
    out = nc.dram_tensor("out_0", inputs["x"].shape, _mybir.dt.float32, kind="ExternalOutput").ap()
    conditioned_stack(nc, *[aps[n] for n in _DATA], {n: aps[n] for n in _WEIGHTS}, aps["consts"], out)
    r = _run(nc, [arrays], core_ids=[0])
    return r.results[0]["out_0"]
```
